# Optimizing a Trainium2 kernel written in Bass

```python
import numpy as np
import jax
import jax.numpy as jnp

def _softmax(x, axis=-1):
    return jax.nn.softmax(x, axis=axis)

def _gelu(x):
    return jax.nn.gelu(x, approximate=True)

def _silu(x):
    return jax.nn.silu(x)

def _sigmoid(x):
    return jax.nn.sigmoid(x)

def _layernorm(x, axis=-1, eps=1e-05):
    m = jnp.mean(x, axis=axis, keepdims=True)
    v = jnp.var(x, axis=axis, keepdims=True)
    return (x - m) / jnp.sqrt(v + eps)

def _scatter_add(tgt, idx, src, axis=0):
    return tgt.at[idx].add(src)

def _segment_sum(src, seg, n):
    return jax.ops.segment_sum(src, seg, n)
kernel_name = 'mk_xattn_seq_d4_seqx_r8_0faa02'

def setup_inputs(seed: int=0):
    np.random.seed(seed)
    _w = jnp.asarray

    def _rec_inputs():
        import jax
        import jax.numpy as jnp
        _rk = jax.random.key(seed)
        x = -0.000125 + 0.9999 * jax.random.normal(jax.random.fold_in(_rk, 1), (8, 128, 256), jnp.float32)
        _lenS = 128 - jax.random.randint(jax.random.fold_in(_rk, 7), (8,), 0, max(1, 128 // 4) + 1, jnp.int32)
        _lenS2 = 128 - jax.random.randint(jax.random.fold_in(_rk, 8), (8,), 0, max(1, 128 // 4) + 1, jnp.int32)
        _ctx_2048P = jax.random.normal(jax.random.fold_in(_rk, 11), (8, 16, 256), jnp.float32)
        _ctx_2048c = jax.random.dirichlet(jax.random.fold_in(_rk, 511), 0.3 * jnp.ones((16,), jnp.float32), (8, 128))
        _ctx_2048t = jnp.einsum('bsk,bkd->bsd', _ctx_2048c, _ctx_2048P)
        _ctx_2048t = _ctx_2048t * jax.lax.rsqrt(jnp.mean(jnp.square(_ctx_2048t)) + 1e-12) * 0.953939
        ctx_2048 = -0.00401388 + 1.00018 * (_ctx_2048t + 0.3 * jax.random.normal(jax.random.fold_in(_rk, 611), (8, 128, 256), jnp.float32))
        _validS = jnp.arange(128)[None, :] < _lenS[:, None]
        _validS2 = jnp.arange(128)[None, :] < _lenS2[:, None]
        _causal = jnp.tril(jnp.ones((128, 128), dtype=bool))
        mask_BxS2_bf1 = jnp.ones((8, 128), dtype=bool)
        mask_Bx1xSxS2_ff0 = jnp.where(jnp.ones((8, 1, 128, 128), dtype=bool), 0.0, -1000000000.0).astype(jnp.float32)
        return (x, ctx_2048, mask_BxS2_bf1, mask_Bx1xSxS2_ff0)
    x, ctx_2048, mask_BxS2_bf1, mask_Bx1xSxS2_ff0 = _rec_inputs()

    def _L0_xattn_setup():
        import jax, jax.numpy as jnp
        import numpy as np
        H = 256
        B, L, S = (4, 512, 10)
        key = jax.random.key(seed)
        k1, k2, k3, k4, k5, k6 = jax.random.split(key, 6)
        scale = 1.0 / np.sqrt(H)
        return {'h_english': jax.random.normal(k1, (B, L, H), dtype=jnp.float32), 'h_lojban': jax.random.normal(k2, (B, S, H), dtype=jnp.float32), 'w_q': jax.random.normal(k3, (H, H), dtype=jnp.float32) * scale, 'w_k': jax.random.normal(k4, (H, H), dtype=jnp.float32) * scale, 'w_v': jax.random.normal(k5, (H, H), dtype=jnp.float32) * scale, 'w_o': jax.random.normal(k6, (H, H), dtype=jnp.float32) * scale, 'alpha': jnp.float32(0.1)}
    _L0_xattn_all = _L0_xattn_setup()
    _L0_xattn_in = {k: v for k, v in _L0_xattn_all.items() if k in ('w_q', 'w_k', 'w_v', 'w_o', 'alpha')}
    del _L0_xattn_all

    def _L1_xattn_setup():
        import jax, jax.numpy as jnp
        import numpy as np
        D = 256
        H = 16
        HD = D // H
        INNER = 4 * D
        EPS = 1e-05

        def layer_norm(x, w, b):
            mu = jnp.mean(x, axis=-1, keepdims=True)
            var = jnp.mean(jnp.square(x - mu), axis=-1, keepdims=True)
            return (x - mu) * jax.lax.rsqrt(var + EPS) * w + b
        key = jax.random.key(seed)
        ks = jax.random.split(key, 12)
        B, LQ, LK = (4, 128, 256)
        std = 0.02
        inp = {'hidden_states': jax.random.normal(ks[0], (B, LQ, D), jnp.float32), 'encoder_hidden_states': jax.random.normal(ks[1], (B, LK, D), jnp.float32), 'encoder_attention_mask': jnp.ones((B, LK), dtype=bool), 'ln1_w': jnp.ones((D,), jnp.float32), 'ln1_b': jnp.zeros((D,), jnp.float32), 'q_w': jax.random.normal(ks[2], (D, D), jnp.float32) * std, 'q_b': jnp.zeros((D,), jnp.float32), 'k_w': jax.random.normal(ks[3], (D, D), jnp.float32) * std, 'k_b': jnp.zeros((D,), jnp.float32), 'v_w': jax.random.normal(ks[4], (D, D), jnp.float32) * std, 'v_b': jnp.zeros((D,), jnp.float32), 'cproj_w': jax.random.normal(ks[5], (D, D), jnp.float32) * std, 'cproj_b': jnp.zeros((D,), jnp.float32), 'ln2_w': jnp.ones((D,), jnp.float32), 'ln2_b': jnp.zeros((D,), jnp.float32), 'fc_w': jax.random.normal(ks[6], (D, INNER), jnp.float32) * std, 'fc_b': jnp.zeros((INNER,), jnp.float32), 'proj_w': jax.random.normal(ks[7], (INNER, D), jnp.float32) * std, 'proj_b': jnp.zeros((D,), jnp.float32)}
        return inp
    _L1_xattn_all = _L1_xattn_setup()
    _L1_xattn_in = {k: v for k, v in _L1_xattn_all.items() if k in ('ln1_w', 'ln1_b', 'q_w', 'q_b', 'k_w', 'k_b', 'v_w', 'v_b', 'cproj_w', 'cproj_b', 'ln2_w', 'ln2_b', 'fc_w', 'fc_b', 'proj_w', 'proj_b')}
    del _L1_xattn_all

    def _L2_xattn_setup():
        import jax, jax.numpy as jnp
        import numpy as np
        H = 256
        NH = 32
        KVH = 8
        HD = H // NH
        GROUPS = NH // KVH
        EPS = 1e-06
        B, L, S = (4, 128, 128)

        def _gqa_forward(hidden_state, encoder_hidden_state, encoder_attention_mask, Wq, bq, Wk, bk, Wv, bv, Wo, bo, gamma, beta):
            b, l, _ = hidden_state.shape
            s = encoder_hidden_state.shape[1]
            q = hidden_state @ Wq + bq
            k = encoder_hidden_state @ Wk + bk
            v = encoder_hidden_state @ Wv + bv
            q = q.reshape(b, l, KVH, GROUPS, HD).transpose(0, 2, 3, 1, 4)
            k = k.reshape(b, s, KVH, HD).transpose(0, 2, 1, 3)
            v = v.reshape(b, s, KVH, HD).transpose(0, 2, 1, 3)
            scale = 1.0 / jnp.sqrt(jnp.asarray(HD, q.dtype))
            scores = jnp.einsum('bkgld,bksd->bkgls', q, k) * scale
            scores = scores + encoder_attention_mask[:, :, None, :, :]
            attn = jax.nn.softmax(scores, axis=-1)
            out = jnp.einsum('bkgls,bksd->bkgld', attn, v)
            out = out.transpose(0, 3, 1, 2, 4).reshape(b, l, H)
            out = out @ Wo + bo
            x = out + hidden_state
            mu = jnp.mean(x, axis=-1, keepdims=True)
            var = jnp.var(x, axis=-1, keepdims=True)
            return (x - mu) * jax.lax.rsqrt(var + EPS) * gamma + beta
        key = jax.random.key(seed)
        ks = jax.random.split(key, 12)
        sd = 0.02
        return {'hidden_state': jax.random.normal(ks[0], (B, L, H), jnp.float32), 'encoder_hidden_state': jax.random.normal(ks[1], (B, S, H), jnp.float32), 'encoder_attention_mask': jnp.zeros((B, 1, L, S), jnp.float32), 'Wq': jax.random.normal(ks[2], (H, H), jnp.float32) * sd, 'bq': jnp.zeros((H,), jnp.float32), 'Wk': jax.random.normal(ks[3], (H, KVH * HD), jnp.float32) * sd, 'bk': jnp.zeros((KVH * HD,), jnp.float32), 'Wv': jax.random.normal(ks[4], (H, KVH * HD), jnp.float32) * sd, 'bv': jnp.zeros((KVH * HD,), jnp.float32), 'Wo': jax.random.normal(ks[5], (H, H), jnp.float32) * sd, 'bo': jnp.zeros((H,), jnp.float32), 'gamma': jnp.ones((H,), jnp.float32), 'beta': jnp.zeros((H,), jnp.float32)}
    _L2_xattn_all = _L2_xattn_setup()
    _L2_xattn_in = {k: v for k, v in _L2_xattn_all.items() if k in ('Wq', 'bq', 'Wk', 'bk', 'Wv', 'bv', 'Wo', 'bo', 'gamma', 'beta')}
    del _L2_xattn_all

    def _L3_xattn_setup():
        import jax, jax.numpy as jnp
        import numpy as np
        B, Q, S1, S2 = (4, 32, 256, 256)
        D, H, K, F = (256, 16, 128, 1024)
        LN_EPS = 1e-05

        def _layer_norm(x, scale, offset):
            mu = jnp.mean(x, axis=-1, keepdims=True)
            var = jnp.var(x, axis=-1, keepdims=True)
            return (x - mu) * jax.lax.rsqrt(var + LN_EPS) * scale + offset

        def _cross_attention(q_in, kv_in, wq, bq, wk, bk, wv, bv, wo, bo, bias_k, bias_v):
            b, q_len, _ = q_in.shape
            t = kv_in.shape[1]
            qh = (q_in @ wq + bq).reshape(b, q_len, H, K)
            kh = (kv_in @ wk + bk).reshape(b, t, H, K)
            vh = (kv_in @ wv + bv).reshape(b, t, H, K)
            kh = jnp.concatenate([kh, jnp.broadcast_to(bias_k, (b, 1, H, K))], axis=1)
            vh = jnp.concatenate([vh, jnp.broadcast_to(bias_v, (b, 1, H, K))], axis=1)
            scale = jnp.sqrt(jnp.asarray(K, q_in.dtype))
            logits = jnp.einsum('bqhk,bthk->bhqt', qh, kh) / scale
            weights = jax.nn.softmax(logits, axis=-1)
            ctx = jnp.einsum('bhqt,bthk->bqhk', weights, vh).reshape(b, q_len, H * K)
            return ctx @ wo + bo

        def _forward(x, xf_1, xf_2, ln1_scale, ln1_offset, wq1, bq1, wk1, bk1, wv1, bv1, wo1, bo1, bias_k1, bias_v1, ln2_scale, ln2_offset, wq2, bq2, wk2, bk2, wv2, bv2, wo2, bo2, bias_k2, bias_v2, ln_mlp_scale, ln_mlp_offset, w_fc1, b_fc1, w_fc2, b_fc2):
            res = x
            h = _layer_norm(x, ln1_scale, ln1_offset)
            x = res + _cross_attention(h, xf_1, wq1, bq1, wk1, bk1, wv1, bv1, wo1, bo1, bias_k1, bias_v1)
            res = x
            h = _layer_norm(x, ln2_scale, ln2_offset)
            x = res + _cross_attention(h, xf_2, wq2, bq2, wk2, bk2, wv2, bv2, wo2, bo2, bias_k2, bias_v2)
            h = _layer_norm(x, ln_mlp_scale, ln_mlp_offset)
            h = jax.nn.gelu(h @ w_fc1 + b_fc1, approximate=False) @ w_fc2 + b_fc2
            return x + h
        key = jax.random.key(seed)
        ks = iter(jax.random.split(key, 64))

        def rn(shape, s=0.02):
            return jax.random.normal(next(ks), shape, jnp.float32) * s
        inp = {'x': rn((B, Q, D), 1.0), 'xf_1': rn((B, S1, D), 1.0), 'xf_2': rn((B, S2, D), 1.0)}
        for i in (1, 2):
            inp[f'ln{i}_scale'] = jnp.ones((D,), jnp.float32)
            inp[f'ln{i}_offset'] = jnp.zeros((D,), jnp.float32)
            inp[f'wq{i}'] = rn((D, H * K))
            inp[f'bq{i}'] = jnp.zeros((H * K,), jnp.float32)
            inp[f'wk{i}'] = rn((D, H * K))
            inp[f'bk{i}'] = jnp.zeros((H * K,), jnp.float32)
            inp[f'wv{i}'] = rn((D, H * K))
            inp[f'bv{i}'] = jnp.zeros((H * K,), jnp.float32)
            inp[f'wo{i}'] = rn((H * K, D))
            inp[f'bo{i}'] = jnp.zeros((D,), jnp.float32)
            inp[f'bias_k{i}'] = rn((1, 1, H, K))
            inp[f'bias_v{i}'] = rn((1, 1, H, K))
        inp['ln_mlp_scale'] = jnp.ones((D,), jnp.float32)
        inp['ln_mlp_offset'] = jnp.zeros((D,), jnp.float32)
        inp['w_fc1'] = rn((D, F))
        inp['b_fc1'] = jnp.zeros((F,), jnp.float32)
        inp['w_fc2'] = rn((F, D))
        inp['b_fc2'] = jnp.zeros((D,), jnp.float32)
        return inp
    _L3_xattn_all = _L3_xattn_setup()
    _L3_xattn_in = {k: v for k, v in _L3_xattn_all.items() if k in ('ln1_scale', 'ln1_offset', 'wq1', 'bq1', 'wk1', 'bk1', 'wv1', 'bv1', 'wo1', 'bo1', 'bias_k1', 'bias_v1', 'ln2_scale', 'ln2_offset', 'wq2', 'bq2', 'wk2', 'bk2', 'wv2', 'bv2', 'wo2', 'bo2', 'bias_k2', 'bias_v2', 'ln_mlp_scale', 'ln_mlp_offset', 'w_fc1', 'b_fc1', 'w_fc2', 'b_fc2')}
    del _L3_xattn_all
    return {'x': x, 'ctx_2048': ctx_2048, 'mask_BxS2_bf1': mask_BxS2_bf1, 'mask_Bx1xSxS2_ff0': mask_Bx1xSxS2_ff0, 'L0_xattn_w_q': _L0_xattn_in['w_q'], 'L0_xattn_w_k': _L0_xattn_in['w_k'], 'L0_xattn_w_v': _L0_xattn_in['w_v'], 'L0_xattn_w_o': _L0_xattn_in['w_o'], 'L0_xattn_alpha': _L0_xattn_in['alpha'], 'L1_xattn_ln1_w': _L1_xattn_in['ln1_w'], 'L1_xattn_ln1_b': _L1_xattn_in['ln1_b'], 'L1_xattn_q_w': _L1_xattn_in['q_w'], 'L1_xattn_q_b': _L1_xattn_in['q_b'], 'L1_xattn_k_w': _L1_xattn_in['k_w'], 'L1_xattn_k_b': _L1_xattn_in['k_b'], 'L1_xattn_v_w': _L1_xattn_in['v_w'], 'L1_xattn_v_b': _L1_xattn_in['v_b'], 'L1_xattn_cproj_w': _L1_xattn_in['cproj_w'], 'L1_xattn_cproj_b': _L1_xattn_in['cproj_b'], 'L1_xattn_ln2_w': _L1_xattn_in['ln2_w'], 'L1_xattn_ln2_b': _L1_xattn_in['ln2_b'], 'L1_xattn_fc_w': _L1_xattn_in['fc_w'], 'L1_xattn_fc_b': _L1_xattn_in['fc_b'], 'L1_xattn_proj_w': _L1_xattn_in['proj_w'], 'L1_xattn_proj_b': _L1_xattn_in['proj_b'], 'L2_xattn_Wq': _L2_xattn_in['Wq'], 'L2_xattn_bq': _L2_xattn_in['bq'], 'L2_xattn_Wk': _L2_xattn_in['Wk'], 'L2_xattn_bk': _L2_xattn_in['bk'], 'L2_xattn_Wv': _L2_xattn_in['Wv'], 'L2_xattn_bv': _L2_xattn_in['bv'], 'L2_xattn_Wo': _L2_xattn_in['Wo'], 'L2_xattn_bo': _L2_xattn_in['bo'], 'L2_xattn_gamma': _L2_xattn_in['gamma'], 'L2_xattn_beta': _L2_xattn_in['beta'], 'L3_xattn_ln1_scale': _L3_xattn_in['ln1_scale'], 'L3_xattn_ln1_offset': _L3_xattn_in['ln1_offset'], 'L3_xattn_wq1': _L3_xattn_in['wq1'], 'L3_xattn_bq1': _L3_xattn_in['bq1'], 'L3_xattn_wk1': _L3_xattn_in['wk1'], 'L3_xattn_bk1': _L3_xattn_in['bk1'], 'L3_xattn_wv1': _L3_xattn_in['wv1'], 'L3_xattn_bv1': _L3_xattn_in['bv1'], 'L3_xattn_wo1': _L3_xattn_in['wo1'], 'L3_xattn_bo1': _L3_xattn_in['bo1'], 'L3_xattn_bias_k1': _L3_xattn_in['bias_k1'], 'L3_xattn_bias_v1': _L3_xattn_in['bias_v1'], 'L3_xattn_ln2_scale': _L3_xattn_in['ln2_scale'], 'L3_xattn_ln2_offset': _L3_xattn_in['ln2_offset'], 'L3_xattn_wq2': _L3_xattn_in['wq2'], 'L3_xattn_bq2': _L3_xattn_in['bq2'], 'L3_xattn_wk2': _L3_xattn_in['wk2'], 'L3_xattn_bk2': _L3_xattn_in['bk2'], 'L3_xattn_wv2': _L3_xattn_in['wv2'], 'L3_xattn_bv2': _L3_xattn_in['bv2'], 'L3_xattn_wo2': _L3_xattn_in['wo2'], 'L3_xattn_bo2': _L3_xattn_in['bo2'], 'L3_xattn_bias_k2': _L3_xattn_in['bias_k2'], 'L3_xattn_bias_v2': _L3_xattn_in['bias_v2'], 'L3_xattn_ln_mlp_scale': _L3_xattn_in['ln_mlp_scale'], 'L3_xattn_ln_mlp_offset': _L3_xattn_in['ln_mlp_offset'], 'L3_xattn_w_fc1': _L3_xattn_in['w_fc1'], 'L3_xattn_b_fc1': _L3_xattn_in['b_fc1'], 'L3_xattn_w_fc2': _L3_xattn_in['w_fc2'], 'L3_xattn_b_fc2': _L3_xattn_in['b_fc2']}

def reference(x, ctx_2048, mask_BxS2_bf1, mask_Bx1xSxS2_ff0, L0_xattn_w_q, L0_xattn_w_k, L0_xattn_w_v, L0_xattn_w_o, L0_xattn_alpha, L1_xattn_ln1_w, L1_xattn_ln1_b, L1_xattn_q_w, L1_xattn_q_b, L1_xattn_k_w, L1_xattn_k_b, L1_xattn_v_w, L1_xattn_v_b, L1_xattn_cproj_w, L1_xattn_cproj_b, L1_xattn_ln2_w, L1_xattn_ln2_b, L1_xattn_fc_w, L1_xattn_fc_b, L1_xattn_proj_w, L1_xattn_proj_b, L2_xattn_Wq, L2_xattn_bq, L2_xattn_Wk, L2_xattn_bk, L2_xattn_Wv, L2_xattn_bv, L2_xattn_Wo, L2_xattn_bo, L2_xattn_gamma, L2_xattn_beta, L3_xattn_ln1_scale, L3_xattn_ln1_offset, L3_xattn_wq1, L3_xattn_bq1, L3_xattn_wk1, L3_xattn_bk1, L3_xattn_wv1, L3_xattn_bv1, L3_xattn_wo1, L3_xattn_bo1, L3_xattn_bias_k1, L3_xattn_bias_v1, L3_xattn_ln2_scale, L3_xattn_ln2_offset, L3_xattn_wq2, L3_xattn_bq2, L3_xattn_wk2, L3_xattn_bk2, L3_xattn_wv2, L3_xattn_bv2, L3_xattn_wo2, L3_xattn_bo2, L3_xattn_bias_k2, L3_xattn_bias_v2, L3_xattn_ln_mlp_scale, L3_xattn_ln_mlp_offset, L3_xattn_w_fc1, L3_xattn_b_fc1, L3_xattn_w_fc2, L3_xattn_b_fc2):
    import jax
    import jax.numpy as jnp

    def _L0_xattn_ref(h_english, h_lojban, w_q, w_k, w_v, w_o, alpha):
        import jax, jax.numpy as jnp
        import numpy as np
        H = 256
        B, L, S = (4, 512, 10)
        h = h_english.shape[-1]
        q = jnp.einsum('blh,oh->blo', h_english, w_q)
        k = jnp.einsum('bsh,oh->bso', h_lojban, w_k)
        v = jnp.einsum('bsh,oh->bso', h_lojban, w_v)
        scores = jnp.einsum('blh,bsh->bls', q, k) / jnp.sqrt(jnp.float32(h))
        probs = jax.nn.softmax(scores, axis=-1)
        context = jnp.einsum('bls,bsh->blh', probs, v)
        delta = jnp.einsum('blh,oh->blo', context, w_o)
        return h_english + alpha * delta

    def _L1_xattn_ref(hidden_states, encoder_hidden_states, encoder_attention_mask, ln1_w, ln1_b, q_w, q_b, k_w, k_b, v_w, v_b, cproj_w, cproj_b, ln2_w, ln2_b, fc_w, fc_b, proj_w, proj_b):
        import jax, jax.numpy as jnp
        import numpy as np
        D = 256
        H = 16
        HD = D // H
        INNER = 4 * D
        EPS = 1e-05

        def layer_norm(x, w, b):
            mu = jnp.mean(x, axis=-1, keepdims=True)
            var = jnp.mean(jnp.square(x - mu), axis=-1, keepdims=True)
            return (x - mu) * jax.lax.rsqrt(var + EPS) * w + b
        B, LQ, _ = hidden_states.shape
        LK = encoder_hidden_states.shape[1]
        residual = hidden_states
        x = layer_norm(hidden_states, ln1_w, ln1_b)
        q = (x @ q_w + q_b).reshape(B, LQ, H, HD).transpose(0, 2, 1, 3)
        k = (encoder_hidden_states @ k_w + k_b).reshape(B, LK, H, HD).transpose(0, 2, 1, 3)
        v = (encoder_hidden_states @ v_w + v_b).reshape(B, LK, H, HD).transpose(0, 2, 1, 3)
        scale = 1.0 / np.sqrt(HD).astype(np.float32)
        scores = jnp.einsum('bhqd,bhkd->bhqk', q, k) * scale
        mask = encoder_attention_mask[:, None, None, :]
        mask_value = jnp.finfo(scores.dtype).min
        scores = jnp.where(mask, scores, mask_value)
        attn = jax.nn.softmax(scores, axis=-1)
        out = jnp.einsum('bhqk,bhkd->bhqd', attn, v)
        out = out.transpose(0, 2, 1, 3).reshape(B, LQ, D)
        out = out @ cproj_w + cproj_b
        hidden = out + residual
        residual = hidden
        y = layer_norm(hidden, ln2_w, ln2_b)
        y = jax.nn.gelu(y @ fc_w + fc_b, approximate=True)
        y = y @ proj_w + proj_b
        return residual + y

    def _L2_xattn_ref(hidden_state, encoder_hidden_state, encoder_attention_mask, Wq, bq, Wk, bk, Wv, bv, Wo, bo, gamma, beta):
        import jax, jax.numpy as jnp
        import numpy as np
        H = 256
        NH = 32
        KVH = 8
        HD = H // NH
        GROUPS = NH // KVH
        EPS = 1e-06
        B, L, S = (4, 128, 128)

        def _gqa_forward(hidden_state, encoder_hidden_state, encoder_attention_mask, Wq, bq, Wk, bk, Wv, bv, Wo, bo, gamma, beta):
            b, l, _ = hidden_state.shape
            s = encoder_hidden_state.shape[1]
            q = hidden_state @ Wq + bq
            k = encoder_hidden_state @ Wk + bk
            v = encoder_hidden_state @ Wv + bv
            q = q.reshape(b, l, KVH, GROUPS, HD).transpose(0, 2, 3, 1, 4)
            k = k.reshape(b, s, KVH, HD).transpose(0, 2, 1, 3)
            v = v.reshape(b, s, KVH, HD).transpose(0, 2, 1, 3)
            scale = 1.0 / jnp.sqrt(jnp.asarray(HD, q.dtype))
            scores = jnp.einsum('bkgld,bksd->bkgls', q, k) * scale
            scores = scores + encoder_attention_mask[:, :, None, :, :]
            attn = jax.nn.softmax(scores, axis=-1)
            out = jnp.einsum('bkgls,bksd->bkgld', attn, v)
            out = out.transpose(0, 3, 1, 2, 4).reshape(b, l, H)
            out = out @ Wo + bo
            x = out + hidden_state
            mu = jnp.mean(x, axis=-1, keepdims=True)
            var = jnp.var(x, axis=-1, keepdims=True)
            return (x - mu) * jax.lax.rsqrt(var + EPS) * gamma + beta
        return _gqa_forward(hidden_state, encoder_hidden_state, encoder_attention_mask, Wq, bq, Wk, bk, Wv, bv, Wo, bo, gamma, beta)

    def _L3_xattn_ref(x, xf_1, xf_2, ln1_scale, ln1_offset, wq1, bq1, wk1, bk1, wv1, bv1, wo1, bo1, bias_k1, bias_v1, ln2_scale, ln2_offset, wq2, bq2, wk2, bk2, wv2, bv2, wo2, bo2, bias_k2, bias_v2, ln_mlp_scale, ln_mlp_offset, w_fc1, b_fc1, w_fc2, b_fc2):
        import jax, jax.numpy as jnp
        import numpy as np
        B, Q, S1, S2 = (4, 32, 256, 256)
        D, H, K, F = (256, 16, 128, 1024)
        LN_EPS = 1e-05

        def _layer_norm(x, scale, offset):
            mu = jnp.mean(x, axis=-1, keepdims=True)
            var = jnp.var(x, axis=-1, keepdims=True)
            return (x - mu) * jax.lax.rsqrt(var + LN_EPS) * scale + offset

        def _cross_attention(q_in, kv_in, wq, bq, wk, bk, wv, bv, wo, bo, bias_k, bias_v):
            b, q_len, _ = q_in.shape
            t = kv_in.shape[1]
            qh = (q_in @ wq + bq).reshape(b, q_len, H, K)
            kh = (kv_in @ wk + bk).reshape(b, t, H, K)
            vh = (kv_in @ wv + bv).reshape(b, t, H, K)
            kh = jnp.concatenate([kh, jnp.broadcast_to(bias_k, (b, 1, H, K))], axis=1)
            vh = jnp.concatenate([vh, jnp.broadcast_to(bias_v, (b, 1, H, K))], axis=1)
            scale = jnp.sqrt(jnp.asarray(K, q_in.dtype))
            logits = jnp.einsum('bqhk,bthk->bhqt', qh, kh) / scale
            weights = jax.nn.softmax(logits, axis=-1)
            ctx = jnp.einsum('bhqt,bthk->bqhk', weights, vh).reshape(b, q_len, H * K)
            return ctx @ wo + bo

        def _forward(x, xf_1, xf_2, ln1_scale, ln1_offset, wq1, bq1, wk1, bk1, wv1, bv1, wo1, bo1, bias_k1, bias_v1, ln2_scale, ln2_offset, wq2, bq2, wk2, bk2, wv2, bv2, wo2, bo2, bias_k2, bias_v2, ln_mlp_scale, ln_mlp_offset, w_fc1, b_fc1, w_fc2, b_fc2):
            res = x
            h = _layer_norm(x, ln1_scale, ln1_offset)
            x = res + _cross_attention(h, xf_1, wq1, bq1, wk1, bk1, wv1, bv1, wo1, bo1, bias_k1, bias_v1)
            res = x
            h = _layer_norm(x, ln2_scale, ln2_offset)
            x = res + _cross_attention(h, xf_2, wq2, bq2, wk2, bk2, wv2, bv2, wo2, bo2, bias_k2, bias_v2)
            h = _layer_norm(x, ln_mlp_scale, ln_mlp_offset)
            h = jax.nn.gelu(h @ w_fc1 + b_fc1, approximate=False) @ w_fc2 + b_fc2
            return x + h
        return _forward(x, xf_1, xf_2, ln1_scale, ln1_offset, wq1, bq1, wk1, bk1, wv1, bv1, wo1, bo1, bias_k1, bias_v1, ln2_scale, ln2_offset, wq2, bq2, wk2, bk2, wv2, bv2, wo2, bo2, bias_k2, bias_v2, ln_mlp_scale, ln_mlp_offset, w_fc1, b_fc1, w_fc2, b_fc2)
    x = _L0_xattn_ref(x, ctx_2048, L0_xattn_w_q, L0_xattn_w_k, L0_xattn_w_v, L0_xattn_w_o, L0_xattn_alpha)
    x = _L1_xattn_ref(x, ctx_2048, mask_BxS2_bf1, L1_xattn_ln1_w, L1_xattn_ln1_b, L1_xattn_q_w, L1_xattn_q_b, L1_xattn_k_w, L1_xattn_k_b, L1_xattn_v_w, L1_xattn_v_b, L1_xattn_cproj_w, L1_xattn_cproj_b, L1_xattn_ln2_w, L1_xattn_ln2_b, L1_xattn_fc_w, L1_xattn_fc_b, L1_xattn_proj_w, L1_xattn_proj_b)
    x = _L2_xattn_ref(x, ctx_2048, mask_Bx1xSxS2_ff0, L2_xattn_Wq, L2_xattn_bq, L2_xattn_Wk, L2_xattn_bk, L2_xattn_Wv, L2_xattn_bv, L2_xattn_Wo, L2_xattn_bo, L2_xattn_gamma, L2_xattn_beta)
    x = _L3_xattn_ref(x, ctx_2048, ctx_2048, L3_xattn_ln1_scale, L3_xattn_ln1_offset, L3_xattn_wq1, L3_xattn_bq1, L3_xattn_wk1, L3_xattn_bk1, L3_xattn_wv1, L3_xattn_bv1, L3_xattn_wo1, L3_xattn_bo1, L3_xattn_bias_k1, L3_xattn_bias_v1, L3_xattn_ln2_scale, L3_xattn_ln2_offset, L3_xattn_wq2, L3_xattn_bq2, L3_xattn_wk2, L3_xattn_bk2, L3_xattn_wv2, L3_xattn_bv2, L3_xattn_wo2, L3_xattn_bo2, L3_xattn_bias_k2, L3_xattn_bias_v2, L3_xattn_ln_mlp_scale, L3_xattn_ln_mlp_offset, L3_xattn_w_fc1, L3_xattn_b_fc1, L3_xattn_w_fc2, L3_xattn_b_fc2)
    return x

_drawn_inputs = setup_inputs


def setup_inputs(seed=0):
    import zlib

    import numpy as np

    out = dict(_drawn_inputs(seed))
    spreads = {'L1_xattn_ln1_w': (1.0, 0.6),
     'L1_xattn_ln1_b': (0.0, 0.8),
     'L1_xattn_q_b': (0.0, 0.8),
     'L1_xattn_k_b': (0.0, 2.0),
     'L1_xattn_v_b': (0.0, 0.273),
     'L1_xattn_cproj_b': (0.0, 0.1),
     'L1_xattn_ln2_w': (1.0, 0.6),
     'L1_xattn_ln2_b': (0.0, 0.8),
     'L1_xattn_fc_b': (0.0, 0.1),
     'L1_xattn_proj_b': (0.0, 0.1),
     'L2_xattn_bq': (0.0, 0.8),
     'L2_xattn_bk': (0.0, 2.0),
     'L2_xattn_bv': (0.0, 0.1),
     'L2_xattn_bo': (0.0, 0.1),
     'L2_xattn_gamma': (1.0, 0.2),
     'L2_xattn_beta': (0.0, 0.1),
     'L3_xattn_ln1_scale': (1.0, 0.6),
     'L3_xattn_ln1_offset': (0.0, 0.8),
     'L3_xattn_bq1': (0.0, 0.8),
     'L3_xattn_bk1': (0.0, 2.0),
     'L3_xattn_bv1': (0.0, 0.1),
     'L3_xattn_bo1': (0.0, 0.1),
     'L3_xattn_ln2_scale': (1.0, 0.6),
     'L3_xattn_ln2_offset': (0.0, 0.8),
     'L3_xattn_bq2': (0.0, 0.8),
     'L3_xattn_bk2': (0.0, 2.0),
     'L3_xattn_bv2': (0.0, 0.1),
     'L3_xattn_bo2': (0.0, 0.1),
     'L3_xattn_ln_mlp_scale': (1.0, 0.6),
     'L3_xattn_ln_mlp_offset': (0.0, 0.8),
     'L3_xattn_b_fc1': (0.0, 0.1),
     'L3_xattn_b_fc2': (0.0, 0.1)}
    factors = {'L0_xattn_w_q': 2.922,
     'L0_xattn_w_k': 2.924,
     'L1_xattn_q_w': 8.0,
     'L1_xattn_k_w': 8.0,
     'L2_xattn_Wq': 8.0,
     'L2_xattn_Wk': 8.0,
     'L3_xattn_wq1': 8.0,
     'L3_xattn_wk1': 8.0,
     'L3_xattn_bias_k1': 64.0,
     'L3_xattn_bias_v1': 64.0,
     'L3_xattn_wq2': 8.0,
     'L3_xattn_wk2': 8.0,
     'L3_xattn_bias_k2': 64.0,
     'L3_xattn_bias_v2': 64.0}
    for name, (base, spread) in spreads.items():
        noise = np.random.default_rng([zlib.crc32(name.encode()), seed]).standard_normal(out[name].shape)
        drawn = base * np.exp(spread * noise) if base else spread * noise
        out[name] = jnp.asarray(drawn.astype(out[name].dtype))
    for name, factor in factors.items():
        out[name] = (out[name] * factor).astype(out[name].dtype)
    return out
```

```python
import concourse.bass as bass
from concourse import mybir
from contextlib import ExitStack

F32 = mybir.dt.float32
R32 = mybir.dt.float32r
U8 = mybir.dt.uint8
ALU = mybir.AluOpType
ACT = mybir.ActivationFunctionType
AX_X = mybir.AxisListType.X

P = 128
D = 256
KT = D // P
NB = 4
HALVES = 2
B = NB * HALVES
TOK = NB * P
INNER = 4 * D
MT = INNER // P
LN_EPS, LN2_EPS = 1e-5, 1e-6
BIG = 2.0 ** 127
EXPS = 3
TWO_BANKS = 2

H3 = 16
HG3 = 2
T3 = P + 2
GROUPS3 = [(0, 3), (3, 6), (6, 8)]

STACK_A = [("L1_xattn_q_b", 2), ("L1_xattn_k_b", 2), ("L1_xattn_fc_b", 8), ("L2_xattn_bq", 2),
           ("L2_xattn_bk", 2), ("L3_xattn_b_fc1", 8),
           ("L3_xattn_bq1", H3), ("L3_xattn_bk1", H3), ("L3_xattn_bias_k1", H3), ("L3_xattn_bias_v1", H3)]
STACK_B = [("L3_xattn_bq2", H3), ("L3_xattn_bk2", H3), ("L3_xattn_bias_k2", H3), ("L3_xattn_bias_v2", H3)]
ROWS = ["L1_xattn_ln1_w", "L1_xattn_ln1_b", "L1_xattn_v_b", "L1_xattn_cproj_b", "L1_xattn_ln2_w",
        "L1_xattn_ln2_b", "L1_xattn_proj_b", "L2_xattn_bo", "L2_xattn_gamma", "L2_xattn_beta"]
ROWS3 = ["L3_xattn_ln1_scale", "L3_xattn_ln1_offset", "L3_xattn_bo1",
        "L3_xattn_ln2_scale", "L3_xattn_ln2_offset", "L3_xattn_bo2",
        "L3_xattn_ln_mlp_scale", "L3_xattn_ln_mlp_offset", "L3_xattn_b_fc2"]


def place(stack):
    at, n = {}, 0
    for name, rows in stack:
        at[name] = n
        n += rows
    return at, n


T_FILLS = ([("c", 1)] * KT + [("x", 1)] * KT + [("p0", 0)] + [("z1", 1)] * KT + [("p1", 0)] * 16
           + [("ctx1", 1)] * KT + [("z2", 1)] * KT + [("x2", 1)] * KT + [("p2", 0)] * 32 + [("ctx2", 1)] * KT)
A_FILLS = ([("q0", "AV")] * 2 + [("v0", "V")] * 2 + [("k1", "AV")] * 2 + [("v1", "V")] * 2
           + [("q1", "AV")] * 2 + [("o1", "V")] * 2 + [("k2", "AV")] * 2 + [("v2", "V")]
           + [("fc", "A")] * MT + [("q2", "AV")] * 2 + [("o2", "V")] * 2)
O_FILLS = ["pv0"] * NB + ["pv1"] * 4 + ["mlp"] * 2 + ["pv2"] * 8
S_FILLS = ["s0"] + ["s1"] * 16 + ["s2"] * 32
MLP_T, MLP_A = [("z", 1)] * KT, [("fc", "A")] * MT


def first(fills, what):
    return [f[0] if isinstance(f, tuple) else f for f in fills].index(what)


def splits_in(fills, n):
    return sum(f[1] for f in fills[:n])


def read_by(fills, n, engine):
    return sum(engine in f[1] for f in fills[:n])


def products(pe, out, left, right, begin, end):
    (lh, ll), (rh, rl) = left, right
    pe.matmul(out, lh, rh, start=begin, stop=False)
    pe.matmul(out, ll, rh, start=False, stop=False)
    return pe.matmul(out, lh, rl, start=False, stop=end)


def network(nc, a, out):
    ctx = ExitStack()
    with ctx:
        def sb(name, shape, dt=F32, where=ctx):
            return where.enter_context(nc.sbuf_tensor(name, shape, dt))

        banks = [ctx.enter_context(nc.psum_tensor(f"bank{i}", [P, 512], F32)) for i in range(8)]
        Sb, Tb, Ab, Ob = banks[0:2], banks[2:4], banks[4:6], banks[6:8]

        atA, nA = place(STACK_A)
        atB, nB = place(STACK_B)
        x_all = sb("x_all", [P, B, D])
        ident = sb("ident", [P, P])
        identR = sb("identR", [P, P], R32)
        colsA = sb("colsA", [P, nA])
        colsB = sb("colsB", [P, nB])
        rows = sb("rows", [P, len(ROWS), D])
        stats = sb("stats", [P, B, 6])
        mv = sb("mv", [P, B, 2])
        rstd = sb("rstd", [P, B])
        var = sb("var", [P, B])
        neg_half = sb("neg_half", [P, B])

        def mlp_memory(where, tag):
            return (sb("xh" + tag, [P, NB, D], F32, where), sb("z" + tag, [P, NB, D], F32, where),
                    sb("aT" + tag, [P, 2, KT, TOK], R32, where), sb("g" + tag, [P, 2, TOK], F32, where),
                    sb("gT" + tag, [P, 2, 2, TOK], R32, where), sb("fcw" + tag, [P, 2, KT, INNER], R32, where),
                    sb("pjw" + tag, [P, 2, MT, D], R32, where))

        def row(name):
            return rows[:, (ROWS if name in ROWS else ROWS3).index(name), :]

        def col(name, i):
            return colsA[:, atA[name] + i:atA[name] + i + 1]

        def pair(t, *idx):
            return t[(slice(None), 0) + idx], t[(slice(None), 1) + idx]

        s1 = ExitStack()
        xh, z, aT, g, gT, fcw, pjw = mlp_memory(s1, "_half")
        m0w = sb("m0w", [P, 2, KT, D], R32, s1)
        v0w = sb("v0w", [P, 2, KT, D], R32, s1)
        w1 = [sb(f"w1_{n}", [P, 2, KT, D], R32, s1) for n in "qkvo"]
        w2 = [sb(f"w2_{n}", [P, 2, KT, D], R32, s1) for n in "qko"]
        w2v = sb("w2v", [P, 2, KT, 64], R32, s1)
        hmask1 = sb("hmask1", [P, 8], F32, s1)
        hmask2 = sb("hmask2", [P, 16], F32, s1)
        bv2 = sb("bv2", [P, 64], F32, s1)
        alpha = sb("alpha", [P, 1], F32, s1)
        one_row = sb("one_row", [P, P], R32, s1)
        key_mask = sb("key_mask", [P, TOK], R32, s1)
        v0 = sb("v0", [P, NB, D + 1], F32, s1)
        v1 = sb("v1", [P, NB, 16, 17], F32, s1)
        v2 = sb("v2", [P, NB, 8, 9], F32, s1)

        s0 = ExitStack()
        stage = [sb(f"stage{i}", [P, KT, D], F32, s0) for i in range(4)]
        stage1 = [sb(f"stage1_{i}", [P, KT, D], F32, s0) for i in range(7)]
        stage_v = sb("stage_v", [P, KT, 64], F32, s0)
        w0 = [sb(f"w0_{n}", [P, 2, KT, D], R32, s0) for n in "qkvo"]
        stackA = sb("stackA", [P, P], F32, s0)
        stackB = sb("stackB", [P, P], F32, s0)
        ones = sb("ones", [P, P], F32, s0)
        stage_fc = sb("stage_fc", [P, KT, INNER], F32, s0)
        stage_pj = sb("stage_pj", [P, MT, D], F32, s0)
        s0.close()

        names0 = ["L0_xattn_w_q", "L0_xattn_w_k", "L0_xattn_w_v", "L0_xattn_w_o"]
        names1 = ["L1_xattn_q_w", "L1_xattn_k_w", "L1_xattn_v_w", "L1_xattn_cproj_w",
                  "L2_xattn_Wq", None, "L2_xattn_Wo"]

        sem = lambda n: ctx.enter_context(nc.semaphore(n))
        loaded = [sem(f"w0_loaded{i}") for i in range(4)]
        loaded1 = [sem(f"w1_loaded{i}") for i in range(7)]
        wk2_loaded, wv2_loaded = sem("wk2_loaded"), sem("wv2_loaded")
        fc_loaded, pj_loaded = sem("fc_loaded"), sem("pj_loaded")
        stacked, rows_loaded = sem("stacked"), sem("rows_loaded")
        consts, dve_step, act_step = sem("consts"), sem("dve_step"), sem("act_step")
        high0, low0 = sem("high0"), sem("low0")
        wo_turned, wo_high, wo_low = sem("wo_turned"), sem("wo_high"), sem("wo_low")
        m_full, m_high = sem("m_full"), sem("m_high")
        cols_turned = sem("cols_turned")
        scaled2, high1 = sem("scaled2"), sem("high1")
        cleared = sem("cleared")
        with nc.Block() as block:
            @block.sync
            def _(sp):
                for n in range(4):
                    sp.dma_start(stage[n][:, :, :], a[names0[n]].rearrange("(k p) n -> p k n", p=P)).then_inc(loaded[n], 16)
                for n in range(7):
                    if n == 5:
                        for k in range(KT):
                            for q in range(4):
                                sp.dma_start(stage1[5][:, k, :].rearrange("p (h g d) -> p h g d", h=8, g=4)[:, :, q, :],
                                             a["L2_xattn_Wk"][k * P:(k + 1) * P, :].rearrange("p (h d) -> p h d", d=8)
                                             ).then_inc(wk2_loaded, 16)
                        continue
                    sp.dma_start(stage1[n][:, :, :], a[names1[n]].rearrange("(k p) n -> p k n", p=P)).then_inc(loaded1[n], 16)
                sp.dma_start(stage_v[:, :, :], a["L2_xattn_Wv"].rearrange("(k p) n -> p k n", p=P)).then_inc(wv2_loaded, 16)
                sp.dma_start(stage_fc[:, :, :], a["L1_xattn_fc_w"].rearrange("(k p) n -> p k n", p=P)).then_inc(fc_loaded, 16)
                sp.dma_start(stage_pj[:, :, :], a["L1_xattn_proj_w"].rearrange("(m p) n -> p m n", p=P)).then_inc(pj_loaded, 16)
                sp.wait_ge(rows_loaded, 16 * (len(ROWS) + 2))

            @block.scalar
            def _(act):
                for stack, at, tile in ((STACK_A, atA, stackA), (STACK_B, atB, stackB)):
                    for name, n in stack:
                        if name == "L2_xattn_bk":
                            src = a[name].rearrange("(r h d) -> r h d", r=2, d=8)
                            for q in range(4):
                                act.dma_start(tile[at[name]:at[name] + 2, :].rearrange("r (h g d) -> r h g d", g=4, d=8)[:, :, q, :],
                                              src).then_inc(stacked, 16)
                        else:
                            v = a[name]
                            if len(v.shape) == 4:
                                v = v.rearrange("a b h k -> (a b h k)")
                            act.dma_start(tile[at[name]:at[name] + n, :], v.rearrange("(r p) -> r p", p=P)).then_inc(stacked, 16)
                for i, name in enumerate(ROWS):
                    act.dma_start(rows[:, i, :], a[name][None, :].broadcast_to([P, D])).then_inc(rows_loaded, 16)
                act.dma_start(bv2[:, :], a["L2_xattn_bv"][None, :].broadcast_to([P, 64])).then_inc(rows_loaded, 16)
                act.dma_start(alpha[:, :], a["L0_xattn_alpha"][None, :].broadcast_to([P, 1])).then_inc(rows_loaded, 16)
                for n in range(3):
                    act.wait_ge(loaded[n], 16)
                    nc.scalar.activation(w0[n][:, 0], stage[n][:, :, :], ACT.Copy).then_inc(high0, 1)
                act.wait_ge(wo_turned, 1)
                nc.scalar.activation(w0[3][:, 0], Ab[0][:, :].rearrange("p (k n) -> p k n", k=KT), ACT.Copy).then_inc(wo_high, 1)
                for n, (full, dst) in enumerate(((Sb[0], m0w), (Sb[1], v0w))):
                    act.wait_ge(m_full, n + 1)
                    nc.scalar.activation(dst[:, 0], full[:, :].rearrange("p (k n) -> p k n", k=KT), ACT.Copy).then_inc(m_high, 1)
                for n in range(7):
                    if n == 5:
                        act.wait_ge(wk2_loaded, 16 * 4 * KT)
                    else:
                        act.wait_ge(loaded1[n], 16)
                    if n == 4:
                        act.wait_ge(scaled2, 1)
                    nc.scalar.activation((w1 + w2)[n][:, 0], stage1[n][:, :, :], ACT.Copy).then_inc(high1, 1)
                act.wait_ge(wv2_loaded, 16)
                nc.scalar.activation(w2v[:, 0], stage_v[:, :, :], ACT.Copy).then_inc(high1, 1)
                act.wait_ge(fc_loaded, 16)
                nc.scalar.activation(fcw[:, 0], stage_fc[:, :, :], ACT.Copy).then_inc(high1, 1)
                act.wait_ge(pj_loaded, 16)
                nc.scalar.activation(pjw[:, 0], stage_pj[:, :, :], ACT.Copy).then_inc(high1, 1)

            @block.gpsimd
            def _(pool):
                nc.gpsimd.memset(ident[:, :], 0.0).then_inc(cleared, 1)
                nc.gpsimd.memset(ones[:, :], 0.0).then_inc(cleared, 1)
                nc.gpsimd.memset(neg_half[:, :], -0.5)
                pool.wait_ge(cleared, 1)
                nc.gpsimd.affine_select(out=ident[:, :], in_=ident[:, :], compare_op=ALU.not_equal, fill=1.0,
                                        base=0, pattern=[[-1, P]], channel_multiplier=1).then_inc(consts, 1)
                pool.wait_ge(cleared, 2)
                nc.gpsimd.memset(ones[0:1, :], 1.0).then_inc(consts, 1)
                nc.gpsimd.memset(v0[:, :, D:D + 1], 1.0)
                nc.gpsimd.memset(v1[:, :, :, 16:17], 1.0)
                nc.gpsimd.memset(v2[:, :, :, 8:9], 1.0)

            @block.vector
            def _(dve):
                dve.wait_ge(consts, 1)
                nc.vector.tensor_copy(identR[:, :], ident[:, :])
                nc.vector.tensor_reduce(hmask1[:, :], ident[:, :].rearrange("p (h d) -> p h d", d=16), AX_X, ALU.add)
                nc.vector.tensor_reduce(hmask2[:, :], ident[:, :].rearrange("p (h d) -> p h d", d=8), AX_X, ALU.add)
                dve.wait_ge(consts, 2)
                nc.vector.tensor_copy(one_row[:, :], ones[:, :])
                nc.vector.memset(key_mask[:, :].bitcast(F32), 0.0)
                for n in range(3):
                    dve.wait_ge(high0, n + 1)
                    nc.vector.tensor_tensor(w0[n][:, 1], stage[n][:, :, :], w0[n][:, 0].bitcast(F32), ALU.subtract).then_inc(low0, 1)
                dve.wait_ge(wo_high, 1)
                nc.vector.tensor_tensor(w0[3][:, 1], Ab[0][:, :].rearrange("p (k n) -> p k n", k=KT),
                                        w0[3][:, 0].bitcast(F32), ALU.subtract).then_inc(wo_low, 1)
                for n, (full, dst) in enumerate(((Sb[0], m0w), (Sb[1], v0w))):
                    dve.wait_ge(m_high, n + 1)
                    nc.vector.tensor_tensor(dst[:, 1], full[:, :].rearrange("p (k n) -> p k n", k=KT),
                                            dst[:, 0].bitcast(F32), ALU.subtract)
                dve.wait_ge(cols_turned, 1)
                nc.vector.tensor_copy(colsA[:, :], Tb[0][:, 0:nA]).then_inc(dve_step, 1)
                dve.wait_ge(cols_turned, 2)
                nc.vector.tensor_copy(colsB[:, :], Tb[1][:, 0:nB])
                dve.wait_ge(dve_step, 1)
                nc.vector.tensor_scalar(colsA[:, atA["L2_xattn_bq"]:atA["L2_xattn_bq"] + 2],
                                        colsA[:, atA["L2_xattn_bq"]:atA["L2_xattn_bq"] + 2], 8 ** -0.5, None, ALU.mult)
                dve.wait_ge(loaded1[4], 16)
                nc.vector.tensor_scalar(stage1[4][:, :, :], stage1[4][:, :, :], 8 ** -0.5, None, ALU.mult).then_inc(scaled2, 1)
                dsts = [t for t in w1 + w2] + [w2v, fcw, pjw]
                srcs = stage1 + [stage_v, stage_fc, stage_pj]
                for n, (s, d) in enumerate(zip(srcs, dsts)):
                    dve.wait_ge(high1, n + 1)
                    nc.vector.tensor_tensor(d[:, 1], s[:, :, :], d[:, 0].bitcast(F32), ALU.subtract)

            @block.tensor
            def _(pe):
                pe.wait_ge(consts, 1)
                pe.wait_ge(loaded[3], 16)
                for kt in range(KT):
                    for mt in range(KT):
                        last = nc.tensor.transpose(Ab[0][:, kt * D + mt * P:kt * D + (mt + 1) * P],
                                                   stage[3][:, mt, kt * P:(kt + 1) * P], ident[:, :])
                last.then_inc(wo_turned, 1)
                pe.wait_ge(high0, 3)
                pe.wait_ge(low0, 3)
                for mt in range(KT):
                    for kt in range(KT):
                        last = products(pe, Sb[0][:, mt * D:(mt + 1) * D], pair(w0[0], kt, slice(mt * P, (mt + 1) * P)),
                                        pair(w0[1], kt), kt == 0, kt == KT - 1)
                last.then_inc(m_full, 1)
                pe.wait_ge(wo_high, 1)
                pe.wait_ge(wo_low, 1)
                for mt in range(KT):
                    for kt in range(KT):
                        last = products(pe, Sb[1][:, mt * D:(mt + 1) * D], pair(w0[2], kt, slice(mt * P, (mt + 1) * P)),
                                        pair(w0[3], kt), kt == 0, kt == KT - 1)
                last.then_inc(m_full, 1)
                pe.wait_ge(stacked, 16 * (len(STACK_A) + 3 + len(STACK_B)))
                nc.tensor.transpose(Tb[0][:, 0:nA], stackA[0:nA, :], ident[0:nA, 0:nA]).then_inc(cols_turned, 1)
                nc.tensor.transpose(Tb[1][:, 0:nB], stackB[0:nB, :], ident[0:nB, 0:nB]).then_inc(cols_turned, 1)

        cT = sb("cT", [P, 2, KT, TOK], R32, s1)
        qT = sb("qT", [P, 2, KT, TOK], R32, s1)
        kT = sb("kT", [P, 2, KT, TOK], R32, s1)
        km = sb("km", [P, 2, 2, 4, TOK], R32, s1)
        E = sb("E", [P, EXPS, 4, P], F32, s1)
        PT = sb("PT", [P, 2, 4, P], F32, s1)
        o = sb("o", [P, NB, D], F32, s1)
        mask2f = g[:, 0, :].rearrange("p (b t) -> p b t", b=NB)
        mask2 = sb("mask2", [P, 2, NB, P], R32, s1)
        mask1b = sb("mask1b", [1, TOK], U8, s1)
        mx = sb("mx", [P, EXPS, 4], F32, s1)
        r0 = sb("r0", [P, NB], F32, s1)
        r1 = sb("r1", [P, NB, 4], F32, s1)
        s1.close()

        sem = lambda n: ctx.enter_context(nc.semaphore(n))
        S = {n: sem(n) for n in (
            "c_loaded", "x_loaded", "mask1_loaded", "mask2_loaded", "T_full", "A_full", "S_full", "O_full",
            "T_act", "T_dve", "A_act", "A_dve", "S_sub", "O_read", "P_ready", "pv_done",
            "km_high", "km_low", "norm_ready", "var_ready", "rstd_ready", "x_biased", "g_ready", "g_high",
            "g_low", "g_used", "masks_ready", "vstep", "x_out")}

        LAYERS = {1: dict(hd=16, hg=4, scale=0.25, v=v1, hmask=hmask1, kbias="L1_xattn_k_b"),
                  2: dict(hd=8, hg=8, scale=1.0, v=v2, hmask=hmask2, kbias="L2_xattn_bk")}
        for n, L in LAYERS.items():
            L["S"], L["T"], L["O"] = first(S_FILLS, f"s{n}"), first(T_FILLS, f"p{n}"), first(O_FILLS, f"pv{n}")
            L["km"] = 0 if n == 1 else 4
            L["G"] = L["hg"] * NB
            L["kfill"] = first(A_FILLS, f"k{n}")
            L["heads_kt"] = P // L["hd"]

        def T_free(pe, fills, n):
            if n >= 2:
                pe.wait_ge(S["T_act"], n - 1)
                if splits_in(fills, n - 1):
                    pe.wait_ge(S["T_dve"], splits_in(fills, n - 1))

        def A_free(pe, fills, n):
            if n >= 2:
                for s, e in (("A_act", "A"), ("A_dve", "V")):
                    if read_by(fills, n - 1, e):
                        pe.wait_ge(S[s], read_by(fills, n - 1, e))

        def turn(pe, src, fills, n):
            for kt in range(KT):
                T_free(pe, fills, n + kt)
                for b in range(NB):
                    last = nc.tensor.transpose(Tb[(n + kt) % 2][:, b * P:(b + 1) * P],
                                               src[:, b, kt * P:(kt + 1) * P], ident[:, :])
                last.then_inc(S["T_full"], 1)

        def split_high(act, dst, n):
            for kt in range(KT):
                act.wait_ge(S["T_full"], n + kt + 1)
                nc.scalar.activation(dst[:, 0, kt, :], Tb[(n + kt) % 2][:, :], ACT.Copy).then_inc(S["T_act"], 1)

        def split_low(dve, dst, n):
            for kt in range(KT):
                dve.wait_ge(S["T_act"], n + kt + 1)
                nc.vector.tensor_tensor(dst[:, 1, kt, :], Tb[(n + kt) % 2][:, :], dst[:, 0, kt, :].bitcast(F32),
                                        ALU.subtract).then_inc(S["T_dve"], 1)

        def a_free(eng, what, fills):
            eng.wait_ge(S["A_full"], fA[what] + fills)

        def project_T(pe, w, src, fills, n):
            for mt in range(KT):
                A_free(pe, fills, n + mt)
                for kt in range(KT):
                    last = products(pe, Ab[(n + mt) % 2][:, :], pair(w, kt, slice(mt * P, (mt + 1) * P)), pair(src, kt),
                                    kt == 0, kt == KT - 1)
                last.then_inc(S["A_full"], 1)
            return last

        def project(pe, w, width, src, fills, n):
            per = 512 // width if width < D else 2
            per = min(per, NB)
            for f in range(NB // per):
                A_free(pe, fills, n + f)
                for i in range(per):
                    b = f * per + i
                    for kt in range(KT):
                        last = products(pe, Ab[(n + f) % 2][:, i * width:(i + 1) * width],
                                        pair(src, kt, slice(b * P, (b + 1) * P)), pair(w, kt), kt == 0, kt == KT - 1)
                last.then_inc(S["A_full"], 1)
            return last

        def A_high(act, dst, n, bias=None):
            for mt in range(KT):
                act.wait_ge(S["A_full"], n + mt + 1)
                if bias is None:
                    i = nc.scalar.activation(dst[:, 0, mt, :], Ab[(n + mt) % 2][:, :], ACT.Copy)
                else:
                    i = nc.scalar.activation(dst[:, 0, mt, :], Ab[(n + mt) % 2][:, :], ACT.Identity, bias=col(bias, mt))
                i.then_inc(S["A_act"], 1)

        def A_low(dve, dst, n, bias=None):
            for mt in range(KT):
                dve.wait_ge(S["A_act"], read_by(A_FILLS, n + mt + 1, "A"))
                if bias is None:
                    i = nc.vector.tensor_tensor(dst[:, 1, mt, :], Ab[(n + mt) % 2][:, :], dst[:, 0, mt, :].bitcast(F32),
                                                ALU.subtract)
                else:
                    i = nc.vector.scalar_tensor_tensor(out=dst[:, 1, mt, :], in0=Ab[(n + mt) % 2][:, :], scalar=col(bias, mt),
                                                       in1=dst[:, 0, mt, :].bitcast(F32), op0=ALU.add, op1=ALU.subtract)
                i.then_inc(S["A_dve"], 1)

        def attend_pe(pe, L):
            G = L["G"]

            def scores(i):
                hg, b = divmod(i, NB)
                n = L["S"] + i
                kt = hg * 4 // L["heads_kt"]
                if n >= 2:
                    pe.wait_ge(S["S_sub"], n - 1)
                if b == 0:
                    pe.wait_ge(S["km_high"], 4 * (L["km"] + hg + 1))
                    pe.wait_ge(S["km_low"], 4 * (L["km"] + hg + 1))
                bank = Sb[n % 2][:, :].rearrange("p (h t) -> p h t", h=4)
                buf = (L["km"] + hg) % 2
                products(pe, bank, pair(qT, kt, slice(b * P, (b + 1) * P)),
                         (km[:, buf, 0, :, b * P:(b + 1) * P], km[:, buf, 1, :, b * P:(b + 1) * P]), True, False)
                if L["hd"] == 16:
                    m = key_mask[:, None, b * P:(b + 1) * P].broadcast_to([P, 4, P])
                    last = pe.matmul(bank, one_row[:, :], m, start=False, stop=True)
                else:
                    pe.matmul(bank, identR[:, :], mask2[:, 0, b, None, :].broadcast_to([P, 4, P]), start=False, stop=False)
                    last = pe.matmul(bank, identR[:, :], mask2[:, 1, b, None, :].broadcast_to([P, 4, P]), start=False, stop=True)
                last.then_inc(S["S_full"], 1)

            def turn_probs(i):
                n = L["T"] + i
                T_free(pe, T_FILLS, n)
                pe.wait_ge(S["P_ready"], L["S"] + i + 1)
                for h in range(4):
                    last = nc.tensor.transpose(Tb[n % 2][:, h * P:(h + 1) * P], E[:, (L["S"] + i) % EXPS, h, :], ident[:, :])
                last.then_inc(S["T_full"], 1)

            def values(i):
                hg, b = divmod(i, NB)
                o_n, w = L["O"] + hg, L["hd"] + 1
                pe.wait_ge(S["T_act"], L["T"] + i + 1)
                if b == 0:
                    pe.wait_ge(S["O_read"], o_n - 1)
                bank = Ob[o_n % 2][:, 0:NB * 4 * w].rearrange("p (b h d) -> p b h d", b=NB, h=4)
                for h in range(4):
                    vh = hg * 4 + h if L["hd"] == 16 else hg
                    last = pe.matmul(bank[:, b, h, :], PT[:, (L["S"] + i) % 2, h, :], L["v"][:, b, vh, :], start=True, stop=True)
                last.then_inc(S["pv_done"], 1)

            for i in range(G + 3):
                if i < G:
                    scores(i)
                if 2 <= i < G + 2:
                    turn_probs(i - 2)
                if i >= 3:
                    values(i - 3)

        def attend_act(act, L):
            G = L["G"]
            for i in range(G + 2):
                if i < G:
                    act.wait_ge(S["S_sub"], L["S"] + i + 1)
                    e = E[:, (L["S"] + i) % EXPS]
                    nc.scalar.activation(e, e, ACT.Exp, scale=L["scale"]).then_inc(S["P_ready"], 1)
                if i >= 2:
                    evict_probs(act, L["S"] + i - 2, L["T"] + i - 2)

        def evict_probs(act, s, t):
            act.wait_ge(S["T_full"], t + 1)
            if s >= 2:
                act.wait_ge(S["pv_done"], s - 1)
            nc.scalar.activation(PT[:, s % 2], Tb[t % 2][:, :].rearrange("p (h t) -> p h t", h=4), ACT.Copy).then_inc(S["T_act"], 1)

        def soften(dve, s, t):
            bank = Sb[s % 2][:, :].rearrange("p (h t) -> p h t", h=4)
            dve.wait_ge(S["S_full"], s + 1)
            nc.vector.tensor_reduce(mx[:, s % EXPS], bank, AX_X, ALU.max).then_inc(S["vstep"], 1)
            steps[0] += 1
            dve.wait_ge(S["vstep"], steps[0])
            if s >= EXPS:
                dve.wait_ge(S["T_full"], T_of_S[s - EXPS] + 1)
            nc.vector.tensor_tensor(E[:, s % EXPS], bank, mx[:, s % EXPS, :, None].broadcast_to([P, 4, P]),
                                    ALU.subtract).then_inc(S["S_sub"], 1)

        T_of_S = [first(T_FILLS, "p0")] + [first(T_FILLS, "p1") + i for i in range(16)] + [first(T_FILLS, "p2") + i for i in range(32)]
        steps = [0]

        def mask_low(dve, L, hg):
            if L["km"] + hg >= 2:
                dve.wait_ge(S["S_full"], km_used(L, hg))
            for h in range(4):
                kt, j = divmod(hg * 4 + h, L["heads_kt"])
                nc.vector.tensor_scalar(km[:, (L["km"] + hg) % 2, 1, h, :], kT[:, 1, kt, :].bitcast(F32), L["hmask"][:, j:j + 1],
                                        None, ALU.mult).then_inc(S["km_low"], 1)

        def km_used(L, hg):
            n = L["km"] + hg - 2
            return 1 + NB * (n + 1)

        def mask_high(pool, L, hg):
            if L["km"] + hg >= 2:
                pool.wait_ge(S["S_full"], km_used(L, hg))
            for h in range(4):
                kt, j = divmod(hg * 4 + h, L["heads_kt"])
                nc.gpsimd.tensor_scalar(km[:, (L["km"] + hg) % 2, 0, h, :], kT[:, 0, kt, :].bitcast(F32), L["hmask"][:, j:j + 1],
                                        1.0, ALU.mult, ALU.mult).then_inc(S["km_high"], 1)

        def attend_dve(dve, L):
            w = L["hd"] + 1

            def normalise(hg):
                o_n = L["O"] + hg
                dve.wait_ge(S["pv_done"], L["S"] + NB * (hg + 1))
                dve.wait_ge(S["O_read"], o_n)
                bank = Ob[o_n % 2][:, 0:NB * 4 * w].rearrange("p (b h d) -> p b h d", b=NB, h=4)
                nc.vector.reciprocal(r1[:, :, :], bank[:, :, :, w - 1]).then_inc(S["vstep"], 1)
                steps[0] += 1
                dve.wait_ge(S["vstep"], steps[0])
                dst = o[:, :, hg * 4 * L["hd"]:(hg + 1) * 4 * L["hd"]].rearrange("p b (h d) -> p b h d", h=4)
                nc.vector.tensor_tensor(dst, bank[:, :, :, 0:w - 1], r1[:, :, :, None].broadcast_to([P, NB, 4, w - 1]),
                                        ALU.mult).then_inc(S["O_read"], 1)

            dve.wait_ge(S["A_dve"], read_by(A_FILLS, L["kfill"] + KT, "V"))
            mask_low(dve, L, 0)
            for i in range(L["G"]):
                hg, b = divmod(i, NB)
                if b == 0 and hg + 1 < L["hg"]:
                    mask_low(dve, L, hg + 1)
                soften(dve, L["S"] + i, L["T"] + i)
                if b == NB - 1 and hg >= 1:
                    normalise(hg - 1)
            normalise(L["hg"] - 1)

        norms = [0]

        def norm(dve, src, dst, nb, w):
            for b in range(nb):
                nc.vector.bn_stats(stats[:, b], src(b)).then_inc(S["vstep"], 1)
            steps[0] += nb
            dve.wait_ge(S["vstep"], steps[0])
            for b in range(nb):
                nc.vector.bn_aggr(mv[:, b], stats[:, b]).then_inc(S["var_ready"], 1)
            norms[0] += 1
            dve.wait_ge(S["var_ready"], nb * norms[0])
            for b in range(nb):
                nc.vector.scalar_tensor_tensor(out=dst[:, b], in0=src(b), scalar=mv[:, b, 0:1], in1=w,
                                               op0=ALU.subtract, op1=ALU.mult).then_inc(S["vstep"], 1)
            steps[0] += nb
            dve.wait_ge(S["vstep"], steps[0])
            dve.wait_ge(S["rstd_ready"], norms[0])

        def power(pool, n, nb, eps):
            pool.wait_ge(S["var_ready"], nb * n)
            nc.gpsimd.tensor_scalar(var[:, 0:nb], mv[:, 0:nb, 1], eps, 1.0, ALU.add, ALU.mult).then_inc(S["pool_step"], 1)
            psteps[0] += 1
            pool.wait_ge(S["pool_step"], psteps[0])
            nc.gpsimd.tensor_tensor(rstd[:, 0:nb], var[:, 0:nb], neg_half[:, 0:nb], ALU.pow).then_inc(S["rstd_ready"], 1)

        psteps = [0]
        S["pool_step"] = sem("pool_step")

        def mlp_pe(pe, fills, n, o_n):
            def up(m):
                A_free(pe, fills, n + m)
                for kt in range(KT):
                    last = products(pe, Ab[(n + m) % 2][:, :], pair(fcw, kt, slice(m * P, (m + 1) * P)), pair(aT, kt),
                                    kt == 0, kt == KT - 1)
                last.then_inc(S["A_full"], 1)
                return last

            def down(m):
                pe.wait_ge(S["g_high"], m + 1)
                pe.wait_ge(S["g_low"], m + 1)
                if m == 0 and o_n:
                    pe.wait_ge(S["O_read"], o_n)
                for b in range(NB):
                    bank = Ob[(o_n + b // 2) % 2][:, (b % 2) * D:(b % 2 + 1) * D]
                    left = pair(gT[:, m % 2], slice(b * P, (b + 1) * P))
                    right = pair(pjw, m)
                    pe.matmul(bank, left[0], right[0], start=(m == 0 and b % 2 == 0), stop=False, skip_group_check=True)
                    pe.matmul(bank, left[1], right[0], start=False, stop=False, skip_group_check=True)
                    last = pe.matmul(bank, left[0], right[1], start=False, stop=(m == MT - 1), skip_group_check=True)
                last.then_inc(S["g_used"], 1)

            for m in range(MT + 2):
                if m < MT:
                    up(m)
                if m >= 2:
                    down(m - 2)

        def mlp_act(act, fills, n, func, bias):
            for m in range(MT):
                act.wait_ge(S["A_full"], n + m + 1)
                if m >= 2:
                    act.wait_ge(S["g_low"], m - 1)
                    act.wait_ge(S["g_used"], m - 1)
                nc.scalar.activation(g[:, m % 2], Ab[(n + m) % 2][:, :], func, bias=col(bias, m)).then_inc(S["A_act"], 1)
                act.wait_ge(S["A_act"], read_by(fills, n + m + 1, "A"))
                nc.scalar.activation(gT[:, m % 2, 0], g[:, m % 2], ACT.Copy).then_inc(S["g_high"], 1)

        def mlp_dve(dve):
            for m in range(MT):
                dve.wait_ge(S["g_high"], m + 1)
                nc.vector.tensor_tensor(gT[:, m % 2, 1], g[:, m % 2], gT[:, m % 2, 0].bitcast(F32), ALU.subtract).then_inc(S["g_low"], 1)

        def mlp_add(dve, o_n):
            dve.wait_ge(S["g_used"], MT)
            for f in range(2):
                nc.vector.tensor_tensor(xh[:, 2 * f:2 * f + 2], Ob[(o_n + f) % 2][:, :].rearrange("p (b d) -> p b d", b=2),
                                        xh[:, 2 * f:2 * f + 2], ALU.add).then_inc(S["O_read"], 1)

        fT = {n: first(T_FILLS, n) for n in ("c", "x", "p0", "z1", "ctx1", "z2", "x2", "ctx2")}
        fA = {n: first(A_FILLS, n) for n in ("q0", "v0", "k1", "v1", "q1", "o1", "k2", "v2", "fc", "q2", "o2")}

        with nc.Fori(0, HALVES) as half:
            with nc.Block() as block:
                @block.sync
                def _(sp):
                    sp.dma_start(o[:, :, :], a["ctx_2048"][bass.ds(half * NB, NB)].rearrange("b t d -> t b d")).then_inc(S["c_loaded"], 16)
                    sp.dma_start(xh[:, :, :], a["x"][bass.ds(half * NB, NB)].rearrange("b t d -> t b d")).then_inc(S["x_loaded"], 16)
                    sp.dma_start(mask1b[:, :], a["mask_BxS2_bf1"][bass.ds(half * NB, NB)].rearrange("b t -> (b t)")[None, :]).then_inc(S["mask1_loaded"], 16)
                    sp.dma_start(mask2f[:, :, :], a["mask_Bx1xSxS2_ff0"][bass.ds(half * NB, NB)].rearrange("b o q t -> q (b o) t")).then_inc(S["mask2_loaded"], 16)

                @block.tensor
                def _(pe):
                    pe.wait_ge(S["c_loaded"], 16)
                    turn(pe, o, T_FILLS, fT["c"])
                    pe.wait_ge(S["x_loaded"], 16)
                    turn(pe, xh, T_FILLS, fT["x"])
                    pe.wait_ge(S["T_act"], 4)
                    pe.wait_ge(S["T_dve"], 4)
                    project_T(pe, m0w, aT, A_FILLS, fA["q0"])
                    project(pe, v0w, D, cT, A_FILLS, fA["v0"])
                    pe.wait_ge(S["A_act"], 2)
                    pe.wait_ge(S["A_dve"], 2)
                    for b in range(NB):
                        for kt in range(KT):
                            last = products(pe, Sb[0][:, b * P:(b + 1) * P], pair(qT, kt, slice(b * P, (b + 1) * P)),
                                            pair(cT, kt, slice(b * P, (b + 1) * P)), kt == 0, kt == KT - 1)
                    last.then_inc(S["S_full"], 1)
                    project_T(pe, w1[1], cT, A_FILLS, fA["k1"])
                    project(pe, w1[2], D, cT, A_FILLS, fA["v1"])
                    T_free(pe, T_FILLS, fT["p0"])
                    pe.wait_ge(S["P_ready"], 1)
                    for b in range(NB):
                        last = nc.tensor.transpose(Tb[fT["p0"] % 2][:, b * P:(b + 1) * P], E[:, 0, b, :], ident[:, :])
                    last.then_inc(S["T_full"], 1)
                    pe.wait_ge(S["T_act"], fT["p0"] + 1)
                    pe.wait_ge(S["A_dve"], read_by(A_FILLS, fA["v0"] + 2, "V"))
                    for b in range(NB):
                        if b >= 2:
                            pe.wait_ge(S["O_read"], b - 1)
                        last = pe.matmul(Ob[b % 2][:, 0:D + 1], PT[:, 0, b, :], v0[:, b, :], start=True, stop=True)
                        last.then_inc(S["O_full" if b < NB - 1 else "pv_done"], 1)
                    pe.wait_ge(S["norm_ready"], NB)
                    turn(pe, z, T_FILLS, fT["z1"])
                    pe.wait_ge(S["T_act"], fT["z1"] + KT)
                    pe.wait_ge(S["T_dve"], splits_in(T_FILLS, fT["z1"] + KT))
                    project_T(pe, w1[0], aT, A_FILLS, fA["q1"])
                    pe.wait_ge(S["A_act"], read_by(A_FILLS, fA["q1"] + KT, "A"))
                    pe.wait_ge(S["A_dve"], read_by(A_FILLS, fA["q1"] + KT, "V"))
                    pe.wait_ge(S["masks_ready"], 3)
                    attend_pe(pe, LAYERS[1])
                    pe.wait_ge(S["O_read"], LAYERS[1]["O"] + 4)
                    turn(pe, o, T_FILLS, fT["ctx1"])
                    pe.wait_ge(S["T_act"], fT["ctx1"] + KT)
                    pe.wait_ge(S["T_dve"], splits_in(T_FILLS, fT["ctx1"] + KT))
                    project(pe, w1[3], D, aT, A_FILLS, fA["o1"])
                    project_T(pe, w2[1], cT, A_FILLS, fA["k2"])
                    project(pe, w2v, 64, cT, A_FILLS, fA["v2"])
                    pe.wait_ge(S["norm_ready"], 2 * NB)
                    turn(pe, z, T_FILLS, fT["z2"])
                    pe.wait_ge(S["T_act"], fT["z2"] + KT)
                    pe.wait_ge(S["T_dve"], splits_in(T_FILLS, fT["z2"] + KT))
                    mlp_pe(pe, A_FILLS, fA["fc"], first(O_FILLS, "mlp"))
                    pe.wait_ge(S["O_read"], LAYERS[2]["O"])
                    turn(pe, xh, T_FILLS, fT["x2"])
                    pe.wait_ge(S["T_act"], fT["x2"] + KT)
                    pe.wait_ge(S["T_dve"], splits_in(T_FILLS, fT["x2"] + KT))
                    project_T(pe, w2[0], aT, A_FILLS, fA["q2"])
                    pe.wait_ge(S["A_act"], read_by(A_FILLS, fA["q2"] + KT, "A"))
                    pe.wait_ge(S["A_dve"], read_by(A_FILLS, fA["q2"] + KT, "V"))
                    attend_pe(pe, LAYERS[2])
                    pe.wait_ge(S["O_read"], LAYERS[2]["O"] + 8)
                    turn(pe, o, T_FILLS, fT["ctx2"])
                    pe.wait_ge(S["T_act"], fT["ctx2"] + KT)
                    pe.wait_ge(S["T_dve"], splits_in(T_FILLS, fT["ctx2"] + KT))
                    project(pe, w2[2], D, aT, A_FILLS, fA["o2"])

                @block.scalar
                def _(act):
                    split_high(act, cT, fT["c"])
                    split_high(act, aT, fT["x"])
                    A_high(act, qT, fA["q0"])
                    act.wait_ge(S["S_sub"], 1)
                    nc.scalar.activation(E[:, 0], E[:, 0], ACT.Exp, scale=D ** -0.5).then_inc(S["P_ready"], 1)
                    A_high(act, kT, fA["k1"], "L1_xattn_k_b")
                    evict_probs(act, 0, fT["p0"])
                    a_free(act, "q0", 2)
                    split_high(act, aT, fT["z1"])
                    act.wait_ge(S["S_full"], 1)
                    A_high(act, qT, fA["q1"], "L1_xattn_q_b")
                    attend_act(act, LAYERS[1])
                    a_free(act, "q1", 2)
                    split_high(act, aT, fT["ctx1"])
                    act.wait_ge(S["km_high"], 16)
                    act.wait_ge(S["km_low"], 16)
                    A_high(act, kT, fA["k2"], "L2_xattn_bk")
                    a_free(act, "o1", 2)
                    split_high(act, aT, fT["z2"])
                    mlp_act(act, A_FILLS, fA["fc"], ACT.Gelu_apprx_tanh, "L1_xattn_fc_b")
                    a_free(act, "fc", MT)
                    split_high(act, aT, fT["x2"])
                    act.wait_ge(S["S_full"], LAYERS[2]["S"])
                    A_high(act, qT, fA["q2"], "L2_xattn_bq")
                    attend_act(act, LAYERS[2])
                    a_free(act, "q2", 2)
                    split_high(act, aT, fT["ctx2"])

                @block.gpsimd
                def _(pool):
                    psteps[0] = 0
                    power(pool, 1, NB, LN_EPS)
                    pool.wait_ge(S["norm_ready"], NB)
                    nc.gpsimd.tensor_tensor(xh[:, :, :], xh[:, :, :], row("L1_xattn_cproj_b")[:, None, :].broadcast_to([P, NB, D]),
                                            ALU.add).then_inc(S["x_biased"], 1)
                    pool.wait_ge(S["A_act"], read_by(A_FILLS, fA["k1"] + KT, "A"))
                    for hg in range(4):
                        mask_high(pool, LAYERS[1], hg)
                    power(pool, 2, NB, LN_EPS)
                    pool.wait_ge(S["norm_ready"], 2 * NB)
                    nc.gpsimd.tensor_tensor(xh[:, :, :], xh[:, :, :], row("L1_xattn_proj_b")[:, None, :].broadcast_to([P, NB, D]),
                                            ALU.add).then_inc(S["x_biased"], 1)
                    pool.wait_ge(S["A_act"], read_by(A_FILLS, fA["k2"] + KT, "A"))
                    for hg in range(2):
                        mask_high(pool, LAYERS[2], hg)
                    pool.wait_ge(S["T_full"], fT["x2"] + KT)
                    pool.wait_ge(S["O_read"], LAYERS[2]["O"])
                    nc.gpsimd.tensor_tensor(xh[:, :, :], xh[:, :, :], row("L2_xattn_bo")[:, None, :].broadcast_to([P, NB, D]),
                                            ALU.add).then_inc(S["x_biased"], 1)
                    for hg in range(2, 8):
                        mask_high(pool, LAYERS[2], hg)
                    power(pool, 3, NB, LN2_EPS)

                @block.vector
                def _(dve):
                    steps[0] = norms[0] = 0
                    dve.wait_ge(S["mask1_loaded"], 16)
                    nc.vector.tensor_scalar(key_mask[0:1, :], mask1b[:, :], 1.0, BIG, ALU.subtract, ALU.mult).then_inc(S["masks_ready"], 1)
                    dve.wait_ge(S["mask2_loaded"], 16)
                    nc.vector.tensor_copy(mask2[:, 0], mask2f[:, :, :]).then_inc(S["masks_ready"], 1)
                    dve.wait_ge(S["masks_ready"], 2)
                    nc.vector.tensor_tensor(mask2[:, 1], mask2f[:, :, :], mask2[:, 0].bitcast(F32), ALU.subtract).then_inc(S["masks_ready"], 1)
                    split_low(dve, cT, fT["c"])
                    split_low(dve, aT, fT["x"])
                    A_low(dve, qT, fA["q0"])
                    for f in range(2):
                        n = fA["v0"] + f
                        dve.wait_ge(S["A_full"], n + 1)
                        nc.vector.tensor_copy(v0[:, 2 * f:2 * f + 2, 0:D], Ab[n % 2][:, :].rearrange("p (b d) -> p b d", b=2)).then_inc(S["A_dve"], 1)
                    soften(dve, 0, fT["p0"])
                    A_low(dve, kT, fA["k1"], "L1_xattn_k_b")
                    for f in range(2):
                        n = fA["v1"] + f
                        dve.wait_ge(S["A_full"], n + 1)
                        nc.vector.tensor_tensor(v1[:, 2 * f:2 * f + 2, :, 0:16], Ab[n % 2][:, :].rearrange("p (b h d) -> p b h d", b=2, d=16),
                                                row("L1_xattn_v_b").rearrange("p (h d) -> p h d", d=16)[:, None].broadcast_to([P, 2, 16, 16]),
                                                ALU.add).then_inc(S["A_dve"], 1)
                    for b in range(NB):
                        if b < NB - 1:
                            dve.wait_ge(S["O_full"], b + 1)
                        else:
                            dve.wait_ge(S["pv_done"], 1)
                        nc.vector.reciprocal(r0[:, b:b + 1], Ob[b % 2][:, D:D + 1]).then_inc(S["vstep"], 1)
                        steps[0] += 1
                        dve.wait_ge(S["vstep"], steps[0])
                        nc.vector.tensor_scalar(r0[:, b:b + 1], r0[:, b:b + 1], alpha[:, 0:1], None, ALU.mult).then_inc(S["vstep"], 1)
                        steps[0] += 1
                        dve.wait_ge(S["vstep"], steps[0])
                        dve.wait_ge(S["T_full"], fT["x"] + KT)
                        nc.vector.scalar_tensor_tensor(out=xh[:, b], in0=Ob[b % 2][:, 0:D], scalar=r0[:, b:b + 1], in1=xh[:, b],
                                                       op0=ALU.mult, op1=ALU.add).then_inc(S["O_read"], 1)
                    dve.wait_ge(S["O_read"], NB)
                    norm(dve, lambda b: xh[:, b], z, NB, row("L1_xattn_ln1_w"))
                    for b in range(NB):
                        nc.vector.scalar_tensor_tensor(out=z[:, b], in0=z[:, b], scalar=rstd[:, b:b + 1], in1=row("L1_xattn_ln1_b"),
                                                       op0=ALU.mult, op1=ALU.add).then_inc(S["norm_ready"], 1)
                    split_low(dve, aT, fT["z1"])
                    A_low(dve, qT, fA["q1"], "L1_xattn_q_b")
                    attend_dve(dve, LAYERS[1])
                    split_low(dve, aT, fT["ctx1"])
                    dve.wait_ge(S["x_biased"], 1)
                    for f in range(2):
                        n = fA["o1"] + f
                        dve.wait_ge(S["A_full"], n + 1)
                        nc.vector.tensor_tensor(xh[:, 2 * f:2 * f + 2], Ab[n % 2][:, :].rearrange("p (b d) -> p b d", b=2),
                                                xh[:, 2 * f:2 * f + 2], ALU.add).then_inc(S["A_dve"], 1)
                    dve.wait_ge(S["A_dve"], read_by(A_FILLS, fA["o1"] + 2, "V"))
                    dve.wait_ge(S["T_full"], fT["z1"] + KT)
                    norm(dve, lambda b: xh[:, b], z, NB, row("L1_xattn_ln2_w"))
                    for b in range(NB):
                        nc.vector.scalar_tensor_tensor(out=z[:, b], in0=z[:, b], scalar=rstd[:, b:b + 1], in1=row("L1_xattn_ln2_b"),
                                                       op0=ALU.mult, op1=ALU.add).then_inc(S["norm_ready"], 1)
                    dve.wait_ge(S["km_low"], 16)
                    A_low(dve, kT, fA["k2"], "L2_xattn_bk")
                    n = fA["v2"]
                    dve.wait_ge(S["A_full"], n + 1)
                    nc.vector.tensor_tensor(v2[:, :, :, 0:8], Ab[n % 2][:, 0:NB * 64].rearrange("p (b h d) -> p b h d", b=NB, d=8),
                                            bv2[:, :].rearrange("p (h d) -> p h d", d=8)[:, None].broadcast_to([P, NB, 8, 8]),
                                            ALU.add).then_inc(S["A_dve"], 1)
                    split_low(dve, aT, fT["z2"])
                    mlp_dve(dve)
                    dve.wait_ge(S["x_biased"], 2)
                    mlp_add(dve, first(O_FILLS, "mlp"))
                    split_low(dve, aT, fT["x2"])
                    A_low(dve, qT, fA["q2"], "L2_xattn_bq")
                    attend_dve(dve, LAYERS[2])
                    split_low(dve, aT, fT["ctx2"])
                    dve.wait_ge(S["x_biased"], 3)
                    for f in range(2):
                        n = fA["o2"] + f
                        dve.wait_ge(S["A_full"], n + 1)
                        nc.vector.tensor_tensor(xh[:, 2 * f:2 * f + 2], Ab[n % 2][:, :].rearrange("p (b d) -> p b d", b=2),
                                                xh[:, 2 * f:2 * f + 2], ALU.add).then_inc(S["A_dve"], 1)
                    dve.wait_ge(S["A_dve"], read_by(A_FILLS, fA["o2"] + 2, "V"))
                    dve.wait_ge(S["T_full"], fT["z2"] + KT)
                    norm(dve, lambda b: xh[:, b], z, NB, row("L2_xattn_gamma"))
                    for b in range(NB):
                        nc.vector.scalar_tensor_tensor(out=x_all[:, bass.ds(half * NB + b, 1), :], in0=z[:, b:b + 1], scalar=rstd[:, b:b + 1],
                                                       in1=row("L2_xattn_beta")[:, None, :], op0=ALU.mult, op1=ALU.add).then_inc(S["x_out"], 1)
            for each in S.values():
                nc.sync.sem_clear(each)
            nc.all_engine_barrier()

        s3 = ExitStack()
        cT3 = sb("cT3", [P, 2, KT, B * P], R32, s3)
        hT3 = sb("hT3", [P, 2, KT, B * P], R32, s3)
        t3 = ExitStack()
        c3 = sb("c3", [P, B, D], F32, t3)
        z3 = sb("z3", [P, B, D], F32, t3)
        t3.close()
        wst = [sb(f"wst_{n}", [P, KT, HG3 * P], F32, s3) for n in "qkv"]
        wo_st = sb("wo_st", [P, HG3, D], F32, s3)
        w3 = [sb(f"w3_{n}", [P, 2, KT, HG3 * P], R32, s3) for n in "qkv"]
        wo3 = sb("wo3", [P, 2, HG3, D], R32, s3)
        v_row = sb("v_row", [P, HG3 * P], F32, s3)
        bias_v_row = sb("bias_v_row", [P, HG3 * P], F32, s3)
        vec = sb("vec", [P, 4, HG3], F32, s3)
        qT3 = sb("qT3", [P, 2, 2, B * P], R32, s3)
        kT3 = sb("kT3", [P, 2, 2, B, T3], R32, s3)
        vf = sb("vf", [P, 2, 2, HG3 * P], F32, s3)
        v3 = sb("v3", [P, 2, B, HG3 * P], R32, s3)
        E3 = sb("E3", [P, EXPS, 3, T3], F32, s3)
        PT3 = sb("PT3", [P, 2, 2, 3 * P], R32, s3)
        ctxT3 = sb("ctxT3", [P, 2, HG3, B * P], R32, s3)
        mx3 = sb("mx3", [P, EXPS, 3], F32, s3)
        nm3 = sb("nm3", [P, EXPS, 3], F32, s3)
        sum3 = sb("sum3", [P, EXPS, 3], F32, s3)
        rs3 = sb("rs3", [P, EXPS, 3], F32, s3)
        s3.close()
        SCALE3 = float(P) ** -0.5

        ORDER = [("q", 0, 0), ("q", 0, 1), ("k", 0, 0), ("k", 0, 1)]
        for h in range(HG3):
            after = [("q", h + 1, 0), ("q", h + 1, 1), ("k", h + 1, 0), ("k", h + 1, 1)] if h + 1 < HG3 else []
            vs = [("v", 0, f) for f in range(NB)] if h == 0 else []
            late = [("PV", h - 1, 1), ("PV", h - 1, 2)] if h else []
            ORDER += ([("S", h, 0), ("S", h, 1)] + late + vs[:3] + after[:1] + [("T", h, 0), ("S", h, 2)] + vs[3:] + after[1:2]
                      + [("T", h, 1), ("PV", h, 0)] + after[2:] + [("T", h, 2)])
        ORDER += [("PV", HG3 - 1, 1), ("PV", HG3 - 1, 2)]
        ORDER += [("out", 0, f) for f in range(NB)]
        A3 = [(w, "V" if w[0] in ("v", "out") else "AV") for w in ORDER if w[0] in ("q", "k", "v", "out")]
        A3_at = {w[0]: i for i, w in enumerate(A3)}

        sem = lambda n: ctx.enter_context(nc.semaphore(f"{n}3"))
        N = {n: sem(n) for n in (
            "wq_loaded", "wk_loaded", "wv_loaded", "wo_loaded", "rows_loaded", "rowb_loaded", "w_high", "w_low", "wo_high", "wo_low",
            "vec_ready", "v_row_ready", "A_full", "A_act", "A_dve", "bias_high", "bias_low", "v_high", "v_low",
            "S_full", "max_ready", "nm_ready", "exp_done", "r_ready", "P_ready", "T_full", "T_act", "T_dve", "pv_done",
            "ctx_high", "ctx_low")}

        def attention3(att):
            names = {n: f"L3_xattn_{n}{att + 1}" for n in ("wq", "wk", "wv", "wo", "bv", "bias_v")}
            ln_w, ln_b, bo = f"L3_xattn_ln{att + 1}_scale", f"L3_xattn_ln{att + 1}_offset", f"L3_xattn_bo{att + 1}"
            cols = colsA[:, atA["L3_xattn_bq1"]:atA["L3_xattn_bq1"] + 4 * H3] if att == 0 else colsB[:, 0:4 * H3]
            cols = cols.rearrange("p (k h) -> p k h", k=4)

            turns = ([("c", f) for f in range(4)] if att == 0 else []) + [("h", f) for f in range(4)]
            with nc.Block() as block:
                @block.sync
                def _(sp):
                    if att == 0:
                        sp.dma_start(c3[:, :, :], a["ctx_2048"].rearrange("b t d -> t b d")).then_inc(S["c_loaded"], 16)

                @block.tensor
                def _(pe):
                    for n, (what, f) in enumerate(turns):
                        if (what, f) == ("c", 0):
                            pe.wait_ge(S["c_loaded"], 16)
                        if (what, f) == ("h", 0):
                            pe.wait_ge(S["norm_ready"], B)
                        if n >= 2:
                            pe.wait_ge(S["T_act"], n - 1)
                            pe.wait_ge(S["T_dve"], n - 1)
                        kt, half = divmod(f, 2)
                        src = c3 if what == "c" else z3
                        for b in range(NB):
                            last = nc.tensor.transpose(Tb[n % 2][:, b * P:(b + 1) * P],
                                                       src[:, half * NB + b, kt * P:(kt + 1) * P], ident[:, :])
                        last.then_inc(S["T_full"], 1)

                @block.scalar
                def _(act):
                    for n, (what, f) in enumerate(turns):
                        kt, half = divmod(f, 2)
                        dst = cT3 if what == "c" else hT3
                        act.wait_ge(S["T_full"], n + 1)
                        nc.scalar.activation(dst[:, 0, kt, half * TOK:(half + 1) * TOK], Tb[n % 2][:, :], ACT.Copy).then_inc(S["T_act"], 1)

                @block.gpsimd
                def _(pool):
                    psteps[0] = 0
                    power(pool, 1, B, LN_EPS)
                    pool.wait_ge(S["norm_ready"], B)
                    nc.gpsimd.tensor_tensor(x_all[:, :, :], x_all[:, :, :], row(bo)[:, None, :].broadcast_to([P, B, D]), ALU.add)

                @block.vector
                def _(dve):
                    steps[0] = norms[0] = 0
                    norm(dve, lambda b: x_all[:, b], z3, B, row(ln_w))
                    for b in range(B):
                        nc.vector.scalar_tensor_tensor(out=z3[:, b], in0=z3[:, b], scalar=rstd[:, b:b + 1], in1=row(ln_b),
                                                       op0=ALU.mult, op1=ALU.add).then_inc(S["norm_ready"], 1)
                    for n, (what, f) in enumerate(turns):
                        kt, half = divmod(f, 2)
                        dst = cT3 if what == "c" else hT3
                        part = (kt, slice(half * TOK, (half + 1) * TOK))
                        dve.wait_ge(S["T_act"], n + 1)
                        nc.vector.tensor_tensor(dst[:, 1, part[0], part[1]], Tb[n % 2][:, :],
                                                dst[:, 0, part[0], part[1]].bitcast(F32), ALU.subtract).then_inc(S["T_dve"], 1)

            for n in ("c_loaded", "T_full", "T_act", "T_dve", "vstep", "var_ready", "rstd_ready", "norm_ready", "pool_step"):
                nc.sync.sem_clear(S[n])
            nc.all_engine_barrier()

            g_of = {(h, j): 3 * h + j for h in range(HG3) for j in range(3)}

            def A_free3(pe, n):
                if n >= 2:
                    if read_by(A3, n - 1, "A"):
                        pe.wait_ge(N["A_act"], read_by(A3, n - 1, "A"))
                    if read_by(A3, n - 1, "V"):
                        pe.wait_ge(N["A_dve"], read_by(A3, n - 1, "V"))

            with nc.Fori(0, H3 // HG3) as group:
                with nc.Block() as block:
                    @block.sync
                    def _(sp):
                        for w, name, t in zip(("wq", "wk", "wv"), ("wq", "wk", "wv"), wst):
                            sp.dma_start(t[:, :, :], a[names[name]][:, bass.ds(group * HG3 * P, HG3 * P)].rearrange("(k p) n -> p k n", p=P)
                                         ).then_inc(N[w + "_loaded"], 16)
                        sp.dma_start(v_row[:, :], a[names["bv"]][bass.ds(group * HG3 * P, HG3 * P)][None, :].broadcast_to([P, HG3 * P])
                                     ).then_inc(N["rows_loaded"], 16)
                        sp.dma_start(bias_v_row[:, :], a[names["bias_v"]].rearrange("a b h k -> (a b h k)")[bass.ds(group * HG3 * P, HG3 * P)]
                                     [None, :].broadcast_to([P, HG3 * P])).then_inc(N["rowb_loaded"], 16)
                        sp.dma_start(wo_st[:, :, :], a[names["wo"]][bass.ds(group * HG3 * P, HG3 * P), :].rearrange("(h p) n -> p h n", p=P)
                                     ).then_inc(N["wo_loaded"], 16)

                    @block.gpsimd
                    def _(pool):
                        nc.gpsimd.tensor_copy(vec[:, :, :], cols[:, :, bass.ds(group * HG3, HG3)]).then_inc(N["vec_ready"], 1)
                        pool.wait_ge(N["rows_loaded"], 16)
                        pool.wait_ge(N["rowb_loaded"], 16)
                        nc.gpsimd.tensor_tensor(v_row[:, :], v_row[:, :], bias_v_row[:, :], ALU.subtract).then_inc(N["v_row_ready"], 1)
                        pool.wait_ge(N["wo_loaded"], 16)
                        nc.gpsimd.tensor_scalar(wo3[:, 0], wo_st[:, :, :], 1.0, 1.0, ALU.mult, ALU.mult).then_inc(N["wo_high"], 1)
                        pool.wait_ge(N["wo_high"], 1)
                        nc.gpsimd.tensor_tensor(wo3[:, 1], wo_st[:, :, :], wo3[:, 0].bitcast(F32), ALU.subtract).then_inc(N["wo_low"], 1)
                        for what, h, j in ORDER:
                            if what == "S":
                                n = g_of[h, j]
                                nb = GROUPS3[j][1] - GROUPS3[j][0]
                                pool.wait_ge(N["r_ready"], n + 1)
                                e = E3[:, n % EXPS, 0:nb, 0:P]
                                nc.gpsimd.tensor_tensor(e, e, rs3[:, n % EXPS, 0:nb, None].broadcast_to([P, nb, P]),
                                                        ALU.mult).then_inc(N["P_ready"], 1)

                    @block.scalar
                    def _(act):
                        for n, w in enumerate(("wq", "wk", "wv")):
                            act.wait_ge(N[w + "_loaded"], 16)
                            nc.scalar.activation(w3[n][:, 0], wst[n][:, :, :], ACT.Copy).then_inc(N["w_high"], 1)
                        act.wait_ge(N["vec_ready"], 1)
                        for what, h, j in ORDER:
                            if what in ("q", "k"):
                                i = A3_at[what, h, j]
                                act.wait_ge(N["A_full"], i + 1)
                                if h >= 2:
                                    act.wait_ge(N["S_full"], 3 * (h - 1))
                                if what == "q":
                                    nc.scalar.activation(qT3[:, h % 2, 0, j * TOK:(j + 1) * TOK], Ab[i % 2][:, :], ACT.Identity,
                                                         bias=vec[:, 0, h:h + 1]).then_inc(N["A_act"], 1)
                                else:
                                    nc.scalar.activation(kT3[:, h % 2, 0, j * NB:(j + 1) * NB, 0:P],
                                                         Ab[i % 2][:, :].rearrange("p (b t) -> p b t", b=NB), ACT.Identity,
                                                         bias=vec[:, 1, h:h + 1]).then_inc(N["A_act"], 1)
                            elif what == "v":
                                act.wait_ge(N["A_dve"], read_by(A3, A3_at[what, h, j] + 1, "V"))
                                nc.scalar.activation(v3[:, 0, 2 * j:2 * j + 2], vf[:, j % 2], ACT.Copy).then_inc(N["v_high"], 1)
                            elif what == "S":
                                n = g_of[h, j]
                                act.wait_ge(N["nm_ready"], n + 1)
                                if n >= EXPS:
                                    act.wait_ge(N["T_full"], n - EXPS + 1)
                                    act.wait_ge(N["r_ready"], n - EXPS + 1)
                                for b in range(GROUPS3[j][1] - GROUPS3[j][0]):
                                    last = nc.scalar.activation(E3[:, n % EXPS, b, 0:P + 1], Sb[n % 2][:, b * T3:b * T3 + P + 1], ACT.Exp,
                                                                scale=SCALE3, bias=nm3[:, n % EXPS, b:b + 1],
                                                                accum_out=sum3[:, n % EXPS, b:b + 1])
                                last.then_inc(N["exp_done"], 1)
                            elif what == "T":
                                n = g_of[h, j]
                                w = (GROUPS3[j][1] - GROUPS3[j][0]) * P
                                act.wait_ge(N["T_full"], n + 1)
                                if n >= 2:
                                    act.wait_ge(N["pv_done"], n - 1)
                                nc.scalar.activation(PT3[:, n % 2, 0, 0:w], Tb[n % 2][:, 0:w], ACT.Copy).then_inc(N["T_act"], 1)
                            elif what == "PV" and j >= 1:
                                c = 2 * h + j - 1
                                act.wait_ge(N["pv_done"], 3 * h + j + 1)
                                nc.scalar.activation(ctxT3[:, 0, h, (j - 1) * TOK:j * TOK], Ob[c % 2][:, :], ACT.Identity,
                                                     bias=vec[:, 3, h:h + 1]).then_inc(N["ctx_high"], 1)

                    @block.vector
                    def _(dve):
                        for n in range(3):
                            dve.wait_ge(N["w_high"], n + 1)
                            nc.vector.tensor_tensor(w3[n][:, 1], wst[n][:, :, :], w3[n][:, 0].bitcast(F32), ALU.subtract).then_inc(N["w_low"], 1)
                        dve.wait_ge(N["vec_ready"], 1)
                        pending = []

                        def settle():
                            for n, nb in pending:
                                dve.wait_ge(N["exp_done"], n + 1)
                                if n >= EXPS:
                                    dve.wait_ge(N["P_ready"], n - EXPS + 1)
                                nc.vector.reciprocal(rs3[:, n % EXPS, 0:nb], sum3[:, n % EXPS, 0:nb]).then_inc(N["r_ready"], 1)
                            pending.clear()

                        for what, h, j in ORDER:
                            if what not in ("q", "k") or len(pending) > 1:
                                settle()
                            if what in ("q", "k"):
                                i = A3_at[what, h, j]
                                dve.wait_ge(N["A_act"], read_by(A3, i + 1, "A"))
                                if what == "q":
                                    nc.vector.scalar_tensor_tensor(
                                        out=qT3[:, h % 2, 1, j * TOK:(j + 1) * TOK], in0=Ab[i % 2][:, :], scalar=vec[:, 0, h:h + 1],
                                        in1=qT3[:, h % 2, 0, j * TOK:(j + 1) * TOK].bitcast(F32), op0=ALU.add,
                                        op1=ALU.subtract).then_inc(N["A_dve"], 1)
                                else:
                                    nc.vector.scalar_tensor_tensor(
                                        out=kT3[:, h % 2, 1, j * NB:(j + 1) * NB, 0:P],
                                        in0=Ab[i % 2][:, :].rearrange("p (b t) -> p b t", b=NB), scalar=vec[:, 1, h:h + 1],
                                        in1=kT3[:, h % 2, 0, j * NB:(j + 1) * NB, 0:P].bitcast(F32), op0=ALU.add,
                                        op1=ALU.subtract).then_inc(N["A_dve"], 1)
                                    if j == 1:
                                        key = vec[:, 2, h:h + 1].broadcast_to([P, B])
                                        nc.vector.tensor_copy(kT3[:, h % 2, 0, :, P], key).then_inc(N["bias_high"], 1)
                                        dve.wait_ge(N["bias_high"], h + 1)
                                        nc.vector.tensor_tensor(kT3[:, h % 2, 1, :, P], key, kT3[:, h % 2, 0, :, P].bitcast(F32),
                                                                ALU.subtract).then_inc(N["bias_low"], 1)
                            elif what == "v":
                                i = A3_at[what, h, j]
                                dve.wait_ge(N["A_full"], i + 1)
                                if j == 0:
                                    dve.wait_ge(N["v_row_ready"], 1)
                                if j >= 2:
                                    dve.wait_ge(N["v_high"], j - 1)
                                    dve.wait_ge(N["v_low"], j - 1)
                                nc.vector.tensor_tensor(vf[:, j % 2], Ab[i % 2][:, :].rearrange("p (b n) -> p b n", b=2),
                                                        v_row[:, None, :].broadcast_to([P, 2, HG3 * P]), ALU.add).then_inc(N["A_dve"], 1)
                                dve.wait_ge(N["v_high"], j + 1)
                                nc.vector.tensor_tensor(v3[:, 1, 2 * j:2 * j + 2], vf[:, j % 2], v3[:, 0, 2 * j:2 * j + 2].bitcast(F32),
                                                        ALU.subtract).then_inc(N["v_low"], 1)
                            elif what == "S":
                                n = g_of[h, j]
                                nb = GROUPS3[j][1] - GROUPS3[j][0]
                                dve.wait_ge(N["S_full"], n + 1)
                                bank = Sb[n % 2][:, 0:nb * T3].rearrange("p (b t) -> p b t", b=nb)[:, :, 0:P + 1]
                                nc.vector.tensor_reduce(mx3[:, n % EXPS, 0:nb], bank, AX_X, ALU.max).then_inc(N["max_ready"], 1)
                                dve.wait_ge(N["max_ready"], n + 1)
                                nc.vector.tensor_scalar(nm3[:, n % EXPS, 0:nb], mx3[:, n % EXPS, 0:nb], -SCALE3, None,
                                                        ALU.mult).then_inc(N["nm_ready"], 1)
                                pending.append((n, nb))
                            elif what == "T":
                                n = g_of[h, j]
                                w = (GROUPS3[j][1] - GROUPS3[j][0]) * P
                                dve.wait_ge(N["T_act"], n + 1)
                                nc.vector.tensor_tensor(PT3[:, n % 2, 1, 0:w], Tb[n % 2][:, 0:w], PT3[:, n % 2, 0, 0:w].bitcast(F32),
                                                        ALU.subtract).then_inc(N["T_dve"], 1)
                            elif what == "PV" and j >= 1:
                                c = 2 * h + j - 1
                                dve.wait_ge(N["ctx_high"], c + 1)
                                nc.vector.scalar_tensor_tensor(
                                    out=ctxT3[:, 1, h, (j - 1) * TOK:j * TOK], in0=Ob[c % 2][:, :], scalar=vec[:, 3, h:h + 1],
                                    in1=ctxT3[:, 0, h, (j - 1) * TOK:j * TOK].bitcast(F32), op0=ALU.add,
                                    op1=ALU.subtract).then_inc(N["ctx_low"], 1)
                            elif what == "out":
                                i = A3_at[what, h, j]
                                dve.wait_ge(N["A_full"], i + 1)
                                nc.vector.tensor_tensor(x_all[:, 2 * j:2 * j + 2], Ab[i % 2][:, :].rearrange("p (b d) -> p b d", b=2),
                                                        x_all[:, 2 * j:2 * j + 2], ALU.add).then_inc(N["A_dve"], 1)

                    @block.tensor
                    def _(pe):
                        for what, h, j in ORDER:
                            if what in ("q", "k"):
                                i = A3_at[what, h, j]
                                w = 0 if what == "q" else 1
                                if h == 0 and j == 0:
                                    pe.wait_ge(N["w_low"], w + 1)
                                A_free3(pe, i)
                                src = hT3 if what == "q" else cT3
                                for kt in range(KT):
                                    last = products(pe, Ab[i % 2][:, :], pair(w3[w], kt, slice(h * P, (h + 1) * P)),
                                                    pair(src, kt, slice(j * TOK, (j + 1) * TOK)), kt == 0, kt == KT - 1)
                                last.then_inc(N["A_full"], 1)
                            elif what == "v":
                                i = A3_at[what, h, j]
                                if j == 0:
                                    pe.wait_ge(N["w_low"], 3)
                                A_free3(pe, i)
                                for e in range(2):
                                    b = 2 * j + e
                                    for kt in range(KT):
                                        last = products(pe, Ab[i % 2][:, e * HG3 * P:(e + 1) * HG3 * P],
                                                        pair(cT3, kt, slice(b * P, (b + 1) * P)), pair(w3[2], kt), kt == 0, kt == KT - 1)
                                last.then_inc(N["A_full"], 1)
                            elif what == "S":
                                n = g_of[h, j]
                                if n >= 2:
                                    pe.wait_ge(N["exp_done"], n - 1)
                                if j == 0:
                                    done = read_by(A3, A3_at["k", h, 1] + 1, "A")
                                    pe.wait_ge(N["A_act"], done)
                                    pe.wait_ge(N["A_dve"], read_by(A3, A3_at["k", h, 1] + 1, "V"))
                                    pe.wait_ge(N["bias_low"], h + 1)
                                for b in range(*GROUPS3[j]):
                                    e = b - GROUPS3[j][0]
                                    last = products(pe, Sb[n % 2][:, e * T3:(e + 1) * T3],
                                                    (qT3[:, h % 2, 0, b * P:(b + 1) * P], qT3[:, h % 2, 1, b * P:(b + 1) * P]),
                                                    (kT3[:, h % 2, 0, b], kT3[:, h % 2, 1, b]), True, True)
                                last.then_inc(N["S_full"], 1)
                            elif what == "T":
                                n = g_of[h, j]
                                if n >= 2:
                                    pe.wait_ge(N["T_act"], n - 1)
                                    pe.wait_ge(N["T_dve"], n - 1)
                                pe.wait_ge(N["P_ready"], n + 1)
                                for e in range(GROUPS3[j][1] - GROUPS3[j][0]):
                                    last = nc.tensor.transpose(Tb[n % 2][:, e * P:(e + 1) * P], E3[:, n % EXPS, e, 0:P], ident[:, :])
                                last.then_inc(N["T_full"], 1)
                            elif what == "PV":
                                n = g_of[h, j]
                                pe.wait_ge(N["T_dve"], n + 1)
                                if n == 0:
                                    pe.wait_ge(N["v_low"], NB)
                                c = 2 * h if j == 0 else 2 * h + 1
                                if j < 2 and c >= 2:
                                    pe.wait_ge(N["ctx_high"], c - 1)
                                    pe.wait_ge(N["ctx_low"], c - 1)
                                for b in range(*GROUPS3[j]):
                                    e = b - GROUPS3[j][0]
                                    last = products(pe, Ob[b // NB][:, (b % NB) * P:(b % NB + 1) * P],
                                                    (v3[:, 0, b, h * P:(h + 1) * P], v3[:, 1, b, h * P:(h + 1) * P]),
                                                    (PT3[:, n % 2, 0, e * P:(e + 1) * P], PT3[:, n % 2, 1, e * P:(e + 1) * P]), True, True)
                                last.then_inc(N["pv_done"], 1)
                            elif what == "out":
                                i = A3_at[what, h, j]
                                if j == 0:
                                    pe.wait_ge(N["wo_low"], 1)
                                pe.wait_ge(N["ctx_high"], 2 * HG3 - 1 + j // 2)
                                pe.wait_ge(N["ctx_low"], 2 * HG3 - 1 + j // 2)
                                A_free3(pe, i)
                                for e in range(2):
                                    b = 2 * j + e
                                    for hh in range(HG3):
                                        last = products(pe, Ab[i % 2][:, e * D:(e + 1) * D], pair(ctxT3, hh, slice(b * P, (b + 1) * P)),
                                                        pair(wo3, hh), hh == 0, hh == HG3 - 1)
                                last.then_inc(N["A_full"], 1)

                for each in N.values():
                    nc.sync.sem_clear(each)
                nc.all_engine_barrier()

        rows_in = ctx.enter_context(nc.semaphore("rows_in"))
        with nc.Block() as block:
            @block.scalar
            def _(act):
                for i, name in enumerate(ROWS3):
                    act.dma_start(rows[:, i, :], a[name][None, :].broadcast_to([P, D])).then_inc(rows_in, 16)
                act.wait_ge(rows_in, 16 * len(ROWS3))

            @block.gpsimd
            def _(pool):
                nc.gpsimd.memset(kT3[:, :, :, :, P + 1:T3].bitcast(F32), 0.0)
        attention3(0)
        attention3(1)

        s4 = ExitStack()
        xh, z, aT, g, gT, fcw, pjw = mlp_memory(s4, "_last")
        fc_st = sb("fc_st", [P, KT, INNER], F32, s4)
        pj_st = sb("pj_st", [P, MT, D], F32, s4)
        s4.close()
        sem = lambda n: ctx.enter_context(nc.semaphore(n))
        fc_in, pj_in, split3 = sem("fc_in"), sem("pj_in"), sem("split3")
        with nc.Block() as block:
            @block.sync
            def _(sp):
                sp.dma_start(fc_st[:, :, :], a["L3_xattn_w_fc1"].rearrange("(k p) n -> p k n", p=P)).then_inc(fc_in, 16)
                sp.dma_start(pj_st[:, :, :], a["L3_xattn_w_fc2"].rearrange("(m p) n -> p m n", p=P)).then_inc(pj_in, 16)

            @block.scalar
            def _(act):
                act.wait_ge(fc_in, 16)
                nc.scalar.activation(fcw[:, 0], fc_st[:, :, :], ACT.Copy).then_inc(split3, 1)
                act.wait_ge(pj_in, 16)
                nc.scalar.activation(pjw[:, 0], pj_st[:, :, :], ACT.Copy).then_inc(split3, 1)

            @block.vector
            def _(dve):
                for n, (s, d) in enumerate(((fc_st, fcw), (pj_st, pjw))):
                    dve.wait_ge(split3, n + 1)
                    nc.vector.tensor_tensor(d[:, 1], s[:, :, :], d[:, 0].bitcast(F32), ALU.subtract)
        S["x_copied"], S["stored"] = sem("x_copied"), sem("stored")
        used = [S[n] for n in ("T_full", "T_act", "T_dve", "A_full", "A_act", "A_dve", "O_read", "g_high", "g_low", "g_used", "vstep",
                               "var_ready", "rstd_ready", "norm_ready", "pool_step", "x_biased", "x_copied", "stored")]
        with nc.Fori(0, HALVES) as half:
            with nc.Block() as block:
                @block.vector
                def _(dve):
                    steps[0] = norms[0] = 0
                    nc.vector.tensor_copy(xh[:, :, :], x_all[:, bass.ds(half * NB, NB), :]).then_inc(S["x_copied"], 1)
                    dve.wait_ge(S["x_copied"], 1)
                    norm(dve, lambda b: xh[:, b], z, NB, row("L3_xattn_ln_mlp_scale"))
                    for b in range(NB):
                        nc.vector.scalar_tensor_tensor(out=z[:, b], in0=z[:, b], scalar=rstd[:, b:b + 1], in1=row("L3_xattn_ln_mlp_offset"),
                                                       op0=ALU.mult, op1=ALU.add).then_inc(S["norm_ready"], 1)
                    split_low(dve, aT, 0)
                    mlp_dve(dve)
                    dve.wait_ge(S["x_biased"], 1)
                    mlp_add(dve, 0)

                @block.gpsimd
                def _(pool):
                    psteps[0] = 0
                    power(pool, 1, NB, LN_EPS)
                    pool.wait_ge(S["norm_ready"], NB)
                    nc.gpsimd.tensor_tensor(xh[:, :, :], xh[:, :, :], row("L3_xattn_b_fc2")[:, None, :].broadcast_to([P, NB, D]),
                                            ALU.add).then_inc(S["x_biased"], 1)

                @block.scalar
                def _(act):
                    split_high(act, aT, 0)
                    mlp_act(act, MLP_A, 0, ACT.Gelu, "L3_xattn_b_fc1")

                @block.tensor
                def _(pe):
                    pe.wait_ge(S["norm_ready"], NB)
                    turn(pe, z, MLP_T, 0)
                    pe.wait_ge(S["T_act"], KT)
                    pe.wait_ge(S["T_dve"], KT)
                    mlp_pe(pe, MLP_A, 0, 0)

                @block.sync
                def _(sp):
                    sp.wait_ge(S["O_read"], 2)
                    sp.dma_start(out[bass.ds(half * NB, NB)].rearrange("b t d -> t b d"), xh[:, :, :]).then_inc(S["stored"], 16)
                    sp.wait_ge(S["stored"], 16)
            for each in used:
                nc.sync.sem_clear(each)
            nc.all_engine_barrier()


_OUTS = [((B, P, D), "float32")]


def kernel(**inputs):
    import numpy as _np
    import concourse.bacc as _bacc
    from concourse import mybir as _mybir
    from concourse.bass_utils import run_bass_kernel_spmd as _run

    nc = _bacc.Bacc("TRN2", target_bir_lowering=False, num_devices=1)
    arrays, args = {}, {}
    for name, value in inputs.items():
        v = _np.ascontiguousarray(value).reshape(_np.shape(value) or (1,))
        arrays[f"in_{name}_dram"] = v
        args[name] = nc.dram_tensor(f"in_{name}_dram", v.shape, _mybir.dt.from_np(v.dtype), kind="ExternalInput").ap()
    out = nc.dram_tensor("out_0_dram", _OUTS[0][0], F32, kind="ExternalOutput").ap()
    network(nc, args, out)
    r = _run(nc, [arrays], core_ids=[0])
    return r.results[0]["out_0_dram"]
```

```python
import concourse.bass as bass
from concourse import mybir
from contextlib import ExitStack

F32 = mybir.dt.float32
R32 = mybir.dt.float32r
U8 = mybir.dt.uint8
ALU = mybir.AluOpType
ACT = mybir.ActivationFunctionType
AX_X = mybir.AxisListType.X

P = 128
D = 256
KT = D // P
NB = 4
HALVES = 2
B = NB * HALVES
TOK = NB * P
INNER = 4 * D
MT = INNER // P
LN_EPS, LN2_EPS = 1e-5, 1e-6
BIG = 2.0 ** 127
EXPS = 3
VW = 32
TWO_BANKS = 2

H3 = 16
HG3 = 2
T3 = P + 2
GROUPS3 = [(0, 3), (3, 6), (6, 8)]

STACK_A = [("L1_xattn_q_b", 2), ("L1_xattn_k_b", 2), ("L1_xattn_fc_b", 8), ("L2_xattn_bq", 2),
           ("L2_xattn_bk", 2), ("L3_xattn_b_fc1", 8),
           ("L3_xattn_bq1", H3), ("L3_xattn_bk1", H3), ("L3_xattn_bias_k1", H3), ("L3_xattn_bias_v1", H3)]
STACK_B = [("L3_xattn_bq2", H3), ("L3_xattn_bk2", H3), ("L3_xattn_bias_k2", H3), ("L3_xattn_bias_v2", H3)]
ROWS = ["L1_xattn_ln1_w", "L1_xattn_ln1_b", "L1_xattn_v_b", "L1_xattn_cproj_b", "L1_xattn_ln2_w",
        "L1_xattn_ln2_b", "L1_xattn_proj_b", "L2_xattn_bo", "L2_xattn_gamma", "L2_xattn_beta"]
ROWS3 = ["L3_xattn_ln1_scale", "L3_xattn_ln1_offset", "L3_xattn_bo1",
        "L3_xattn_ln2_scale", "L3_xattn_ln2_offset", "L3_xattn_bo2",
        "L3_xattn_ln_mlp_scale", "L3_xattn_ln_mlp_offset", "L3_xattn_b_fc2"]


def place(stack):
    at, n = {}, 0
    for name, rows in stack:
        at[name] = n
        n += rows
    return at, n


T_FILLS = ([("c", 1)] * KT + [("x", 1)] * KT + [("p0", 0)] + [("z1", 1)] * KT + [("p1", 0)] * 16
           + [("ctx1", 1)] * KT + [("z2", 1)] * KT + [("x2", 1)] * KT + [("p2", 0)] * 32 + [("ctx2", 1)] * KT)
A_FILLS = ([("q0", "AV")] * 2 + [("v0", "V")] * 2 + [("k1", "AV")] * 2 + [("v1", "V")] * 2
           + [("q1", "AV")] * 2 + [("ctx1", "V")] * 4 + [("o1", "V")] * 2 + [("k2", "AV")] * 2 + [("v2", "V")]
           + [("fc", "A")] * MT + [("q2", "AV")] * 2 + [("ctx2", "V")] * 8 + [("o2", "V")] * 2)
O_FILLS = ["pv0"] * NB + ["pv1"] * 4 + ["mlp"] * 2 + ["pv2"] * 8
S_FILLS = ["s0"] + ["s1"] * 16 + ["s2"] * 32
MLP_T, MLP_A = [("z", 1)] * KT, [("fc", "A")] * MT


def first(fills, what):
    return [f[0] if isinstance(f, tuple) else f for f in fills].index(what)


def splits_in(fills, n):
    return sum(f[1] for f in fills[:n])


def read_by(fills, n, engine):
    return sum(engine in f[1] for f in fills[:n])


def products(pe, out, left, right, begin, end):
    (lh, ll), (rh, rl) = left, right
    pe.matmul(out, lh, rh, start=begin, stop=False)
    pe.matmul(out, ll, rh, start=False, stop=False)
    return pe.matmul(out, lh, rl, start=False, stop=end)


def network(nc, a, out):
    ctx = ExitStack()
    with ctx:
        def sb(name, shape, dt=F32, where=ctx):
            return where.enter_context(nc.sbuf_tensor(name, shape, dt))

        banks = [ctx.enter_context(nc.psum_tensor(f"bank{i}", [P, 512], F32)) for i in range(8)]
        Sb, Tb, Ab, Ob = banks[0:2], banks[2:4], banks[4:6], banks[6:8]

        atA, nA = place(STACK_A)
        atB, nB = place(STACK_B)
        x_all = sb("x_all", [P, B, D])
        ident = sb("ident", [P, P])
        colsA = sb("colsA", [P, nA])
        colsB = sb("colsB", [P, nB])
        rows = sb("rows", [P, len(ROWS), D])
        stats = sb("stats", [P, B, 6])
        mv = sb("mv", [P, B, 2])
        rstd = sb("rstd", [P, B])
        var = sb("var", [P, B])
        neg_half = sb("neg_half", [P, B])

        def mlp_memory(where, tag):
            return (sb("xh" + tag, [P, NB, D], F32, where), sb("z" + tag, [P, NB, D], F32, where),
                    sb("aT" + tag, [P, 2, KT, TOK], R32, where), sb("g" + tag, [P, 2, TOK], F32, where),
                    sb("gT" + tag, [P, 2, 2, TOK], R32, where))

        def row(name):
            return rows[:, (ROWS if name in ROWS else ROWS3).index(name), :]

        def col(name, i):
            return colsA[:, atA[name] + i:atA[name] + i + 1]

        def pair(t, *idx):
            return t[(slice(None), 0) + idx], t[(slice(None), 1) + idx]

        fcw = sb("fcw", [P, 2, KT, INNER], R32)
        pjw = sb("pjw", [P, 2, MT, D], R32)

        s1 = ExitStack()
        xh, z, aT, g, gT = mlp_memory(s1, "_half")
        m0w = sb("m0w", [P, 2, KT, D], R32, s1)
        v0w = sb("v0w", [P, 2, KT, D], R32, s1)
        w1 = [sb(f"w1_{n}", [P, 2, KT, D], R32, s1) for n in "qkvo"]
        w2 = [sb(f"w2_{n}", [P, 2, KT, D], R32, s1) for n in "qko"]
        w2v = sb("w2v", [P, 2, KT, 64], R32, s1)
        hmask1 = sb("hmask1", [P, 8], F32, s1)
        hmask2 = sb("hmask2", [P, 16], F32, s1)
        bv2 = sb("bv2", [P, 64], F32, s1)
        alpha = sb("alpha", [P, 1], F32, s1)
        v0 = sb("v0", [P, NB, D + 1], F32, s1)
        v1 = sb("v1", [P, NB, 16, VW], F32, s1)
        v2 = sb("v2", [P, NB, 8, VW], F32, s1)

        s0 = ExitStack()
        stage = [sb(f"stage{i}", [P, KT, D], F32, s0) for i in range(4)]
        stage1 = [sb(f"stage1_{i}", [P, KT, D], F32, s0) for i in range(7)]
        stage_v = sb("stage_v", [P, KT, 64], F32, s0)
        w0 = [sb(f"w0_{n}", [P, 2, KT, D], R32, s0) for n in "qkvo"]
        stackA = sb("stackA", [P, P], F32, s0)
        stackB = sb("stackB", [P, P], F32, s0)
        stage_fc = sb("stage_fc", [P, KT, INNER], F32, s0)
        stage_pj = sb("stage_pj", [P, MT, D], F32, s0)
        s0.close()

        names0 = ["L0_xattn_w_q", "L0_xattn_w_k", "L0_xattn_w_v", "L0_xattn_w_o"]
        names1 = ["L1_xattn_q_w", "L1_xattn_k_w", "L1_xattn_v_w", "L1_xattn_cproj_w",
                  "L2_xattn_Wq", None, "L2_xattn_Wo"]

        sem = lambda n: ctx.enter_context(nc.semaphore(n))
        loaded = [sem(f"w0_loaded{i}") for i in range(4)]
        loaded1 = [sem(f"w1_loaded{i}") for i in range(7)]
        wk2_loaded, wv2_loaded = sem("wk2_loaded"), sem("wv2_loaded")
        fc_loaded, pj_loaded = sem("fc_loaded"), sem("pj_loaded")
        stacked, rows_loaded = sem("stacked"), sem("rows_loaded")
        consts, dve_step, act_step = sem("consts"), sem("dve_step"), sem("act_step")
        high0, low0 = sem("high0"), sem("low0")
        wo_turned, wo_high, wo_low = sem("wo_turned"), sem("wo_high"), sem("wo_low")
        m_full, m_high = sem("m_full"), sem("m_high")
        cols_turned = sem("cols_turned")
        scaled2, high1 = sem("scaled2"), sem("high1")
        cleared = sem("cleared")
        with nc.Block() as block:
            @block.sync
            def _(sp):
                for n in range(4):
                    sp.dma_start(stage[n][:, :, :], a[names0[n]].rearrange("(k p) n -> p k n", p=P)).then_inc(loaded[n], 16)
                for n in range(7):
                    if n == 5:
                        for k in range(KT):
                            for q in range(4):
                                sp.dma_start(stage1[5][:, k, :].rearrange("p (h g d) -> p h g d", h=8, g=4)[:, :, q, :],
                                             a["L2_xattn_Wk"][k * P:(k + 1) * P, :].rearrange("p (h d) -> p h d", d=8)
                                             ).then_inc(wk2_loaded, 16)
                        continue
                    sp.dma_start(stage1[n][:, :, :], a[names1[n]].rearrange("(k p) n -> p k n", p=P)).then_inc(loaded1[n], 16)
                sp.dma_start(stage_v[:, :, :], a["L2_xattn_Wv"].rearrange("(k p) n -> p k n", p=P)).then_inc(wv2_loaded, 16)
                sp.dma_start(stage_fc[:, :, :], a["L1_xattn_fc_w"].rearrange("(k p) n -> p k n", p=P)).then_inc(fc_loaded, 16)
                sp.dma_start(stage_pj[:, :, :], a["L1_xattn_proj_w"].rearrange("(m p) n -> p m n", p=P)).then_inc(pj_loaded, 16)
                sp.wait_ge(rows_loaded, 16 * (len(ROWS) + 2))

            @block.scalar
            def _(act):
                for stack, at, tile in ((STACK_A, atA, stackA), (STACK_B, atB, stackB)):
                    for name, n in stack:
                        if name == "L2_xattn_bk":
                            src = a[name].rearrange("(r h d) -> r h d", r=2, d=8)
                            for q in range(4):
                                act.dma_start(tile[at[name]:at[name] + 2, :].rearrange("r (h g d) -> r h g d", g=4, d=8)[:, :, q, :],
                                              src).then_inc(stacked, 16)
                        else:
                            v = a[name]
                            if len(v.shape) == 4:
                                v = v.rearrange("a b h k -> (a b h k)")
                            act.dma_start(tile[at[name]:at[name] + n, :], v.rearrange("(r p) -> r p", p=P)).then_inc(stacked, 16)
                for i, name in enumerate(ROWS):
                    act.dma_start(rows[:, i, :], a[name][None, :].broadcast_to([P, D])).then_inc(rows_loaded, 16)
                act.dma_start(bv2[:, :], a["L2_xattn_bv"][None, :].broadcast_to([P, 64])).then_inc(rows_loaded, 16)
                act.dma_start(alpha[:, :], a["L0_xattn_alpha"][None, :].broadcast_to([P, 1])).then_inc(rows_loaded, 16)
                for n in range(3):
                    act.wait_ge(loaded[n], 16)
                    nc.scalar.activation(w0[n][:, 0], stage[n][:, :, :], ACT.Copy).then_inc(high0, 1)
                act.wait_ge(wo_turned, 1)
                nc.scalar.activation(w0[3][:, 0], Ab[0][:, :].rearrange("p (k n) -> p k n", k=KT), ACT.Copy).then_inc(wo_high, 1)
                for n, (full, dst) in enumerate(((Sb[0], m0w), (Sb[1], v0w))):
                    act.wait_ge(m_full, n + 1)
                    nc.scalar.activation(dst[:, 0], full[:, :].rearrange("p (k n) -> p k n", k=KT), ACT.Copy).then_inc(m_high, 1)
                for n in range(7):
                    if n == 5:
                        act.wait_ge(wk2_loaded, 16 * 4 * KT)
                    else:
                        act.wait_ge(loaded1[n], 16)
                    if n == 4:
                        act.wait_ge(scaled2, 1)
                    nc.scalar.activation((w1 + w2)[n][:, 0], stage1[n][:, :, :], ACT.Copy).then_inc(high1, 1)
                act.wait_ge(wv2_loaded, 16)
                nc.scalar.activation(w2v[:, 0], stage_v[:, :, :], ACT.Copy).then_inc(high1, 1)
                act.wait_ge(fc_loaded, 16)
                nc.scalar.activation(fcw[:, 0], stage_fc[:, :, :], ACT.Copy).then_inc(high1, 1)
                act.wait_ge(pj_loaded, 16)
                nc.scalar.activation(pjw[:, 0], stage_pj[:, :, :], ACT.Copy).then_inc(high1, 1)

            @block.gpsimd
            def _(pool):
                nc.gpsimd.memset(ident[:, :], 0.0).then_inc(cleared, 1)
                nc.gpsimd.memset(neg_half[:, :], -0.5)
                pool.wait_ge(cleared, 1)
                nc.gpsimd.affine_select(out=ident[:, :], in_=ident[:, :], compare_op=ALU.not_equal, fill=1.0,
                                        base=0, pattern=[[-1, P]], channel_multiplier=1).then_inc(consts, 1)
                nc.gpsimd.memset(v0[:, :, D:D + 1], 1.0)
                nc.gpsimd.memset(v1[:, :, :, 16:17], 1.0)
                nc.gpsimd.memset(v1[:, :, :, 17:VW], 0.0)
                nc.gpsimd.memset(v2[:, :, :, 8:9], 1.0)
                nc.gpsimd.memset(v2[:, :, :, 9:VW], 0.0)

            @block.vector
            def _(dve):
                dve.wait_ge(consts, 1)
                nc.vector.tensor_reduce(hmask1[:, :], ident[:, :].rearrange("p (h d) -> p h d", d=16), AX_X, ALU.add)
                nc.vector.tensor_reduce(hmask2[:, :], ident[:, :].rearrange("p (h d) -> p h d", d=8), AX_X, ALU.add)
                for n in range(3):
                    dve.wait_ge(high0, n + 1)
                    nc.vector.tensor_tensor(w0[n][:, 1], stage[n][:, :, :], w0[n][:, 0].bitcast(F32), ALU.subtract).then_inc(low0, 1)
                dve.wait_ge(wo_high, 1)
                nc.vector.tensor_tensor(w0[3][:, 1], Ab[0][:, :].rearrange("p (k n) -> p k n", k=KT),
                                        w0[3][:, 0].bitcast(F32), ALU.subtract).then_inc(wo_low, 1)
                for n, (full, dst) in enumerate(((Sb[0], m0w), (Sb[1], v0w))):
                    dve.wait_ge(m_high, n + 1)
                    nc.vector.tensor_tensor(dst[:, 1], full[:, :].rearrange("p (k n) -> p k n", k=KT),
                                            dst[:, 0].bitcast(F32), ALU.subtract)
                dve.wait_ge(cols_turned, 1)
                nc.vector.tensor_copy(colsA[:, :], Tb[0][:, 0:nA]).then_inc(dve_step, 1)
                dve.wait_ge(cols_turned, 2)
                nc.vector.tensor_copy(colsB[:, :], Tb[1][:, 0:nB])
                dve.wait_ge(dve_step, 1)
                nc.vector.tensor_scalar(colsA[:, atA["L2_xattn_bq"]:atA["L2_xattn_bq"] + 2],
                                        colsA[:, atA["L2_xattn_bq"]:atA["L2_xattn_bq"] + 2], 8 ** -0.5, None, ALU.mult)
                dve.wait_ge(loaded1[4], 16)
                nc.vector.tensor_scalar(stage1[4][:, :, :], stage1[4][:, :, :], 8 ** -0.5, None, ALU.mult).then_inc(scaled2, 1)
                dsts = [t for t in w1 + w2] + [w2v, fcw, pjw]
                srcs = stage1 + [stage_v, stage_fc, stage_pj]
                for n, (s, d) in enumerate(zip(srcs, dsts)):
                    dve.wait_ge(high1, n + 1)
                    nc.vector.tensor_tensor(d[:, 1], s[:, :, :], d[:, 0].bitcast(F32), ALU.subtract)

            @block.tensor
            def _(pe):
                pe.wait_ge(consts, 1)
                pe.wait_ge(loaded[3], 16)
                for kt in range(KT):
                    for mt in range(KT):
                        last = nc.tensor.transpose(Ab[0][:, kt * D + mt * P:kt * D + (mt + 1) * P],
                                                   stage[3][:, mt, kt * P:(kt + 1) * P], ident[:, :])
                last.then_inc(wo_turned, 1)
                pe.wait_ge(high0, 3)
                pe.wait_ge(low0, 3)
                for mt in range(KT):
                    for kt in range(KT):
                        last = products(pe, Sb[0][:, mt * D:(mt + 1) * D], pair(w0[0], kt, slice(mt * P, (mt + 1) * P)),
                                        pair(w0[1], kt), kt == 0, kt == KT - 1)
                last.then_inc(m_full, 1)
                pe.wait_ge(wo_high, 1)
                pe.wait_ge(wo_low, 1)
                for mt in range(KT):
                    for kt in range(KT):
                        last = products(pe, Sb[1][:, mt * D:(mt + 1) * D], pair(w0[2], kt, slice(mt * P, (mt + 1) * P)),
                                        pair(w0[3], kt), kt == 0, kt == KT - 1)
                last.then_inc(m_full, 1)
                pe.wait_ge(stacked, 16 * (len(STACK_A) + 3 + len(STACK_B)))
                nc.tensor.transpose(Tb[0][:, 0:nA], stackA[0:nA, :], ident[0:nA, 0:nA]).then_inc(cols_turned, 1)
                nc.tensor.transpose(Tb[1][:, 0:nB], stackB[0:nB, :], ident[0:nB, 0:nB]).then_inc(cols_turned, 1)

        cT = sb("cT", [P, 2, KT, TOK], R32, s1)
        qT = sb("qT", [P, 2, KT, TOK], R32, s1)
        kT = sb("kT", [P, 2, KT, TOK], R32, s1)
        km = sb("km", [P, 2, 2, 4, TOK], R32, s1)
        E = sb("E", [P, EXPS, 4, P], F32, s1)
        PT = sb("PT", [P, 2, 4, P], F32, s1)
        o = sb("o", [P, NB, D], F32, s1)
        mask1b = sb("mask1b", [P, NB, P], U8, s1)
        masks = {1: sb("mask1", [P, NB, P], F32, s1), 2: sb("mask2", [P, NB, P], F32, s1)}
        nm = sb("nm", [P, EXPS, 4], F32, s1)
        mx = sb("mx", [P, EXPS, 4], F32, s1)
        r0 = sb("r0", [P, NB], F32, s1)
        r1 = sb("r1", [P, NB, 4], F32, s1)
        sums = g
        s1.close()

        sem = lambda n: ctx.enter_context(nc.semaphore(n))
        S = {n: sem(n) for n in (
            "c_loaded", "x_loaded", "mask1_loaded", "mask2_loaded", "T_full", "A_full", "S_full", "O_full",
            "T_act", "T_dve", "A_act", "A_dve", "S_read", "nm_ready", "O_read", "P_ready", "pv_done",
            "km_high", "km_low", "norm_ready", "var_ready", "rstd_ready", "x_biased", "g_high",
            "g_low", "g_used", "mask1_ready", "vstep", "x_out")}

        LAYERS = {1: dict(hd=16, hg=4, scale=0.25, v=v1, mask=masks[1], hmask=hmask1, kbias="L1_xattn_k_b"),
                  2: dict(hd=8, hg=8, scale=1.0, v=v2, mask=masks[2], hmask=hmask2, kbias="L2_xattn_bk")}
        for n, L in LAYERS.items():
            L["S"], L["T"], L["O"] = first(S_FILLS, f"s{n}"), first(T_FILLS, f"p{n}"), first(O_FILLS, f"pv{n}")
            L["km"] = 0 if n == 1 else 4
            L["G"] = L["hg"] * NB
            L["ctx"] = first(A_FILLS, f"ctx{n}")
            L["kfill"] = first(A_FILLS, f"k{n}")
            L["heads_kt"] = P // L["hd"]

        def T_free(pe, fills, n):
            if n >= 2:
                pe.wait_ge(S["T_act"], n - 1)
                if splits_in(fills, n - 1):
                    pe.wait_ge(S["T_dve"], splits_in(fills, n - 1))

        def A_free(pe, fills, n):
            if n >= 2:
                for s, e in (("A_act", "A"), ("A_dve", "V")):
                    if read_by(fills, n - 1, e):
                        pe.wait_ge(S[s], read_by(fills, n - 1, e))

        def turn(pe, src, fills, n):
            for kt in range(KT):
                T_free(pe, fills, n + kt)
                for b in range(NB):
                    last = nc.tensor.transpose(Tb[(n + kt) % 2][:, b * P:(b + 1) * P],
                                               src[:, b, kt * P:(kt + 1) * P], ident[:, :])
                last.then_inc(S["T_full"], 1)

        def split_high(act, dst, n):
            for kt in range(KT):
                act.wait_ge(S["T_full"], n + kt + 1)
                nc.scalar.activation(dst[:, 0, kt, :], Tb[(n + kt) % 2][:, :], ACT.Copy).then_inc(S["T_act"], 1)

        def split_low(dve, dst, n):
            for kt in range(KT):
                dve.wait_ge(S["T_act"], n + kt + 1)
                nc.vector.tensor_tensor(dst[:, 1, kt, :], Tb[(n + kt) % 2][:, :], dst[:, 0, kt, :].bitcast(F32),
                                        ALU.subtract).then_inc(S["T_dve"], 1)

        def a_free(eng, what, fills):
            eng.wait_ge(S["A_full"], fA[what] + fills)

        def project_T(pe, w, src, fills, n):
            for mt in range(KT):
                A_free(pe, fills, n + mt)
                for kt in range(KT):
                    last = products(pe, Ab[(n + mt) % 2][:, :], pair(w, kt, slice(mt * P, (mt + 1) * P)), pair(src, kt),
                                    kt == 0, kt == KT - 1)
                last.then_inc(S["A_full"], 1)
            return last

        def project(pe, w, width, src, fills, n):
            per = 512 // width if width < D else 2
            per = min(per, NB)
            for f in range(NB // per):
                A_free(pe, fills, n + f)
                for i in range(per):
                    b = f * per + i
                    for kt in range(KT):
                        last = products(pe, Ab[(n + f) % 2][:, i * width:(i + 1) * width],
                                        pair(src, kt, slice(b * P, (b + 1) * P)), pair(w, kt), kt == 0, kt == KT - 1)
                last.then_inc(S["A_full"], 1)
            return last

        def A_high(act, dst, n, bias=None):
            for mt in range(KT):
                act.wait_ge(S["A_full"], n + mt + 1)
                if bias is None:
                    i = nc.scalar.activation(dst[:, 0, mt, :], Ab[(n + mt) % 2][:, :], ACT.Copy)
                else:
                    i = nc.scalar.activation(dst[:, 0, mt, :], Ab[(n + mt) % 2][:, :], ACT.Identity, bias=col(bias, mt))
                i.then_inc(S["A_act"], 1)

        def A_low(dve, dst, n, bias=None):
            for mt in range(KT):
                dve.wait_ge(S["A_act"], read_by(A_FILLS, n + mt + 1, "A"))
                if bias is None:
                    i = nc.vector.tensor_tensor(dst[:, 1, mt, :], Ab[(n + mt) % 2][:, :], dst[:, 0, mt, :].bitcast(F32),
                                                ALU.subtract)
                else:
                    i = nc.vector.scalar_tensor_tensor(out=dst[:, 1, mt, :], in0=Ab[(n + mt) % 2][:, :], scalar=col(bias, mt),
                                                       in1=dst[:, 0, mt, :].bitcast(F32), op0=ALU.add, op1=ALU.subtract)
                i.then_inc(S["A_dve"], 1)

        def attend_pe(pe, L):
            G = L["G"]

            def scores(i):
                hg, b = divmod(i, NB)
                n = L["S"] + i
                kt = hg * 4 // L["heads_kt"]
                if n >= 2:
                    pe.wait_ge(S["S_read"], n - 1)
                if b == 0:
                    pe.wait_ge(S["km_high"], 4 * (L["km"] + hg + 1))
                    if hg == 0:
                        pe.wait_ge(S["km_low"], L["km"] + 4)
                bank = Sb[n % 2][:, :].rearrange("p (h t) -> p h t", h=4)
                buf = (L["km"] + hg) % 2
                last = products(pe, bank, pair(qT, kt, slice(b * P, (b + 1) * P)),
                                (km[:, buf, 0, :, b * P:(b + 1) * P], km[:, buf, 1, :, b * P:(b + 1) * P]), True, True)
                last.then_inc(S["S_full"], 1)

            def turn_probs(i):
                n = L["T"] + i
                T_free(pe, T_FILLS, n)
                pe.wait_ge(S["P_ready"], L["S"] + i + 1)
                for h in range(4):
                    last = nc.tensor.transpose(Tb[n % 2][:, h * P:(h + 1) * P], E[:, (L["S"] + i) % EXPS, h, :], ident[:, :])
                last.then_inc(S["T_full"], 1)

            def values(i):
                hg, b = divmod(i, NB)
                o_n = L["O"] + hg
                pe.wait_ge(S["T_act"], L["T"] + i + 1)
                if b == 0:
                    pe.wait_ge(S["O_read"], o_n - 1)
                for h in range(4):
                    vh = hg * 4 + h if L["hd"] == 16 else hg
                    last = pe.matmul(Ob[o_n % 2][h * VW:(h + 1) * VW, b * P:(b + 1) * P], L["v"][:, b, vh, :], PT[:, (L["S"] + i) % 2, h, :],
                                     start=True, stop=True)
                last.then_inc(S["pv_done"], 1)

            def turn_sums(hg):
                n = L["ctx"] + hg
                A_free(pe, A_FILLS, n)
                pe.wait_ge(S["O_read"], L["O"] + hg + 1)
                for b in range(NB):
                    last = nc.tensor.transpose(Ab[n % 2][:, b * P:(b + 1) * P], sums[:, hg % 2, b * P:(b + 1) * P], ident[:, :])
                last.then_inc(S["A_full"], 1)

            for i in range(G + 6):
                if i < G:
                    scores(i)
                if 2 <= i < G + 2:
                    turn_probs(i - 2)
                if 4 <= i < G + 4:
                    values(i - 4)
                if i >= 9 and i % NB == 1:
                    turn_sums(i // NB - 2)

        def attend_act(act, L):
            G = L["G"]
            for i in range(G + 5):
                if i < G:
                    act.wait_ge(S["nm_ready"], L["S"] + i)
                    e, m = E[:, (L["S"] + i) % EXPS], nm[:, (L["S"] + i) % EXPS]
                    for h in range(4):
                        last = nc.scalar.activation(e[:, h], e[:, h], ACT.Exp, scale=L["scale"], bias=m[:, h:h + 1])
                    last.then_inc(S["P_ready"], 1)
                if 2 <= i < G + 2:
                    evict_probs(act, L["S"] + i - 2, L["T"] + i - 2)
                if i >= 8 and i % NB == 0:
                    hg = i // NB - 2
                    act.wait_ge(S["pv_done"], L["S"] + NB * (hg + 1))
                    if hg >= 2:
                        act.wait_ge(S["A_full"], L["ctx"] + hg - 1)
                    nc.scalar.activation(sums[:, hg % 2], Ob[(L["O"] + hg) % 2][:, :], ACT.Copy).then_inc(S["O_read"], 1)

        def evict_probs(act, s, t):
            act.wait_ge(S["T_full"], t + 1)
            if s >= 2:
                act.wait_ge(S["pv_done"], s - 1)
            nc.scalar.activation(PT[:, s % 2], Tb[t % 2][:, :].rearrange("p (h t) -> p h t", h=4), ACT.Copy).then_inc(S["T_act"], 1)

        def soften(dve, s, L, b):
            bank = Sb[s % 2][:, :].rearrange("p (h t) -> p h t", h=4)
            dve.wait_ge(S["S_full"], s + 1)
            if s >= EXPS:
                dve.wait_ge(S["T_full"], T_of_S[s - EXPS] + 1)
            nc.vector.tensor_tensor(E[:, s % EXPS], bank, L["mask"][:, b, None, :].broadcast_to([P, 4, P]),
                                    ALU.add).then_inc(S["S_read"], 1)
            dve.wait_ge(S["S_read"], s + 1)
            nc.vector.tensor_reduce(mx[:, s % EXPS], E[:, s % EXPS], AX_X, ALU.max).then_inc(S["vstep"], 1)
            steps[0] += 1
            dve.wait_ge(S["vstep"], steps[0])
            nc.vector.tensor_scalar(nm[:, s % EXPS], mx[:, s % EXPS], -L["scale"], None, ALU.mult).then_inc(S["nm_ready"], 1)

        T_of_S = [first(T_FILLS, "p0")] + [first(T_FILLS, "p1") + i for i in range(16)] + [first(T_FILLS, "p2") + i for i in range(32)]
        steps = [0]

        def mask_low(dve, L, hg, h):
            if h == 0 and L["km"] + hg >= 2:
                dve.wait_ge(S["S_full"], km_used(L, hg))
            kt, j = divmod(hg * 4 + h, L["heads_kt"])
            nc.vector.tensor_scalar(km[:, (L["km"] + hg) % 2, 1, h, :], kT[:, 1, kt, :].bitcast(F32), L["hmask"][:, j:j + 1],
                                    None, ALU.mult).then_inc(S["km_low"], 1)

        def km_used(L, hg):
            n = L["km"] + hg - 2
            return 1 + NB * (n + 1)

        def mask_high(pool, L, hg):
            if L["km"] + hg >= 2:
                pool.wait_ge(S["S_full"], km_used(L, hg))
            for h in range(4):
                kt, j = divmod(hg * 4 + h, L["heads_kt"])
                if hg > 0:
                    nc.gpsimd.tensor_scalar(km[:, (L["km"] + hg) % 2, 1, h, :], kT[:, 1, kt, :].bitcast(F32), L["hmask"][:, j:j + 1],
                                            1.0, ALU.mult, ALU.mult)
                nc.gpsimd.tensor_scalar(km[:, (L["km"] + hg) % 2, 0, h, :], kT[:, 0, kt, :].bitcast(F32), L["hmask"][:, j:j + 1],
                                        1.0, ALU.mult, ALU.mult).then_inc(S["km_high"], 1)

        def attend_dve(dve, L):
            def normalise(hg):
                n, d = L["ctx"] + hg, L["hd"]
                dve.wait_ge(S["A_full"], n + 1)
                dve.wait_ge(S["A_dve"], read_by(A_FILLS, n, "V"))
                bank = Ab[n % 2][:, :].rearrange("p (b h d) -> p b h d", b=NB, h=4)
                nc.vector.reciprocal(r1[:, :, :], bank[:, :, :, d]).then_inc(S["vstep"], 1)
                steps[0] += 1
                dve.wait_ge(S["vstep"], steps[0])
                dst = o[:, :, hg * 4 * d:(hg + 1) * 4 * d].rearrange("p b (h d) -> p b h d", h=4)
                nc.vector.tensor_tensor(dst, bank[:, :, :, 0:d], r1[:, :, :, None].broadcast_to([P, NB, 4, d]),
                                        ALU.mult).then_inc(S["A_dve"], 1)

            dve.wait_ge(S["A_dve"], read_by(A_FILLS, L["kfill"] + KT, "V"))
            for h in range(4):
                mask_low(dve, L, 0, h)
            if L["hd"] == 16:
                dve.wait_ge(S["mask1_ready"], 1)
            else:
                dve.wait_ge(S["mask2_loaded"], 16)
            for i in range(L["G"] + 6):
                hg, b = divmod(i, NB)
                if i < L["G"]:
                    soften(dve, L["S"] + i, L, b)
                if i >= 9 and b == 1:
                    normalise(hg - 2)

        norms = [0]

        def norm(dve, src, dst, nb, w):
            for b in range(nb):
                nc.vector.bn_stats(stats[:, b], src(b)).then_inc(S["vstep"], 1)
            steps[0] += nb
            dve.wait_ge(S["vstep"], steps[0])
            for b in range(nb):
                nc.vector.bn_aggr(mv[:, b], stats[:, b]).then_inc(S["var_ready"], 1)
            norms[0] += 1
            dve.wait_ge(S["var_ready"], nb * norms[0])
            for b in range(nb):
                nc.vector.scalar_tensor_tensor(out=dst[:, b], in0=src(b), scalar=mv[:, b, 0:1], in1=w,
                                               op0=ALU.subtract, op1=ALU.mult).then_inc(S["vstep"], 1)
            steps[0] += nb
            dve.wait_ge(S["vstep"], steps[0])
            dve.wait_ge(S["rstd_ready"], norms[0])

        def power(pool, n, nb, eps):
            pool.wait_ge(S["var_ready"], nb * n)
            nc.gpsimd.tensor_scalar(var[:, 0:nb], mv[:, 0:nb, 1], eps, 1.0, ALU.add, ALU.mult).then_inc(S["pool_step"], 1)
            psteps[0] += 1
            pool.wait_ge(S["pool_step"], psteps[0])
            nc.gpsimd.tensor_tensor(rstd[:, 0:nb], var[:, 0:nb], neg_half[:, 0:nb], ALU.pow).then_inc(S["rstd_ready"], 1)

        psteps = [0]
        S["pool_step"] = sem("pool_step")

        def mlp_pe(pe, fills, n, o_n):
            def up(m):
                A_free(pe, fills, n + m)
                for kt in range(KT):
                    last = products(pe, Ab[(n + m) % 2][:, :], pair(fcw, kt, slice(m * P, (m + 1) * P)), pair(aT, kt),
                                    kt == 0, kt == KT - 1)
                last.then_inc(S["A_full"], 1)
                return last

            def down(m):
                pe.wait_ge(S["g_high"], m + 1)
                pe.wait_ge(S["g_low"], m + 1)
                if m == 0 and o_n:
                    pe.wait_ge(S["O_read"], o_n)
                for b in range(NB):
                    bank = Ob[(o_n + b // 2) % 2][:, (b % 2) * D:(b % 2 + 1) * D]
                    left = pair(gT[:, m % 2], slice(b * P, (b + 1) * P))
                    right = pair(pjw, m)
                    pe.matmul(bank, left[0], right[0], start=(m == 0 and b % 2 == 0), stop=False, skip_group_check=True)
                    pe.matmul(bank, left[1], right[0], start=False, stop=False, skip_group_check=True)
                    last = pe.matmul(bank, left[0], right[1], start=False, stop=(m == MT - 1), skip_group_check=True)
                last.then_inc(S["g_used"], 1)

            for m in range(MT + 2):
                if m < MT:
                    up(m)
                if m >= 2:
                    down(m - 2)

        def mlp_act(act, fills, n, func, bias):
            for m in range(MT):
                act.wait_ge(S["A_full"], n + m + 1)
                if m >= 2:
                    act.wait_ge(S["g_low"], m - 1)
                    act.wait_ge(S["g_used"], m - 1)
                nc.scalar.activation(g[:, m % 2], Ab[(n + m) % 2][:, :], func, bias=col(bias, m)).then_inc(S["A_act"], 1)
                act.wait_ge(S["A_act"], read_by(fills, n + m + 1, "A"))
                nc.scalar.activation(gT[:, m % 2, 0], g[:, m % 2], ACT.Copy).then_inc(S["g_high"], 1)

        def mlp_dve(dve):
            for m in range(MT):
                dve.wait_ge(S["g_high"], m + 1)
                nc.vector.tensor_tensor(gT[:, m % 2, 1], g[:, m % 2], gT[:, m % 2, 0].bitcast(F32), ALU.subtract).then_inc(S["g_low"], 1)

        def mlp_add(dve, o_n):
            dve.wait_ge(S["g_used"], MT)
            for f in range(2):
                nc.vector.tensor_tensor(xh[:, 2 * f:2 * f + 2], Ob[(o_n + f) % 2][:, :].rearrange("p (b d) -> p b d", b=2),
                                        xh[:, 2 * f:2 * f + 2], ALU.add).then_inc(S["O_read"], 1)

        fT = {n: first(T_FILLS, n) for n in ("c", "x", "p0", "z1", "ctx1", "z2", "x2", "ctx2")}
        fA = {n: first(A_FILLS, n) for n in ("q0", "v0", "k1", "v1", "q1", "o1", "k2", "v2", "fc", "q2", "o2")}

        with nc.Fori(0, HALVES) as half:
            with nc.Block() as block:
                @block.sync
                def _(sp):
                    sp.dma_start(o[:, :, :], a["ctx_2048"][bass.ds(half * NB, NB)].rearrange("b t d -> t b d")).then_inc(S["c_loaded"], 16)
                    sp.dma_start(xh[:, :, :], a["x"][bass.ds(half * NB, NB)].rearrange("b t d -> t b d")).then_inc(S["x_loaded"], 16)
                    sp.dma_start(mask1b[:, :, :], a["mask_BxS2_bf1"][bass.ds(half * NB, NB)][None].broadcast_to([P, NB, P])).then_inc(S["mask1_loaded"], 16)
                    sp.dma_start(masks[2][:, :, :], a["mask_Bx1xSxS2_ff0"][bass.ds(half * NB, NB)].rearrange("b o q t -> q (b o) t")).then_inc(S["mask2_loaded"], 16)

                @block.tensor
                def _(pe):
                    pe.wait_ge(S["c_loaded"], 16)
                    turn(pe, o, T_FILLS, fT["c"])
                    pe.wait_ge(S["x_loaded"], 16)
                    turn(pe, xh, T_FILLS, fT["x"])
                    pe.wait_ge(S["T_act"], 4)
                    pe.wait_ge(S["T_dve"], 4)
                    project_T(pe, m0w, aT, A_FILLS, fA["q0"])
                    project(pe, v0w, D, cT, A_FILLS, fA["v0"])
                    pe.wait_ge(S["A_act"], 2)
                    pe.wait_ge(S["A_dve"], 2)
                    for b in range(NB):
                        for kt in range(KT):
                            last = products(pe, Sb[0][:, b * P:(b + 1) * P], pair(qT, kt, slice(b * P, (b + 1) * P)),
                                            pair(cT, kt, slice(b * P, (b + 1) * P)), kt == 0, kt == KT - 1)
                    last.then_inc(S["S_full"], 1)
                    project_T(pe, w1[1], cT, A_FILLS, fA["k1"])
                    project(pe, w1[2], D, cT, A_FILLS, fA["v1"])
                    T_free(pe, T_FILLS, fT["p0"])
                    pe.wait_ge(S["P_ready"], 1)
                    for b in range(NB):
                        last = nc.tensor.transpose(Tb[fT["p0"] % 2][:, b * P:(b + 1) * P], E[:, 0, b, :], ident[:, :])
                    last.then_inc(S["T_full"], 1)
                    pe.wait_ge(S["T_act"], fT["p0"] + 1)
                    pe.wait_ge(S["A_dve"], read_by(A_FILLS, fA["v0"] + 2, "V"))
                    for b in range(NB):
                        if b >= 2:
                            pe.wait_ge(S["O_read"], b - 1)
                        last = pe.matmul(Ob[b % 2][:, 0:D + 1], PT[:, 0, b, :], v0[:, b, :], start=True, stop=True)
                        last.then_inc(S["O_full" if b < NB - 1 else "pv_done"], 1)
                    pe.wait_ge(S["norm_ready"], NB)
                    turn(pe, z, T_FILLS, fT["z1"])
                    pe.wait_ge(S["T_act"], fT["z1"] + KT)
                    pe.wait_ge(S["T_dve"], splits_in(T_FILLS, fT["z1"] + KT))
                    project_T(pe, w1[0], aT, A_FILLS, fA["q1"])
                    pe.wait_ge(S["A_act"], read_by(A_FILLS, fA["q1"] + KT, "A"))
                    pe.wait_ge(S["A_dve"], read_by(A_FILLS, fA["q1"] + KT, "V"))
                    attend_pe(pe, LAYERS[1])
                    pe.wait_ge(S["A_dve"], read_by(A_FILLS, LAYERS[1]["ctx"] + 4, "V"))
                    turn(pe, o, T_FILLS, fT["ctx1"])
                    pe.wait_ge(S["T_act"], fT["ctx1"] + KT)
                    pe.wait_ge(S["T_dve"], splits_in(T_FILLS, fT["ctx1"] + KT))
                    project(pe, w1[3], D, aT, A_FILLS, fA["o1"])
                    project_T(pe, w2[1], cT, A_FILLS, fA["k2"])
                    project(pe, w2v, 64, cT, A_FILLS, fA["v2"])
                    pe.wait_ge(S["norm_ready"], 2 * NB)
                    turn(pe, z, T_FILLS, fT["z2"])
                    pe.wait_ge(S["T_act"], fT["z2"] + KT)
                    pe.wait_ge(S["T_dve"], splits_in(T_FILLS, fT["z2"] + KT))
                    mlp_pe(pe, A_FILLS, fA["fc"], first(O_FILLS, "mlp"))
                    pe.wait_ge(S["O_read"], LAYERS[2]["O"])
                    turn(pe, xh, T_FILLS, fT["x2"])
                    pe.wait_ge(S["T_act"], fT["x2"] + KT)
                    pe.wait_ge(S["T_dve"], splits_in(T_FILLS, fT["x2"] + KT))
                    project_T(pe, w2[0], aT, A_FILLS, fA["q2"])
                    pe.wait_ge(S["A_act"], read_by(A_FILLS, fA["q2"] + KT, "A"))
                    pe.wait_ge(S["A_dve"], read_by(A_FILLS, fA["q2"] + KT, "V"))
                    attend_pe(pe, LAYERS[2])
                    pe.wait_ge(S["A_dve"], read_by(A_FILLS, LAYERS[2]["ctx"] + 8, "V"))
                    turn(pe, o, T_FILLS, fT["ctx2"])
                    pe.wait_ge(S["T_act"], fT["ctx2"] + KT)
                    pe.wait_ge(S["T_dve"], splits_in(T_FILLS, fT["ctx2"] + KT))
                    project(pe, w2[2], D, aT, A_FILLS, fA["o2"])

                @block.scalar
                def _(act):
                    split_high(act, cT, fT["c"])
                    split_high(act, aT, fT["x"])
                    A_high(act, qT, fA["q0"])
                    act.wait_ge(S["S_read"], 1)
                    nc.scalar.activation(E[:, 0], E[:, 0], ACT.Exp, scale=D ** -0.5).then_inc(S["P_ready"], 1)
                    A_high(act, kT, fA["k1"], "L1_xattn_k_b")
                    evict_probs(act, 0, fT["p0"])
                    a_free(act, "q0", 2)
                    split_high(act, aT, fT["z1"])
                    act.wait_ge(S["S_full"], 1)
                    A_high(act, qT, fA["q1"], "L1_xattn_q_b")
                    attend_act(act, LAYERS[1])
                    a_free(act, "q1", 2)
                    split_high(act, aT, fT["ctx1"])
                    act.wait_ge(S["km_high"], 16)
                    act.wait_ge(S["km_low"], 4)
                    A_high(act, kT, fA["k2"], "L2_xattn_bk")
                    a_free(act, "o1", 2)
                    split_high(act, aT, fT["z2"])
                    mlp_act(act, A_FILLS, fA["fc"], ACT.Gelu_apprx_tanh, "L1_xattn_fc_b")
                    a_free(act, "fc", MT)
                    split_high(act, aT, fT["x2"])
                    act.wait_ge(S["S_full"], LAYERS[2]["S"])
                    A_high(act, qT, fA["q2"], "L2_xattn_bq")
                    attend_act(act, LAYERS[2])
                    a_free(act, "q2", 2)
                    split_high(act, aT, fT["ctx2"])

                @block.gpsimd
                def _(pool):
                    psteps[0] = 0
                    power(pool, 1, NB, LN_EPS)
                    pool.wait_ge(S["norm_ready"], NB)
                    nc.gpsimd.tensor_tensor(xh[:, :, :], xh[:, :, :], row("L1_xattn_cproj_b")[:, None, :].broadcast_to([P, NB, D]),
                                            ALU.add).then_inc(S["x_biased"], 1)
                    pool.wait_ge(S["A_act"], read_by(A_FILLS, fA["k1"] + KT, "A"))
                    pool.wait_ge(S["A_dve"], read_by(A_FILLS, fA["k1"] + KT, "V"))
                    for hg in range(4):
                        mask_high(pool, LAYERS[1], hg)
                    power(pool, 2, NB, LN_EPS)
                    pool.wait_ge(S["norm_ready"], 2 * NB)
                    nc.gpsimd.tensor_tensor(xh[:, :, :], xh[:, :, :], row("L1_xattn_proj_b")[:, None, :].broadcast_to([P, NB, D]),
                                            ALU.add).then_inc(S["x_biased"], 1)
                    pool.wait_ge(S["A_act"], read_by(A_FILLS, fA["k2"] + KT, "A"))
                    pool.wait_ge(S["A_dve"], read_by(A_FILLS, fA["k2"] + KT, "V"))
                    for hg in range(2):
                        mask_high(pool, LAYERS[2], hg)
                    pool.wait_ge(S["T_full"], fT["x2"] + KT)
                    pool.wait_ge(S["O_read"], LAYERS[2]["O"])
                    nc.gpsimd.tensor_tensor(xh[:, :, :], xh[:, :, :], row("L2_xattn_bo")[:, None, :].broadcast_to([P, NB, D]),
                                            ALU.add).then_inc(S["x_biased"], 1)
                    for hg in range(2, 8):
                        mask_high(pool, LAYERS[2], hg)
                    power(pool, 3, NB, LN2_EPS)

                @block.vector
                def _(dve):
                    steps[0] = norms[0] = 0
                    dve.wait_ge(S["mask1_loaded"], 16)
                    nc.vector.tensor_scalar(masks[1][:, :, :], mask1b[:, :, :], 1.0, BIG, ALU.subtract, ALU.mult).then_inc(S["mask1_ready"], 1)
                    split_low(dve, cT, fT["c"])
                    split_low(dve, aT, fT["x"])
                    A_low(dve, qT, fA["q0"])
                    for f in range(2):
                        n = fA["v0"] + f
                        dve.wait_ge(S["A_full"], n + 1)
                        nc.vector.tensor_copy(v0[:, 2 * f:2 * f + 2, 0:D], Ab[n % 2][:, :].rearrange("p (b d) -> p b d", b=2)).then_inc(S["A_dve"], 1)
                    bank = Sb[0][:, :].rearrange("p (b t) -> p b t", b=NB)
                    dve.wait_ge(S["S_full"], 1)
                    nc.vector.tensor_reduce(mx[:, 0], bank, AX_X, ALU.max).then_inc(S["vstep"], 1)
                    steps[0] += 1
                    dve.wait_ge(S["vstep"], steps[0])
                    nc.vector.tensor_tensor(E[:, 0], bank, mx[:, 0, :, None].broadcast_to([P, NB, P]), ALU.subtract).then_inc(S["S_read"], 1)
                    A_low(dve, kT, fA["k1"], "L1_xattn_k_b")
                    for f in range(2):
                        n = fA["v1"] + f
                        dve.wait_ge(S["A_full"], n + 1)
                        nc.vector.tensor_tensor(v1[:, 2 * f:2 * f + 2, :, 0:16], Ab[n % 2][:, :].rearrange("p (b h d) -> p b h d", b=2, d=16),
                                                row("L1_xattn_v_b").rearrange("p (h d) -> p h d", d=16)[:, None].broadcast_to([P, 2, 16, 16]),
                                                ALU.add).then_inc(S["A_dve"], 1)
                    for b in range(NB):
                        if b < NB - 1:
                            dve.wait_ge(S["O_full"], b + 1)
                        else:
                            dve.wait_ge(S["pv_done"], 1)
                        nc.vector.reciprocal(r0[:, b:b + 1], Ob[b % 2][:, D:D + 1]).then_inc(S["vstep"], 1)
                        steps[0] += 1
                        dve.wait_ge(S["vstep"], steps[0])
                        nc.vector.tensor_scalar(r0[:, b:b + 1], r0[:, b:b + 1], alpha[:, 0:1], None, ALU.mult).then_inc(S["vstep"], 1)
                        steps[0] += 1
                        dve.wait_ge(S["vstep"], steps[0])
                        dve.wait_ge(S["T_full"], fT["x"] + KT)
                        nc.vector.scalar_tensor_tensor(out=xh[:, b], in0=Ob[b % 2][:, 0:D], scalar=r0[:, b:b + 1], in1=xh[:, b],
                                                       op0=ALU.mult, op1=ALU.add).then_inc(S["O_read"], 1)
                    dve.wait_ge(S["O_read"], NB)
                    norm(dve, lambda b: xh[:, b], z, NB, row("L1_xattn_ln1_w"))
                    for b in range(NB):
                        nc.vector.scalar_tensor_tensor(out=z[:, b], in0=z[:, b], scalar=rstd[:, b:b + 1], in1=row("L1_xattn_ln1_b"),
                                                       op0=ALU.mult, op1=ALU.add).then_inc(S["norm_ready"], 1)
                    split_low(dve, aT, fT["z1"])
                    A_low(dve, qT, fA["q1"], "L1_xattn_q_b")
                    attend_dve(dve, LAYERS[1])
                    split_low(dve, aT, fT["ctx1"])
                    dve.wait_ge(S["x_biased"], 1)
                    for f in range(2):
                        n = fA["o1"] + f
                        dve.wait_ge(S["A_full"], n + 1)
                        nc.vector.tensor_tensor(xh[:, 2 * f:2 * f + 2], Ab[n % 2][:, :].rearrange("p (b d) -> p b d", b=2),
                                                xh[:, 2 * f:2 * f + 2], ALU.add).then_inc(S["A_dve"], 1)
                    dve.wait_ge(S["A_dve"], read_by(A_FILLS, fA["o1"] + 2, "V"))
                    dve.wait_ge(S["T_full"], fT["z1"] + KT)
                    norm(dve, lambda b: xh[:, b], z, NB, row("L1_xattn_ln2_w"))
                    for b in range(NB):
                        nc.vector.scalar_tensor_tensor(out=z[:, b], in0=z[:, b], scalar=rstd[:, b:b + 1], in1=row("L1_xattn_ln2_b"),
                                                       op0=ALU.mult, op1=ALU.add).then_inc(S["norm_ready"], 1)
                    dve.wait_ge(S["km_high"], 16)
                    A_low(dve, kT, fA["k2"], "L2_xattn_bk")
                    n = fA["v2"]
                    dve.wait_ge(S["A_full"], n + 1)
                    nc.vector.tensor_tensor(v2[:, :, :, 0:8], Ab[n % 2][:, 0:NB * 64].rearrange("p (b h d) -> p b h d", b=NB, d=8),
                                            bv2[:, :].rearrange("p (h d) -> p h d", d=8)[:, None].broadcast_to([P, NB, 8, 8]),
                                            ALU.add).then_inc(S["A_dve"], 1)
                    split_low(dve, aT, fT["z2"])
                    mlp_dve(dve)
                    dve.wait_ge(S["x_biased"], 2)
                    mlp_add(dve, first(O_FILLS, "mlp"))
                    split_low(dve, aT, fT["x2"])
                    A_low(dve, qT, fA["q2"], "L2_xattn_bq")
                    attend_dve(dve, LAYERS[2])
                    split_low(dve, aT, fT["ctx2"])
                    dve.wait_ge(S["x_biased"], 3)
                    for f in range(2):
                        n = fA["o2"] + f
                        dve.wait_ge(S["A_full"], n + 1)
                        nc.vector.tensor_tensor(xh[:, 2 * f:2 * f + 2], Ab[n % 2][:, :].rearrange("p (b d) -> p b d", b=2),
                                                xh[:, 2 * f:2 * f + 2], ALU.add).then_inc(S["A_dve"], 1)
                    dve.wait_ge(S["A_dve"], read_by(A_FILLS, fA["o2"] + 2, "V"))
                    dve.wait_ge(S["T_full"], fT["z2"] + KT)
                    norm(dve, lambda b: xh[:, b], z, NB, row("L2_xattn_gamma"))
                    for b in range(NB):
                        nc.vector.scalar_tensor_tensor(out=x_all[:, bass.ds(half * NB + b, 1), :], in0=z[:, b:b + 1], scalar=rstd[:, b:b + 1],
                                                       in1=row("L2_xattn_beta")[:, None, :], op0=ALU.mult, op1=ALU.add).then_inc(S["x_out"], 1)
            for each in S.values():
                nc.sync.sem_clear(each)
            nc.all_engine_barrier()

        s3 = ExitStack()
        cT3 = sb("cT3", [P, 2, KT, B * P], R32, s3)
        hT3 = sb("hT3", [P, 2, KT, B * P], R32, s3)
        t3 = ExitStack()
        c3 = sb("c3", [P, B, D], F32, t3)
        z3 = sb("z3", [P, B, D], F32, t3)
        t3.close()
        qT3 = sb("qT3", [P, 2, 2, B * P], R32, s3)
        fc_st = sb("fc_st", [P, KT, INNER], F32, s3)
        pj_st = sb("pj_st", [P, MT, D], F32, s3)
        wst = [sb(f"wst_{n}", [P, KT, HG3 * P], F32, s3) for n in "qkv"]
        wo_st = sb("wo_st", [P, HG3, D], F32, s3)
        w3 = [sb(f"w3_{n}", [P, 2, KT, HG3 * P], R32, s3) for n in "qkv"]
        wo3 = sb("wo3", [P, 2, HG3, D], R32, s3)
        v_row = sb("v_row", [P, HG3 * P], F32, s3)
        bias_v_row = sb("bias_v_row", [P, HG3 * P], F32, s3)
        kT3 = sb("kT3", [P, 2, 2, B, T3], R32, s3)
        vf = sb("vf", [P, 2, 2, HG3 * P], F32, s3)
        v3 = sb("v3", [P, 2, B, HG3 * P], R32, s3)
        E3 = sb("E3", [P, EXPS, 3, T3], F32, s3)
        PT3 = sb("PT3", [P, 2, 2, 3 * P], R32, s3)
        ctxT3 = sb("ctxT3", [P, 2, HG3, B * P], R32, s3)
        mx3 = sb("mx3", [P, EXPS, 3], F32, s3)
        nm3 = sb("nm3", [P, EXPS, 3], F32, s3)
        sum3 = sb("sum3", [P, EXPS, 3], F32, s3)
        rs3 = sb("rs3", [P, EXPS, 3], F32, s3)
        s3.close()
        SCALE3 = float(P) ** -0.5

        PASS = [("S", 0, 0, 0), ("q", 0, 1, 0), ("P", 0, 0, 0), ("T", -1, 1, 2), ("q", 0, 1, 1), ("PV", -1, 1, 1), ("W", 1, 0, 0), ("v", 0, 0, 1),
                ("S", 0, 0, 1), ("v", 0, 0, 2), ("P", 0, 0, 1), ("T", 0, 0, 0), ("k", 0, 1, 0), ("PV", -1, 1, 2), ("v", 0, 0, 3),
                ("S", 0, 0, 2), ("k", 0, 1, 1), ("P", 0, 0, 2), ("T", 0, 0, 1), ("W", 1, 1, 0), ("out", -1, 0, 0), ("PV", 0, 0, 0), ("W", 1, 2, 0),
                ("out", -1, 0, 1),
                ("S", 0, 1, 0), ("out", -1, 0, 2), ("P", 0, 1, 0), ("T", 0, 0, 2), ("out", -1, 0, 3), ("row", 1, 0, 0), ("PV", 0, 0, 1), ("WO", 0, 0, 0),
                ("S", 0, 1, 1), ("q", 1, 0, 0), ("P", 0, 1, 1), ("T", 0, 1, 0), ("q", 1, 0, 1), ("PV", 0, 0, 2), ("k", 1, 0, 0),
                ("S", 0, 1, 2), ("k", 1, 0, 1), ("P", 0, 1, 2), ("T", 0, 1, 1), ("PV", 0, 1, 0), ("v", 1, 0, 0)]
        HEAD_START = [("W", 1, n, 0) for n in range(3)] + [("row", 1, 0, 0)] + [w for w in PASS if w[1] == 1 and w[0] in "qkv"]
        FINISH = [w for w in PASS if w[1] == -1]
        PAIRS = H3 // HG3
        FILLS = [w for w in PASS if w[0] in ("q", "k", "v", "out")]
        A_READS = [w for w in FILLS if w[0] in ("q", "k")]
        NF, NG, NC, NV = len(FILLS), 3 * HG3, 2 * HG3, B // 2
        AHEAD = sum(w[1] == 1 for w in FILLS)
        OUTS = NF - sum(w[0] != "out" for w in FILLS)

        def steps_of(p):
            if isinstance(p, int) and p == -1:
                return HEAD_START
            if isinstance(p, int) and p == PAIRS:
                return FINISH
            if isinstance(p, int) and p == 0:
                return [w for w in PASS if w[1] != -1]
            if isinstance(p, int) and p == PAIRS - 1:
                return [w for w in PASS if w[1] != 1]
            return PASS

        def fill3(p, step):
            if isinstance(p, int) and p == -1:
                return FILLS.index(step) % 2, [w for w in HEAD_START if w[0] in "qkv"].index(step)
            at = FILLS.index(step)
            if isinstance(p, int) and p == 0:
                outs = sum(w[0] == "out" for w in FILLS[:at])
                return at % 2, AHEAD + at - outs
            if isinstance(p, int) and p == PAIRS:
                return at % 2, NF * PAIRS - OUTS + [w for w in FINISH if w[0] == "out"].index(step)
            return at % 2, p * NF + (AHEAD - OUTS + at)

        def high3(p, step):
            if isinstance(p, int) and p == -1:
                return [w for w in HEAD_START if w[0] in "qk"].index(step) + 1
            return p * len(A_READS) + (sum(w[1] == 1 for w in A_READS) + A_READS.index(step) + 1)

        def passes(eng, do):
            do(-1)
            do(0)
            with eng.Fori(1, PAIRS - 1) as p:
                do(p)
            do(PAIRS - 1)
            do(PAIRS)

        def reached(eng, sem, value):
            if not isinstance(value, int) or value > 0:
                eng.wait_ge(sem, value)

        sem = lambda n: ctx.enter_context(nc.semaphore(f"{n}3"))
        N = {n: sem(n) for n in (
            "wq_loaded", "wk_loaded", "wv_loaded", "wo_loaded", "rows_loaded", "rowb_loaded", "w_high", "w_low", "wo_high", "wo_low",
            "v_row_ready", "A_full", "A_act", "A_dve", "bias_high", "bias_low", "v_high", "v_low",
            "S_full", "max_ready", "nm_ready", "exp_done", "r_ready", "P_ready", "T_full", "T_act", "T_dve", "pv_done",
            "ctx_high", "ctx_low", "act_apart", "pool_apart")}

        def attention3(att):
            names = {n: f"L3_xattn_{n}{att + 1}" for n in ("wq", "wk", "wv", "wo", "bv", "bias_v")}
            ln_w, ln_b, bo = f"L3_xattn_ln{att + 1}_scale", f"L3_xattn_ln{att + 1}_offset", f"L3_xattn_bo{att + 1}"
            cols = colsA[:, atA["L3_xattn_bq1"]:atA["L3_xattn_bq1"] + 4 * H3] if att == 0 else colsB[:, 0:4 * H3]
            cols = cols.rearrange("p (k h) -> p k h", k=4)

            turns = ([("c", f) for f in range(4)] if att == 0 else []) + [("h", f) for f in range(4)]
            with nc.Block() as block:
                @block.sync
                def _(sp):
                    if att == 1:
                        sp.dma_start(fc_st[:, :, :], a["L3_xattn_w_fc1"].rearrange("(k p) n -> p k n", p=P)).then_inc(fc_in, 16)
                        sp.dma_start(pj_st[:, :, :], a["L3_xattn_w_fc2"].rearrange("(m p) n -> p m n", p=P)).then_inc(pj_in, 16)
                    if att == 0:
                        sp.dma_start(c3[:, :, :], a["ctx_2048"].rearrange("b t d -> t b d")).then_inc(S["c_loaded"], 16)

                @block.tensor
                def _(pe):
                    for n, (what, f) in enumerate(turns):
                        if (what, f) == ("c", 0):
                            pe.wait_ge(S["c_loaded"], 16)
                        if (what, f) == ("h", 0):
                            pe.wait_ge(S["norm_ready"], B)
                        if n >= 2:
                            pe.wait_ge(S["T_act"], n - 1)
                            pe.wait_ge(S["T_dve"], n - 1)
                        kt, half = divmod(f, 2)
                        src = c3 if what == "c" else z3
                        for b in range(NB):
                            last = nc.tensor.transpose(Tb[n % 2][:, b * P:(b + 1) * P],
                                                       src[:, half * NB + b, kt * P:(kt + 1) * P], ident[:, :])
                        last.then_inc(S["T_full"], 1)

                @block.scalar
                def _(act):
                    if att == 1:
                        act.wait_ge(fc_in, 16)
                        nc.scalar.activation(fcw[:, 0], fc_st[:, :, :], ACT.Copy).then_inc(split3, 1)
                        act.wait_ge(pj_in, 16)
                        nc.scalar.activation(pjw[:, 0], pj_st[:, :, :], ACT.Copy).then_inc(split3, 1)
                    for n, (what, f) in enumerate(turns):
                        kt, half = divmod(f, 2)
                        dst = cT3 if what == "c" else hT3
                        act.wait_ge(S["T_full"], n + 1)
                        nc.scalar.activation(dst[:, 0, kt, half * TOK:(half + 1) * TOK], Tb[n % 2][:, :], ACT.Copy).then_inc(S["T_act"], 1)

                @block.gpsimd
                def _(pool):
                    psteps[0] = 0
                    power(pool, 1, B, LN_EPS)
                    pool.wait_ge(S["norm_ready"], B)
                    nc.gpsimd.tensor_tensor(x_all[:, :, :], x_all[:, :, :], row(bo)[:, None, :].broadcast_to([P, B, D]), ALU.add)
                    if att == 1:
                        for n, (full, split) in enumerate(((fc_st, fcw), (pj_st, pjw))):
                            pool.wait_ge(split3, n + 1)
                            nc.gpsimd.tensor_tensor(split[:, 1], full[:, :, :], split[:, 0].bitcast(F32), ALU.subtract)

                @block.vector
                def _(dve):
                    steps[0] = norms[0] = 0
                    norm(dve, lambda b: x_all[:, b], z3, B, row(ln_w))
                    for b in range(B):
                        nc.vector.scalar_tensor_tensor(out=z3[:, b], in0=z3[:, b], scalar=rstd[:, b:b + 1], in1=row(ln_b),
                                                       op0=ALU.mult, op1=ALU.add).then_inc(S["norm_ready"], 1)
                    for n, (what, f) in enumerate(turns):
                        kt, half = divmod(f, 2)
                        dst = cT3 if what == "c" else hT3
                        part = (kt, slice(half * TOK, (half + 1) * TOK))
                        dve.wait_ge(S["T_act"], n + 1)
                        nc.vector.tensor_tensor(dst[:, 1, part[0], part[1]], Tb[n % 2][:, :],
                                                dst[:, 0, part[0], part[1]].bitcast(F32), ALU.subtract).then_inc(S["T_dve"], 1)

            for n in ("c_loaded", "T_full", "T_act", "T_dve", "vstep", "var_ready", "rstd_ready", "norm_ready", "pool_step"):
                nc.sync.sem_clear(S[n])
            nc.all_engine_barrier()

            def const(kind, p, h):
                return cols[:, kind, bass.ds(p * HG3 + h, 1)]

            with nc.Block() as block:
                @block.sync
                def _(sp):
                    def load_pair(p):
                        at = bass.ds(p * HG3 * P, HG3 * P)
                        for n, (w, t) in enumerate((("wq", wst[0]), ("wk", wst[1]), ("wv", wst[2]))):
                            reached(sp, N["w_low"], p * 3 + (n - 2))
                            sp.dma_start(t[:, :, :], a[names[w]][:, at].rearrange("(k p) n -> p k n", p=P)).then_inc(N[w + "_loaded"], 16)
                        reached(sp, N["v_low"], p * NV)
                        sp.dma_start(v_row[:, :], a[names["bv"]][at][None, :].broadcast_to([P, HG3 * P])).then_inc(N["rows_loaded"], 16)
                        sp.dma_start(bias_v_row[:, :], a[names["bias_v"]].rearrange("a b h k -> (a b h k)")[at][None, :]
                                     .broadcast_to([P, HG3 * P])).then_inc(N["rowb_loaded"], 16)

                    def load_out(p):
                        reached(sp, N["wo_low"], p * 1)
                        sp.dma_start(wo_st[:, :, :], a[names["wo"]][bass.ds(p * HG3 * P, HG3 * P), :].rearrange("(h p) n -> p h n", p=P)
                                     ).then_inc(N["wo_loaded"], 16)

                    load_pair(0)
                    load_out(0)
                    load_pair(1)
                    with sp.Fori(1, PAIRS - 1) as p:
                        load_out(p)
                        load_pair(p + 1)
                    load_out(PAIRS - 1)

                @block.gpsimd
                def _(pool):
                    def do(p):
                        for step in steps_of(p):
                            what, dp, h, j = step
                            if what == "row":
                                pool.wait_ge(N["rows_loaded"], (p + 2) * 16)
                                pool.wait_ge(N["rowb_loaded"], (p + 2) * 16)
                                nc.gpsimd.tensor_tensor(v_row[:, :], v_row[:, :], bias_v_row[:, :], ALU.subtract).then_inc(N["v_row_ready"], 1)
                            elif what == "WO":
                                pool.wait_ge(N["wo_loaded"], (p + 1) * 16)
                                if not (isinstance(p, int) and p == 0):
                                    pool.wait_ge(N["A_full"], fill3(p, ("out", -1, 0, NB - 1))[1] + 1)
                                pool.sem_inc(N["pool_apart"], 1)
                                nc.gpsimd.tensor_scalar(wo3[:, 0], wo_st[:, :, :], 1.0, 1.0, ALU.mult, ALU.mult).then_inc(N["wo_high"], 1)
                                pool.wait_ge(N["wo_high"], p + 1)
                                nc.gpsimd.tensor_tensor(wo3[:, 1], wo_st[:, :, :], wo3[:, 0].bitcast(F32), ALU.subtract).then_inc(N["wo_low"], 1)
                            elif what == "v":
                                pool.wait_ge(N["v_high"], (p + dp) * NV + (j + 1))
                                nc.gpsimd.tensor_tensor(v3[:, 1, 2 * j:2 * j + 2], vf[:, j % 2], v3[:, 0, 2 * j:2 * j + 2].bitcast(F32),
                                                        ALU.subtract).then_inc(N["v_low"], 1)
                            elif what == "P":
                                g_ = 3 * h + j
                                nb = GROUPS3[j][1] - GROUPS3[j][0]
                                pool.wait_ge(N["r_ready"], p * NG + (g_ + 1))
                                e = E3[:, g_ % EXPS, 0:nb, 0:P]
                                nc.gpsimd.tensor_tensor(e, e, rs3[:, g_ % EXPS, 0:nb, None].broadcast_to([P, nb, P]),
                                                        ALU.mult).then_inc(N["P_ready"], 1)
                    passes(pool, do)

                @block.scalar
                def _(act):
                    def do(p):
                        for step in steps_of(p):
                            what, dp, h, j = step
                            if what == "W":
                                act.wait_ge(N[("wq", "wk", "wv")[h] + "_loaded"], (p + 2) * 16)
                                if not (isinstance(p, int) and p == -1):
                                    last = (("q", 0, 1, 1), ("k", 0, 1, 1), ("v", 0, 0, 3))[h]
                                    act.wait_ge(N["A_full"], fill3(p, last)[1] + 1)
                                nc.scalar.activation(w3[h][:, 0], wst[h][:, :, :], ACT.Copy).then_inc(N["w_high"], 1)
                            elif what in ("q", "k"):
                                bank, n = fill3(p, step)
                                act.wait_ge(N["A_full"], n + 1)
                                reached(act, N["S_full"], (p + dp) * NG + (3 * h - 3))
                                act.sem_inc(N["act_apart"], 1)
                                c = const(0 if what == "q" else 1, p + dp, h)
                                if what == "q":
                                    nc.scalar.activation(qT3[:, h, 0, j * TOK:(j + 1) * TOK], Ab[bank][:, :], ACT.Identity,
                                                         bias=c).then_inc(N["A_act"], 1)
                                else:
                                    nc.scalar.activation(kT3[:, h, 0, j * NB:(j + 1) * NB, 0:P],
                                                         Ab[bank][:, :].rearrange("p (b t) -> p b t", b=NB), ACT.Identity,
                                                         bias=c).then_inc(N["A_act"], 1)
                            elif what == "v":
                                act.wait_ge(N["A_dve"], fill3(p, step)[1] + 1)
                                group = [2 * j + 1 in range(*g_) for g_ in GROUPS3].index(True)
                                reached(act, N["pv_done"], (p + dp) * NG + (3 + group + 1 - NG))
                                nc.scalar.activation(v3[:, 0, 2 * j:2 * j + 2], vf[:, j % 2], ACT.Copy).then_inc(N["v_high"], 1)
                            elif what == "S":
                                g_ = 3 * h + j
                                act.wait_ge(N["nm_ready"], p * NG + (g_ + 1))
                                reached(act, N["T_full"], p * NG + (g_ - EXPS + 1))
                                reached(act, N["r_ready"], p * NG + (g_ - EXPS + 1))
                                for b in range(GROUPS3[j][1] - GROUPS3[j][0]):
                                    last = nc.scalar.activation(E3[:, g_ % EXPS, b, 0:P + 1], Sb[g_ % 2][:, b * T3:b * T3 + P + 1], ACT.Exp,
                                                                scale=SCALE3, bias=nm3[:, g_ % EXPS, b:b + 1],
                                                                accum_out=sum3[:, g_ % EXPS, b:b + 1])
                                last.then_inc(N["exp_done"], 1)
                            elif what == "T":
                                g_ = 3 * h + j
                                w = (GROUPS3[j][1] - GROUPS3[j][0]) * P
                                act.wait_ge(N["T_full"], (p + dp) * NG + (g_ + 1))
                                reached(act, N["pv_done"], (p + dp) * NG + (g_ - 1))
                                nc.scalar.activation(PT3[:, g_ % 2, 0, 0:w], Tb[g_ % 2][:, 0:w], ACT.Copy).then_inc(N["T_act"], 1)
                            elif what == "PV" and j >= 1:
                                act.wait_ge(N["pv_done"], (p + dp) * NG + (3 * h + j + 1))
                                if (h, j) == (0, 1) and not (isinstance(p, int) and p == 0):
                                    act.wait_ge(N["A_full"], fill3(p, ("out", -1, 0, NB - 1))[1] + 1)
                                act.sem_inc(N["act_apart"], 1)
                                nc.scalar.activation(ctxT3[:, 0, h, (j - 1) * TOK:j * TOK], Ob[j - 1][:, :], ACT.Identity,
                                                     bias=const(3, p + dp, h)).then_inc(N["ctx_high"], 1)
                    passes(act, do)

                @block.vector
                def _(dve):
                    def do(p):
                        pending = []

                        def settle(keep=0):
                            while len(pending) > keep:
                                g_, nb = pending.pop(0)
                                dve.wait_ge(N["exp_done"], p * NG + (g_ + 1))
                                reached(dve, N["P_ready"], p * NG + (g_ - EXPS + 1))
                                nc.vector.reciprocal(rs3[:, g_ % EXPS, 0:nb], sum3[:, g_ % EXPS, 0:nb]).then_inc(N["r_ready"], 1)

                        for step in steps_of(p):
                            what, dp, h, j = step
                            if what == "P":
                                settle()
                            elif what == "W":
                                dve.wait_ge(N["w_high"], p * 3 + (3 + h + 1))
                                nc.vector.tensor_tensor(w3[h][:, 1], wst[h][:, :, :], w3[h][:, 0].bitcast(F32), ALU.subtract).then_inc(N["w_low"], 1)
                            elif what in ("q", "k"):
                                bank, n = fill3(p, step)
                                dve.wait_ge(N["A_act"], high3(p, step))
                                c = const(0 if what == "q" else 1, p + dp, h)
                                if what == "q":
                                    high, low, full = (qT3[:, h, 0, j * TOK:(j + 1) * TOK], qT3[:, h, 1, j * TOK:(j + 1) * TOK], Ab[bank][:, :])
                                else:
                                    high, low = kT3[:, h, 0, j * NB:(j + 1) * NB, 0:P], kT3[:, h, 1, j * NB:(j + 1) * NB, 0:P]
                                    full = Ab[bank][:, :].rearrange("p (b t) -> p b t", b=NB)
                                nc.vector.scalar_tensor_tensor(out=low, in0=full, scalar=c, in1=high.bitcast(F32), op0=ALU.add,
                                                               op1=ALU.subtract).then_inc(N["A_dve"], 1)
                                if what == "k" and j == 1:
                                    key = const(2, p + dp, h).broadcast_to([P, B])
                                    nc.vector.tensor_copy(kT3[:, h, 0, :, P], key).then_inc(N["bias_high"], 1)
                                    dve.wait_ge(N["bias_high"], (p + dp) * HG3 + (h + 1))
                                    nc.vector.tensor_tensor(kT3[:, h, 1, :, P], key, kT3[:, h, 0, :, P].bitcast(F32),
                                                            ALU.subtract).then_inc(N["bias_low"], 1)
                            elif what == "v":
                                bank, n = fill3(p, step)
                                dve.wait_ge(N["A_full"], n + 1)
                                if j == 0:
                                    dve.wait_ge(N["v_row_ready"], p + (dp + 1))
                                reached(dve, N["v_low"], (p + dp) * NV + (j - 1))
                                nc.vector.tensor_tensor(vf[:, j % 2], Ab[bank][:, :].rearrange("p (b n) -> p b n", b=2),
                                                        v_row[:, None, :].broadcast_to([P, 2, HG3 * P]), ALU.add).then_inc(N["A_dve"], 1)
                            elif what == "S":
                                g_ = 3 * h + j
                                nb = GROUPS3[j][1] - GROUPS3[j][0]
                                dve.wait_ge(N["S_full"], p * NG + (g_ + 1))
                                bank = Sb[g_ % 2][:, 0:nb * T3].rearrange("p (b t) -> p b t", b=nb)[:, :, 0:P + 1]
                                nc.vector.tensor_reduce(mx3[:, g_ % EXPS, 0:nb], bank, AX_X, ALU.max).then_inc(N["max_ready"], 1)
                                dve.wait_ge(N["max_ready"], p * NG + (g_ + 1))
                                nc.vector.tensor_scalar(nm3[:, g_ % EXPS, 0:nb], mx3[:, g_ % EXPS, 0:nb], -SCALE3, None,
                                                        ALU.mult).then_inc(N["nm_ready"], 1)
                                pending.append((g_, nb))
                            elif what == "T":
                                g_ = 3 * h + j
                                w = (GROUPS3[j][1] - GROUPS3[j][0]) * P
                                dve.wait_ge(N["T_act"], (p + dp) * NG + (g_ + 1))
                                nc.vector.tensor_tensor(PT3[:, g_ % 2, 1, 0:w], Tb[g_ % 2][:, 0:w], PT3[:, g_ % 2, 0, 0:w].bitcast(F32),
                                                        ALU.subtract).then_inc(N["T_dve"], 1)
                            elif what == "PV" and j >= 1:
                                dve.wait_ge(N["ctx_high"], (p + dp) * NC + (2 * h + j))
                                nc.vector.scalar_tensor_tensor(
                                    out=ctxT3[:, 1, h, (j - 1) * TOK:j * TOK], in0=Ob[j - 1][:, :], scalar=const(3, p + dp, h),
                                    in1=ctxT3[:, 0, h, (j - 1) * TOK:j * TOK].bitcast(F32), op0=ALU.add,
                                    op1=ALU.subtract).then_inc(N["ctx_low"], 1)
                            elif what == "out":
                                bank, n = fill3(p, step)
                                dve.wait_ge(N["A_full"], n + 1)
                                nc.vector.tensor_tensor(x_all[:, 2 * j:2 * j + 2], Ab[bank][:, :].rearrange("p (b d) -> p b d", b=2),
                                                        x_all[:, 2 * j:2 * j + 2], ALU.add).then_inc(N["A_dve"], 1)
                        settle()
                    passes(dve, do)

                @block.tensor
                def _(pe):
                    def do(p):
                        for step in steps_of(p):
                            what, dp, h, j = step
                            if what in ("q", "k", "v", "out"):
                                bank, n = fill3(p, step)
                                reached(pe, N["A_dve"], n - 1)
                            if what in ("q", "k"):
                                w = 0 if what == "q" else 1
                                if dp == 1 and j == 0:
                                    pe.wait_ge(N["w_low"], p * 3 + (3 + w + 1))
                                src = hT3 if what == "q" else cT3
                                for kt in range(KT):
                                    last = products(pe, Ab[bank][:, :], pair(w3[w], kt, slice(h * P, (h + 1) * P)),
                                                    pair(src, kt, slice(j * TOK, (j + 1) * TOK)), kt == 0, kt == KT - 1)
                                last.then_inc(N["A_full"], 1)
                            elif what == "v":
                                if dp == 1 and j == 0:
                                    pe.wait_ge(N["w_low"], p * 3 + (3 + 3))
                                for e in range(2):
                                    b = 2 * j + e
                                    for kt in range(KT):
                                        last = products(pe, Ab[bank][:, e * HG3 * P:(e + 1) * HG3 * P],
                                                        pair(cT3, kt, slice(b * P, (b + 1) * P)), pair(w3[2], kt), kt == 0, kt == KT - 1)
                                last.then_inc(N["A_full"], 1)
                            elif what == "S":
                                g_ = 3 * h + j
                                reached(pe, N["exp_done"], p * NG + (g_ - 1))
                                if j == 0:
                                    if h == 1:
                                        pe.wait_ge(N["A_dve"], fill3(p, ("k", 0, 1, 1))[1] + 1)
                                    else:
                                        before = [w for w in PASS if w[1] == 1 and w[0] in "qkv"]
                                        after_k = len(before) - before.index(("k", 1, 0, 1)) - 1
                                        pe.wait_ge(N["A_dve"], (AHEAD if isinstance(p, int) and p == 0 else p * NF + (AHEAD - OUTS)) - after_k)
                                    pe.wait_ge(N["bias_low"], p * HG3 + (h + 1))
                                for b in range(*GROUPS3[j]):
                                    e = b - GROUPS3[j][0]
                                    last = products(pe, Sb[g_ % 2][:, e * T3:(e + 1) * T3],
                                                    (qT3[:, h, 0, b * P:(b + 1) * P], qT3[:, h, 1, b * P:(b + 1) * P]),
                                                    (kT3[:, h, 0, b], kT3[:, h, 1, b]), True, True)
                                last.then_inc(N["S_full"], 1)
                            elif what == "T":
                                g_ = 3 * h + j
                                reached(pe, N["T_dve"], (p + dp) * NG + (g_ - 1))
                                pe.wait_ge(N["P_ready"], (p + dp) * NG + (g_ + 1))
                                for e in range(GROUPS3[j][1] - GROUPS3[j][0]):
                                    last = nc.tensor.transpose(Tb[g_ % 2][:, e * P:(e + 1) * P], E3[:, g_ % EXPS, e, 0:P], ident[:, :])
                                last.then_inc(N["T_full"], 1)
                            elif what == "PV":
                                g_ = 3 * h + j
                                pe.wait_ge(N["T_dve"], (p + dp) * NG + (g_ + 1))
                                if h == 0:
                                    pe.wait_ge(N["v_low"], (p + dp) * NV + (j + 2))
                                if j < 2:
                                    reached(pe, N["ctx_low"], (p + dp) * NC + (2 * h + j - 1))
                                for b in range(*GROUPS3[j]):
                                    e = b - GROUPS3[j][0]
                                    last = products(pe, Ob[b // NB][:, (b % NB) * P:(b % NB + 1) * P],
                                                    (v3[:, 0, b, h * P:(h + 1) * P], v3[:, 1, b, h * P:(h + 1) * P]),
                                                    (PT3[:, g_ % 2, 0, e * P:(e + 1) * P], PT3[:, g_ % 2, 1, e * P:(e + 1) * P]), True, True)
                                last.then_inc(N["pv_done"], 1)
                            elif what == "out":
                                if j == 0:
                                    pe.wait_ge(N["wo_low"], p * 1)
                                pe.wait_ge(N["ctx_low"], p * NC + (j // 2 - 1))
                                for e in range(2):
                                    b = 2 * j + e
                                    for hh in range(HG3):
                                        last = products(pe, Ab[bank][:, e * D:(e + 1) * D], pair(ctxT3, hh, slice(b * P, (b + 1) * P)),
                                                        pair(wo3, hh), hh == 0, hh == HG3 - 1)
                                last.then_inc(N["A_full"], 1)
                    passes(pe, do)

            for each in N.values():
                nc.sync.sem_clear(each)
            nc.all_engine_barrier()

        rows_in = ctx.enter_context(nc.semaphore("rows_in"))
        fc_in, pj_in, split3 = (ctx.enter_context(nc.semaphore(n)) for n in ("fc_in", "pj_in", "split3"))
        with nc.Block() as block:
            @block.scalar
            def _(act):
                for i, name in enumerate(ROWS3):
                    act.dma_start(rows[:, i, :], a[name][None, :].broadcast_to([P, D])).then_inc(rows_in, 16)
                act.wait_ge(rows_in, 16 * len(ROWS3))

            @block.gpsimd
            def _(pool):
                nc.gpsimd.memset(kT3[:, :, :, :, P + 1:T3].bitcast(F32), 0.0)
        attention3(0)
        attention3(1)

        s4 = ExitStack()
        xh, z, aT, g, gT = mlp_memory(s4, "_last")
        s4.close()
        S["x_copied"], S["stored"] = sem("x_copied"), sem("stored")
        used = [S[n] for n in ("T_full", "T_act", "T_dve", "A_full", "A_act", "A_dve", "O_read", "g_high", "g_low", "g_used", "vstep",
                               "var_ready", "rstd_ready", "norm_ready", "pool_step", "x_biased", "x_copied", "stored")]
        with nc.Fori(0, HALVES) as half:
            with nc.Block() as block:
                @block.vector
                def _(dve):
                    steps[0] = norms[0] = 0
                    nc.vector.tensor_copy(xh[:, :, :], x_all[:, bass.ds(half * NB, NB), :]).then_inc(S["x_copied"], 1)
                    dve.wait_ge(S["x_copied"], 1)
                    norm(dve, lambda b: xh[:, b], z, NB, row("L3_xattn_ln_mlp_scale"))
                    for b in range(NB):
                        nc.vector.scalar_tensor_tensor(out=z[:, b], in0=z[:, b], scalar=rstd[:, b:b + 1], in1=row("L3_xattn_ln_mlp_offset"),
                                                       op0=ALU.mult, op1=ALU.add).then_inc(S["norm_ready"], 1)
                    split_low(dve, aT, 0)
                    mlp_dve(dve)
                    dve.wait_ge(S["x_biased"], 1)
                    mlp_add(dve, 0)

                @block.gpsimd
                def _(pool):
                    psteps[0] = 0
                    power(pool, 1, NB, LN_EPS)
                    pool.wait_ge(S["norm_ready"], NB)
                    nc.gpsimd.tensor_tensor(xh[:, :, :], xh[:, :, :], row("L3_xattn_b_fc2")[:, None, :].broadcast_to([P, NB, D]),
                                            ALU.add).then_inc(S["x_biased"], 1)

                @block.scalar
                def _(act):
                    split_high(act, aT, 0)
                    mlp_act(act, MLP_A, 0, ACT.Gelu, "L3_xattn_b_fc1")

                @block.tensor
                def _(pe):
                    pe.wait_ge(S["norm_ready"], NB)
                    turn(pe, z, MLP_T, 0)
                    pe.wait_ge(S["T_act"], KT)
                    pe.wait_ge(S["T_dve"], KT)
                    mlp_pe(pe, MLP_A, 0, 0)

                @block.sync
                def _(sp):
                    sp.wait_ge(S["O_read"], 2)
                    sp.dma_start(out[bass.ds(half * NB, NB)].rearrange("b t d -> t b d"), xh[:, :, :]).then_inc(S["stored"], 16)
                    sp.wait_ge(S["stored"], 16)
            for each in used:
                nc.sync.sem_clear(each)
            nc.all_engine_barrier()


_OUTS = [((B, P, D), "float32")]


def kernel(**inputs):
    import numpy as _np
    import concourse.bacc as _bacc
    from concourse import mybir as _mybir
    from concourse.bass_utils import run_bass_kernel_spmd as _run

    nc = _bacc.Bacc("TRN2", target_bir_lowering=False, num_devices=1)
    arrays, args = {}, {}
    for name, value in inputs.items():
        v = _np.ascontiguousarray(value).reshape(_np.shape(value) or (1,))
        arrays[f"in_{name}_dram"] = v
        args[name] = nc.dram_tensor(f"in_{name}_dram", v.shape, _mybir.dt.from_np(v.dtype), kind="ExternalInput").ap()
    out = nc.dram_tensor("out_0_dram", _OUTS[0][0], F32, kind="ExternalOutput").ap()
    network(nc, args, out)
    r = _run(nc, [arrays], core_ids=[0])
    return r.results[0]["out_0_dram"]
```

```python
import concourse.bass as bass
from concourse import mybir
from contextlib import ExitStack

F32 = mybir.dt.float32
R32 = mybir.dt.float32r
U8 = mybir.dt.uint8
ALU = mybir.AluOpType
ACT = mybir.ActivationFunctionType
AX_X = mybir.AxisListType.X

P = 128
D = 256
KT = D // P
NB = 4
HALVES = 2
B = NB * HALVES
TOK = NB * P
INNER = 4 * D
MT = INNER // P
LN_EPS, LN2_EPS = 1e-5, 1e-6
BIG = 2.0 ** 127
EXPS = 3
VW = 32
TWO_BANKS = 2

H3 = 16
HG3 = 2
T3 = P + 2
GROUPS3 = [(0, 3), (3, 6), (6, 8)]

STACK_A = [("L1_xattn_q_b", 2), ("L1_xattn_k_b", 2), ("L1_xattn_fc_b", 8), ("L2_xattn_bq", 2),
           ("L2_xattn_bk", 2), ("L3_xattn_b_fc1", 8),
           ("L3_xattn_bq1", H3), ("L3_xattn_bk1", H3), ("L3_xattn_bias_k1", H3), ("L3_xattn_bias_v1", H3)]
STACK_B = [("L3_xattn_bq2", H3), ("L3_xattn_bk2", H3), ("L3_xattn_bias_k2", H3), ("L3_xattn_bias_v2", H3)]
ROWS = ["L1_xattn_ln1_w", "L1_xattn_ln1_b", "L1_xattn_v_b", "L1_xattn_cproj_b", "L1_xattn_ln2_w",
        "L1_xattn_ln2_b", "L1_xattn_proj_b", "L2_xattn_bo", "L2_xattn_gamma", "L2_xattn_beta"]
ROWS3 = ["L3_xattn_ln1_scale", "L3_xattn_ln1_offset", "L3_xattn_bo1",
        "L3_xattn_ln2_scale", "L3_xattn_ln2_offset", "L3_xattn_bo2",
        "L3_xattn_ln_mlp_scale", "L3_xattn_ln_mlp_offset", "L3_xattn_b_fc2"]


def place(stack):
    at, n = {}, 0
    for name, rows in stack:
        at[name] = n
        n += rows
    return at, n


T_FILLS = ([("c", 1)] * KT + [("x", 1)] * KT + [("p0", 0)] + [("z1", 1)] * KT + [("p1", 0)] * 16
           + [("ctx1", 1)] * KT + [("z2", 1)] * KT + [("x2", 1)] * KT + [("p2", 0)] * 32 + [("ctx2", 1)] * KT)
A_FILLS = ([("q0", "AV")] * 2 + [("v0", "V")] * 2 + [("k1", "AV")] * 2 + [("v1", "V")] * 2
           + [("q1", "AV")] * 2 + [("ctx1", "V")] * 4 + [("o1", "V")] * 2 + [("k2", "AV")] * 2 + [("v2", "V")]
           + [("fc", "A")] * MT + [("q2", "AV")] * 2 + [("ctx2", "V")] * 8 + [("o2", "V")] * 2)
O_FILLS = ["pv0"] * NB + ["pv1"] * 4 + ["mlp"] * 2 + ["pv2"] * 8
S_FILLS = ["s0"] + ["s1"] * 16 + ["s2"] * 32
MLP_T = [("z", 1)] * 2 * KT


def first(fills, what):
    return [f[0] if isinstance(f, tuple) else f for f in fills].index(what)


def splits_in(fills, n):
    return sum(f[1] for f in fills[:n])


def read_by(fills, n, engine):
    return sum(engine in f[1] for f in fills[:n])


def products(pe, out, left, right, begin, end):
    (lh, ll), (rh, rl) = left, right
    pe.matmul(out, lh, rh, start=begin, stop=False)
    pe.matmul(out, ll, rh, start=False, stop=False)
    return pe.matmul(out, lh, rl, start=False, stop=end)


def network(nc, a, out):
    ctx = ExitStack()
    with ctx:
        def sb(name, shape, dt=F32, where=ctx):
            return where.enter_context(nc.sbuf_tensor(name, shape, dt))

        banks = [ctx.enter_context(nc.psum_tensor(f"bank{i}", [P, 512], F32)) for i in range(8)]
        Sb, Tb, Ab, Ob = banks[0:2], banks[2:4], banks[4:6], banks[6:8]

        atA, nA = place(STACK_A)
        atB, nB = place(STACK_B)
        x_all = sb("x_all", [P, B, D])
        ident = sb("ident", [P, P])
        colsA = sb("colsA", [P, nA])
        colsB = sb("colsB", [P, nB])
        rows = sb("rows", [P, len(ROWS), D])
        stats = sb("stats", [P, B, 6])
        mv = sb("mv", [P, B, 2])
        rstd = sb("rstd", [P, B])
        var = sb("var", [P, B])
        neg_half = sb("neg_half", [P, B])

        def row(name):
            return rows[:, (ROWS if name in ROWS else ROWS3).index(name), :]

        def col(name, i):
            return colsA[:, atA[name] + i:atA[name] + i + 1]

        def pair(t, *idx):
            return t[(slice(None), 0) + idx], t[(slice(None), 1) + idx]

        fcw = sb("fcw", [P, 2, KT, INNER], R32)
        pjw = sb("pjw", [P, 2, MT, D], R32)

        s1 = ExitStack()
        xh = sb("xh", [P, NB, D], F32, s1)
        z = sb("z", [P, NB, D], F32, s1)
        aT = sb("aT", [P, 2, KT, TOK], R32, s1)
        g = sb("g", [P, 2, TOK], F32, s1)
        gT = sb("gT", [P, 2, 2, TOK], R32, s1)
        m0w = sb("m0w", [P, 2, KT, D], R32, s1)
        v0w = sb("v0w", [P, 2, KT, D], R32, s1)
        w1 = [sb(f"w1_{n}", [P, 2, KT, D], R32, s1) for n in "qkvo"]
        w2 = [sb(f"w2_{n}", [P, 2, KT, D], R32, s1) for n in "qko"]
        w2v = sb("w2v", [P, 2, KT, 64], R32, s1)
        hmask1 = sb("hmask1", [P, 8], F32, s1)
        hmask2 = sb("hmask2", [P, 16], F32, s1)
        bv2 = sb("bv2", [P, 64], F32, s1)
        alpha = sb("alpha", [P, 1], F32, s1)
        v0 = sb("v0", [P, NB, D + 1], F32, s1)
        v1 = sb("v1", [P, NB, 16, VW], F32, s1)
        v2 = sb("v2", [P, NB, 8, VW], F32, s1)

        mask1b = sb("mask1b", [P, NB, P], U8, s1)
        masks = {1: sb("mask1", [P, NB, P], F32, s1), 2: sb("mask2", [P, NB, P], F32, s1)}

        s0 = ExitStack()
        stage = [sb(f"stage{i}", [P, KT, D], F32, s0) for i in range(4)]
        stage1 = [sb(f"stage1_{i}", [P, KT, D], F32, s0) for i in range(7)]
        stage_v = sb("stage_v", [P, KT, 64], F32, s0)
        w0 = [sb(f"w0_{n}", [P, 2, KT, D], R32, s0) for n in "qkvo"]
        stackA = sb("stackA", [P, P], F32, s0)
        stackB = sb("stackB", [P, P], F32, s0)
        stage_fc = sb("stage_fc", [P, KT, INNER], F32, s0)
        stage_pj = sb("stage_pj", [P, MT, D], F32, s0)
        s0.close()

        def load_ctx(sp, at):
            sp.dma_start(z[:, :, :], a["ctx_2048"][at].rearrange("b t d -> t b d")).then_inc(inputs_loaded, 16)

        def load_masks(sp, at):
            sp.dma_start(mask1b[:, :, :], a["mask_BxS2_bf1"][at][None].broadcast_to([P, NB, P])).then_inc(inputs_loaded, 16)
            sp.dma_start(masks[2][:, :, :], a["mask_Bx1xSxS2_ff0"][at].rearrange("b o q t -> q (b o) t")).then_inc(inputs_loaded, 16)

        def load_x(sp, at):
            sp.dma_start(xh[:, :, :], a["x"][at].rearrange("b t d -> t b d")).then_inc(inputs_loaded, 16)

        names0 = ["L0_xattn_w_q", "L0_xattn_w_k", "L0_xattn_w_v", "L0_xattn_w_o"]
        names1 = ["L1_xattn_q_w", "L1_xattn_k_w", "L1_xattn_v_w", "L1_xattn_cproj_w",
                  "L2_xattn_Wq", None, "L2_xattn_Wo"]

        sem = lambda n: ctx.enter_context(nc.semaphore(n))
        inputs_loaded = sem("inputs_loaded")
        loaded = [sem(f"w0_loaded{i}") for i in range(4)]
        loaded1 = [sem(f"w1_loaded{i}") for i in range(7)]
        wk2_loaded, wv2_loaded = sem("wk2_loaded"), sem("wv2_loaded")
        fc_loaded, pj_loaded = sem("fc_loaded"), sem("pj_loaded")
        stacked, rows_loaded = sem("stacked"), sem("rows_loaded")
        consts, dve_step, act_step = sem("consts"), sem("dve_step"), sem("act_step")
        high0, low0 = sem("high0"), sem("low0")
        wo_turned, wo_high, wo_low = sem("wo_turned"), sem("wo_high"), sem("wo_low")
        m_full, m_high = sem("m_full"), sem("m_high")
        cols_turned = sem("cols_turned")
        scaled2, high1 = sem("scaled2"), sem("high1")
        cleared = sem("cleared")
        with nc.Block() as block:
            @block.sync
            def _(sp):
                for n in range(4):
                    sp.dma_start(stage[n][:, :, :], a[names0[n]].rearrange("(k p) n -> p k n", p=P)).then_inc(loaded[n], 16)
                for n in range(7):
                    if n == 5:
                        for k in range(KT):
                            for q in range(4):
                                sp.dma_start(stage1[5][:, k, :].rearrange("p (h g d) -> p h g d", h=8, g=4)[:, :, q, :],
                                             a["L2_xattn_Wk"][k * P:(k + 1) * P, :].rearrange("p (h d) -> p h d", d=8)
                                             ).then_inc(wk2_loaded, 16)
                        continue
                    sp.dma_start(stage1[n][:, :, :], a[names1[n]].rearrange("(k p) n -> p k n", p=P)).then_inc(loaded1[n], 16)
                load_ctx(sp, slice(0, NB))
                load_masks(sp, slice(0, NB))
                load_x(sp, slice(0, NB))
                sp.dma_start(stage_v[:, :, :], a["L2_xattn_Wv"].rearrange("(k p) n -> p k n", p=P)).then_inc(wv2_loaded, 16)
                sp.dma_start(stage_fc[:, :, :], a["L1_xattn_fc_w"].rearrange("(k p) n -> p k n", p=P)).then_inc(fc_loaded, 16)
                sp.dma_start(stage_pj[:, :, :], a["L1_xattn_proj_w"].rearrange("(m p) n -> p m n", p=P)).then_inc(pj_loaded, 16)
                sp.wait_ge(rows_loaded, 16 * (len(ROWS) + 2))
                sp.wait_ge(inputs_loaded, 4 * 16)

            @block.scalar
            def _(act):
                for stack, at, tile in ((STACK_A, atA, stackA), (STACK_B, atB, stackB)):
                    for name, n in stack:
                        if name == "L2_xattn_bk":
                            src = a[name].rearrange("(r h d) -> r h d", r=2, d=8)
                            for q in range(4):
                                act.dma_start(tile[at[name]:at[name] + 2, :].rearrange("r (h g d) -> r h g d", g=4, d=8)[:, :, q, :],
                                              src).then_inc(stacked, 16)
                        else:
                            v = a[name]
                            if len(v.shape) == 4:
                                v = v.rearrange("a b h k -> (a b h k)")
                            act.dma_start(tile[at[name]:at[name] + n, :], v.rearrange("(r p) -> r p", p=P)).then_inc(stacked, 16)
                for i, name in enumerate(ROWS):
                    act.dma_start(rows[:, i, :], a[name][None, :].broadcast_to([P, D])).then_inc(rows_loaded, 16)
                act.dma_start(bv2[:, :], a["L2_xattn_bv"][None, :].broadcast_to([P, 64])).then_inc(rows_loaded, 16)
                act.dma_start(alpha[:, :], a["L0_xattn_alpha"][None, :].broadcast_to([P, 1])).then_inc(rows_loaded, 16)
                for n in range(3):
                    act.wait_ge(loaded[n], 16)
                    nc.scalar.activation(w0[n][:, 0], stage[n][:, :, :], ACT.Copy).then_inc(high0, 1)
                act.wait_ge(wo_turned, 1)
                nc.scalar.activation(w0[3][:, 0], Ab[0][:, :].rearrange("p (k n) -> p k n", k=KT), ACT.Copy).then_inc(wo_high, 1)
                for n, (full, dst) in enumerate(((Sb[0], m0w), (Sb[1], v0w))):
                    act.wait_ge(m_full, n + 1)
                    nc.scalar.activation(dst[:, 0], full[:, :].rearrange("p (k n) -> p k n", k=KT), ACT.Copy).then_inc(m_high, 1)
                for n in range(7):
                    if n == 5:
                        act.wait_ge(wk2_loaded, 16 * 4 * KT)
                    else:
                        act.wait_ge(loaded1[n], 16)
                    if n == 4:
                        act.wait_ge(scaled2, 1)
                    nc.scalar.activation((w1 + w2)[n][:, 0], stage1[n][:, :, :], ACT.Copy).then_inc(high1, 1)
                act.wait_ge(wv2_loaded, 16)
                nc.scalar.activation(w2v[:, 0], stage_v[:, :, :], ACT.Copy).then_inc(high1, 1)
                act.wait_ge(fc_loaded, 16)
                nc.scalar.activation(fcw[:, 0], stage_fc[:, :, :], ACT.Copy).then_inc(high1, 1)
                act.wait_ge(pj_loaded, 16)
                nc.scalar.activation(pjw[:, 0], stage_pj[:, :, :], ACT.Copy).then_inc(high1, 1)

            @block.gpsimd
            def _(pool):
                nc.gpsimd.memset(ident[:, :], 0.0).then_inc(cleared, 1)
                nc.gpsimd.memset(neg_half[:, :], -0.5)
                pool.wait_ge(cleared, 1)
                nc.gpsimd.affine_select(out=ident[:, :], in_=ident[:, :], compare_op=ALU.not_equal, fill=1.0,
                                        base=0, pattern=[[-1, P]], channel_multiplier=1).then_inc(consts, 1)
                nc.gpsimd.memset(v0[:, :, D:D + 1], 1.0)
                nc.gpsimd.memset(v1[:, :, :, 16:17], 1.0)
                nc.gpsimd.memset(v1[:, :, :, 17:VW], 0.0)
                nc.gpsimd.memset(v2[:, :, :, 8:9], 1.0)
                nc.gpsimd.memset(v2[:, :, :, 9:VW], 0.0)

            @block.vector
            def _(dve):
                dve.wait_ge(consts, 1)
                nc.vector.tensor_reduce(hmask1[:, :], ident[:, :].rearrange("p (h d) -> p h d", d=16), AX_X, ALU.add)
                nc.vector.tensor_reduce(hmask2[:, :], ident[:, :].rearrange("p (h d) -> p h d", d=8), AX_X, ALU.add)
                for n in range(3):
                    dve.wait_ge(high0, n + 1)
                    nc.vector.tensor_tensor(w0[n][:, 1], stage[n][:, :, :], w0[n][:, 0].bitcast(F32), ALU.subtract).then_inc(low0, 1)
                dve.wait_ge(wo_high, 1)
                nc.vector.tensor_tensor(w0[3][:, 1], Ab[0][:, :].rearrange("p (k n) -> p k n", k=KT),
                                        w0[3][:, 0].bitcast(F32), ALU.subtract).then_inc(wo_low, 1)
                for n, (full, dst) in enumerate(((Sb[0], m0w), (Sb[1], v0w))):
                    dve.wait_ge(m_high, n + 1)
                    nc.vector.tensor_tensor(dst[:, 1], full[:, :].rearrange("p (k n) -> p k n", k=KT),
                                            dst[:, 0].bitcast(F32), ALU.subtract)
                dve.wait_ge(cols_turned, 1)
                nc.vector.tensor_copy(colsA[:, :], Tb[0][:, 0:nA]).then_inc(dve_step, 1)
                dve.wait_ge(cols_turned, 2)
                nc.vector.tensor_copy(colsB[:, :], Tb[1][:, 0:nB])
                dve.wait_ge(dve_step, 1)
                nc.vector.tensor_scalar(colsA[:, atA["L2_xattn_bq"]:atA["L2_xattn_bq"] + 2],
                                        colsA[:, atA["L2_xattn_bq"]:atA["L2_xattn_bq"] + 2], 8 ** -0.5, None, ALU.mult)
                dve.wait_ge(loaded1[4], 16)
                nc.vector.tensor_scalar(stage1[4][:, :, :], stage1[4][:, :, :], 8 ** -0.5, None, ALU.mult).then_inc(scaled2, 1)
                dsts = [t for t in w1 + w2] + [w2v, fcw, pjw]
                srcs = stage1 + [stage_v, stage_fc, stage_pj]
                for n, (s, d) in enumerate(zip(srcs, dsts)):
                    dve.wait_ge(high1, n + 1)
                    nc.vector.tensor_tensor(d[:, 1], s[:, :, :], d[:, 0].bitcast(F32), ALU.subtract)

            @block.tensor
            def _(pe):
                pe.wait_ge(consts, 1)
                pe.wait_ge(loaded[3], 16)
                for kt in range(KT):
                    for mt in range(KT):
                        last = nc.tensor.transpose(Ab[0][:, kt * D + mt * P:kt * D + (mt + 1) * P],
                                                   stage[3][:, mt, kt * P:(kt + 1) * P], ident[:, :])
                last.then_inc(wo_turned, 1)
                pe.wait_ge(high0, 3)
                pe.wait_ge(low0, 3)
                for mt in range(KT):
                    for kt in range(KT):
                        last = products(pe, Sb[0][:, mt * D:(mt + 1) * D], pair(w0[0], kt, slice(mt * P, (mt + 1) * P)),
                                        pair(w0[1], kt), kt == 0, kt == KT - 1)
                last.then_inc(m_full, 1)
                pe.wait_ge(wo_high, 1)
                pe.wait_ge(wo_low, 1)
                for mt in range(KT):
                    for kt in range(KT):
                        last = products(pe, Sb[1][:, mt * D:(mt + 1) * D], pair(w0[2], kt, slice(mt * P, (mt + 1) * P)),
                                        pair(w0[3], kt), kt == 0, kt == KT - 1)
                last.then_inc(m_full, 1)
                pe.wait_ge(stacked, 16 * (len(STACK_A) + 3 + len(STACK_B)))
                nc.tensor.transpose(Tb[0][:, 0:nA], stackA[0:nA, :], ident[0:nA, 0:nA]).then_inc(cols_turned, 1)
                nc.tensor.transpose(Tb[1][:, 0:nB], stackB[0:nB, :], ident[0:nB, 0:nB]).then_inc(cols_turned, 1)

        cT = sb("cT", [P, 2, KT, TOK], R32, s1)
        qT = sb("qT", [P, 2, KT, TOK], R32, s1)
        kT = sb("kT", [P, 2, KT, TOK], R32, s1)
        km = sb("km", [P, 2, 2, 4, TOK], R32, s1)
        E = sb("E", [P, EXPS, 4, P], F32, s1)
        PT = sb("PT", [P, 2, 4, P], F32, s1)
        o = sb("o", [P, NB, D], F32, s1)
        nm = sb("nm", [P, EXPS, 4], F32, s1)
        mx = sb("mx", [P, EXPS, 4], F32, s1)
        r0 = sb("r0", [P, NB], F32, s1)
        r1 = sb("r1", [P, NB, 4], F32, s1)
        sums = g
        s1.close()

        sem = lambda n: ctx.enter_context(nc.semaphore(n))
        S = {n: sem(n) for n in (
            "c_loaded", "T_full", "A_full", "S_full", "O_full",
            "T_act", "T_dve", "A_act", "A_dve", "S_read", "nm_ready", "O_read", "P_ready", "pv_done",
            "km_high", "km_low", "norm_ready", "var_ready", "rstd_ready", "x_biased", "g_high",
            "g_low", "g_used", "mask1_ready", "vstep", "x_out")}

        LAYERS = {1: dict(hd=16, hg=4, scale=0.25, v=v1, mask=masks[1], hmask=hmask1, kbias="L1_xattn_k_b"),
                  2: dict(hd=8, hg=8, scale=1.0, v=v2, mask=masks[2], hmask=hmask2, kbias="L2_xattn_bk")}
        for n, L in LAYERS.items():
            L["S"], L["T"], L["O"] = first(S_FILLS, f"s{n}"), first(T_FILLS, f"p{n}"), first(O_FILLS, f"pv{n}")
            L["km"] = 0 if n == 1 else 4
            L["G"] = L["hg"] * NB
            L["ctx"] = first(A_FILLS, f"ctx{n}")
            L["kfill"], L["qfill"] = first(A_FILLS, f"k{n}"), first(A_FILLS, f"q{n}")
            L["heads_kt"] = P // L["hd"]

        def T_free(pe, fills, n):
            if n >= 2:
                pe.wait_ge(S["T_act"], n - 1)
                if splits_in(fills, n - 1):
                    pe.wait_ge(S["T_dve"], splits_in(fills, n - 1))

        def A_free(pe, fills, n):
            if n >= 2:
                for s, e in (("A_act", "A"), ("A_dve", "V")):
                    if read_by(fills, n - 1, e):
                        pe.wait_ge(S[s], read_by(fills, n - 1, e))

        def turn(pe, src, fills, n, norms_before=None):
            for kt in range(KT):
                T_free(pe, fills, n + kt)
                for b in range(NB):
                    if kt == 0 and norms_before is not None:
                        pe.wait_ge(S["norm_ready"], norms_before * NB + b + 1)
                    last = nc.tensor.transpose(Tb[(n + kt) % 2][:, b * P:(b + 1) * P], src[:, b, kt * P:(kt + 1) * P], ident[:, :])
                last.then_inc(S["T_full"], 1)

        def split_high(act, dst, n):
            for kt in range(KT):
                act.wait_ge(S["T_full"], n + kt + 1)
                nc.scalar.activation(dst[:, 0, kt, :], Tb[(n + kt) % 2][:, :], ACT.Copy).then_inc(S["T_act"], 1)

        def split_low(dve, dst, n):
            for kt in range(KT):
                dve.wait_ge(S["T_act"], n + kt + 1)
                nc.vector.tensor_tensor(dst[:, 1, kt, :], Tb[(n + kt) % 2][:, :], dst[:, 0, kt, :].bitcast(F32),
                                        ALU.subtract).then_inc(S["T_dve"], 1)

        def a_free(eng, what, fills):
            eng.wait_ge(S["A_full"], fA[what] + fills)

        def project_T(pe, w, src, fills, n, turned=None):
            for mt in range(KT):
                A_free(pe, fills, n + mt)
                for kt in range(KT):
                    if turned is not None and mt == 0:
                        pe.wait_ge(S["T_act"], turned + kt + 1)
                        pe.wait_ge(S["T_dve"], splits_in(T_FILLS, turned + kt + 1))
                    last = products(pe, Ab[(n + mt) % 2][:, :], pair(w, kt, slice(mt * P, (mt + 1) * P)), pair(src, kt),
                                    kt == 0, kt == KT - 1)
                last.then_inc(S["A_full"], 1)
            return last

        def project(pe, w, width, src, fills, n):
            per = 512 // width if width < D else 2
            per = min(per, NB)
            for f in range(NB // per):
                A_free(pe, fills, n + f)
                for i in range(per):
                    b = f * per + i
                    for kt in range(KT):
                        last = products(pe, Ab[(n + f) % 2][:, i * width:(i + 1) * width],
                                        pair(src, kt, slice(b * P, (b + 1) * P)), pair(w, kt), kt == 0, kt == KT - 1)
                last.then_inc(S["A_full"], 1)
            return last

        def A_high(act, dst, n, bias=None):
            for mt in range(KT):
                act.wait_ge(S["A_full"], n + mt + 1)
                if bias is None:
                    i = nc.scalar.activation(dst[:, 0, mt, :], Ab[(n + mt) % 2][:, :], ACT.Copy)
                else:
                    i = nc.scalar.activation(dst[:, 0, mt, :], Ab[(n + mt) % 2][:, :], ACT.Identity, bias=col(bias, mt))
                i.then_inc(S["A_act"], 1)

        def A_low(dve, dst, n, bias=None):
            for mt in range(KT):
                dve.wait_ge(S["A_act"], read_by(A_FILLS, n + mt + 1, "A"))
                if bias is None:
                    i = nc.vector.tensor_tensor(dst[:, 1, mt, :], Ab[(n + mt) % 2][:, :], dst[:, 0, mt, :].bitcast(F32),
                                                ALU.subtract)
                else:
                    i = nc.vector.scalar_tensor_tensor(out=dst[:, 1, mt, :], in0=Ab[(n + mt) % 2][:, :], scalar=col(bias, mt),
                                                       in1=dst[:, 0, mt, :].bitcast(F32), op0=ALU.add, op1=ALU.subtract)
                i.then_inc(S["A_dve"], 1)

        def attend_pe(pe, L):
            G = L["G"]

            def scores(i):
                hg, b = divmod(i, NB)
                n = L["S"] + i
                kt = hg * 4 // L["heads_kt"]
                if n >= 2:
                    pe.wait_ge(S["S_read"], n - 1)
                if b == 0 and hg * 4 % L["heads_kt"] == 0:
                    pe.wait_ge(S["A_act"], read_by(A_FILLS, L["qfill"] + kt + 1, "A"))
                    pe.wait_ge(S["A_dve"], read_by(A_FILLS, L["qfill"] + kt + 1, "V"))
                if b == 0:
                    pe.wait_ge(S["km_high"], 4 * (L["km"] + hg + 1))
                    if hg == 0:
                        pe.wait_ge(S["km_low"], L["km"] + 4)
                bank = Sb[n % 2][:, :].rearrange("p (h t) -> p h t", h=4)
                buf = (L["km"] + hg) % 2
                last = products(pe, bank, pair(qT, kt, slice(b * P, (b + 1) * P)),
                                (km[:, buf, 0, :, b * P:(b + 1) * P], km[:, buf, 1, :, b * P:(b + 1) * P]), True, True)
                last.then_inc(S["S_full"], 1)

            def turn_probs(i):
                n = L["T"] + i
                T_free(pe, T_FILLS, n)
                pe.wait_ge(S["P_ready"], L["S"] + i + 1)
                for h in range(4):
                    last = nc.tensor.transpose(Tb[n % 2][:, h * P:(h + 1) * P], E[:, (L["S"] + i) % EXPS, h, :], ident[:, :])
                last.then_inc(S["T_full"], 1)

            def values(i):
                hg, b = divmod(i, NB)
                o_n = L["O"] + hg
                pe.wait_ge(S["T_act"], L["T"] + i + 1)
                if b == 0:
                    pe.wait_ge(S["O_read"], o_n - 1)
                for h in range(4):
                    vh = hg * 4 + h if L["hd"] == 16 else hg
                    last = pe.matmul(Ob[o_n % 2][h * VW:(h + 1) * VW, b * P:(b + 1) * P], L["v"][:, b, vh, :], PT[:, (L["S"] + i) % 2, h, :],
                                     start=True, stop=True)
                last.then_inc(S["pv_done"], 1)

            def turn_sums(hg):
                n = L["ctx"] + hg
                A_free(pe, A_FILLS, n)
                pe.wait_ge(S["O_read"], L["O"] + hg + 1)
                for b in range(NB):
                    last = nc.tensor.transpose(Ab[n % 2][:, b * P:(b + 1) * P], sums[:, hg % 2, b * P:(b + 1) * P], ident[:, :])
                last.then_inc(S["A_full"], 1)

            for i in range(G + 6):
                if i < G:
                    scores(i)
                if 2 <= i < G + 2:
                    turn_probs(i - 2)
                if 4 <= i < G + 4:
                    values(i - 4)
                if i >= 9 and i % NB == 1:
                    turn_sums(i // NB - 2)

        def attend_act(act, L):
            G = L["G"]
            for i in range(G + 5):
                if i < G:
                    act.wait_ge(S["nm_ready"], L["S"] + i)
                    e, m = E[:, (L["S"] + i) % EXPS], nm[:, (L["S"] + i) % EXPS]
                    for h in range(4):
                        last = nc.scalar.activation(e[:, h], e[:, h], ACT.Exp, scale=L["scale"], bias=m[:, h:h + 1])
                    last.then_inc(S["P_ready"], 1)
                if 2 <= i < G + 2:
                    evict_probs(act, L["S"] + i - 2, L["T"] + i - 2)
                if i >= 8 and i % NB == 0:
                    hg = i // NB - 2
                    act.wait_ge(S["pv_done"], L["S"] + NB * (hg + 1))
                    if hg >= 2:
                        act.wait_ge(S["A_full"], L["ctx"] + hg - 1)
                    nc.scalar.activation(sums[:, hg % 2], Ob[(L["O"] + hg) % 2][:, :], ACT.Copy).then_inc(S["O_read"], 1)

        def evict_probs(act, s, t):
            act.wait_ge(S["T_full"], t + 1)
            if s >= 2:
                act.wait_ge(S["pv_done"], s - 1)
            nc.scalar.activation(PT[:, s % 2], Tb[t % 2][:, :].rearrange("p (h t) -> p h t", h=4), ACT.Copy).then_inc(S["T_act"], 1)

        def soften(dve, s, L, b):
            bank = Sb[s % 2][:, :].rearrange("p (h t) -> p h t", h=4)
            dve.wait_ge(S["S_full"], s + 1)
            if s >= EXPS:
                dve.wait_ge(S["T_full"], T_of_S[s - EXPS] + 1)
            nc.vector.tensor_tensor(E[:, s % EXPS], bank, L["mask"][:, b, None, :].broadcast_to([P, 4, P]),
                                    ALU.add).then_inc(S["S_read"], 1)
            dve.wait_ge(S["S_read"], s + 1)
            nc.vector.tensor_reduce(mx[:, s % EXPS], E[:, s % EXPS], AX_X, ALU.max).then_inc(S["vstep"], 1)
            steps[0] += 1
            dve.wait_ge(S["vstep"], steps[0])
            nc.vector.tensor_scalar(nm[:, s % EXPS], mx[:, s % EXPS], -L["scale"], None, ALU.mult).then_inc(S["nm_ready"], 1)

        T_of_S = [first(T_FILLS, "p0")] + [first(T_FILLS, "p1") + i for i in range(16)] + [first(T_FILLS, "p2") + i for i in range(32)]
        steps = [0]

        def mask_low(dve, L, hg, h):
            if h == 0 and L["km"] + hg >= 2:
                dve.wait_ge(S["S_full"], km_used(L, hg))
            kt, j = divmod(hg * 4 + h, L["heads_kt"])
            nc.vector.tensor_scalar(km[:, (L["km"] + hg) % 2, 1, h, :], kT[:, 1, kt, :].bitcast(F32), L["hmask"][:, j:j + 1],
                                    None, ALU.mult).then_inc(S["km_low"], 1)

        def km_used(L, hg):
            n = L["km"] + hg - 2
            return 1 + NB * (n + 1)

        def mask_high(pool, L, hg):
            if L["km"] + hg >= 2:
                pool.wait_ge(S["S_full"], km_used(L, hg))
            for h in range(4):
                kt, j = divmod(hg * 4 + h, L["heads_kt"])
                if hg > 0:
                    nc.gpsimd.tensor_scalar(km[:, (L["km"] + hg) % 2, 1, h, :], kT[:, 1, kt, :].bitcast(F32), L["hmask"][:, j:j + 1],
                                            1.0, ALU.mult, ALU.mult)
                nc.gpsimd.tensor_scalar(km[:, (L["km"] + hg) % 2, 0, h, :], kT[:, 0, kt, :].bitcast(F32), L["hmask"][:, j:j + 1],
                                        1.0, ALU.mult, ALU.mult).then_inc(S["km_high"], 1)

        def attend_dve(dve, L):
            def normalise(hg):
                n, d = L["ctx"] + hg, L["hd"]
                dve.wait_ge(S["A_full"], n + 1)
                dve.wait_ge(S["A_dve"], read_by(A_FILLS, n, "V"))
                bank = Ab[n % 2][:, :].rearrange("p (b h d) -> p b h d", b=NB, h=4)
                nc.vector.reciprocal(r1[:, :, :], bank[:, :, :, d]).then_inc(S["vstep"], 1)
                steps[0] += 1
                dve.wait_ge(S["vstep"], steps[0])
                dst = o[:, :, hg * 4 * d:(hg + 1) * 4 * d].rearrange("p b (h d) -> p b h d", h=4)
                nc.vector.tensor_tensor(dst, bank[:, :, :, 0:d], r1[:, :, :, None].broadcast_to([P, NB, 4, d]),
                                        ALU.mult).then_inc(S["A_dve"], 1)

            dve.wait_ge(S["A_dve"], read_by(A_FILLS, L["kfill"] + KT, "V"))
            for h in range(4):
                mask_low(dve, L, 0, h)
            dve.wait_ge(S["mask1_ready"], 1)
            for i in range(L["G"] + 6):
                hg, b = divmod(i, NB)
                if i < L["G"]:
                    soften(dve, L["S"] + i, L, b)
                if i >= 9 and b == 1:
                    normalise(hg - 2)

        norms = [0]

        def norm(dve, src, dst, nb, w, w_loaded=None, meanwhile=None):
            for b in range(nb):
                nc.vector.bn_stats(stats[:, b], src(b)).then_inc(S["vstep"], 1)
            steps[0] += nb
            dve.wait_ge(S["vstep"], steps[0])
            for b in range(nb):
                nc.vector.bn_aggr(mv[:, b], stats[:, b]).then_inc(S["var_ready"], 1)
            norms[0] += 1
            if meanwhile:
                meanwhile()
            if w_loaded:
                dve.wait_ge(*w_loaded)
            dve.wait_ge(S["var_ready"], nb * norms[0])
            for b in range(nb):
                nc.vector.scalar_tensor_tensor(out=dst[:, b], in0=src(b), scalar=mv[:, b, 0:1], in1=w,
                                               op0=ALU.subtract, op1=ALU.mult).then_inc(S["vstep"], 1)
            steps[0] += nb
            dve.wait_ge(S["vstep"], steps[0])
            dve.wait_ge(S["rstd_ready"], norms[0])

        def power(pool, n, nb, eps):
            pool.wait_ge(S["var_ready"], nb * n)
            nc.gpsimd.tensor_scalar(var[:, 0:nb], mv[:, 0:nb, 1], eps, 1.0, ALU.add, ALU.mult).then_inc(S["pool_step"], 1)
            psteps[0] += 1
            pool.wait_ge(S["pool_step"], psteps[0])
            nc.gpsimd.tensor_tensor(rstd[:, 0:nb], var[:, 0:nb], neg_half[:, 0:nb], ALU.pow).then_inc(S["rstd_ready"], 1)

        psteps = [0]
        S["pool_step"] = sem("pool_step")

        def mlp_pe(pe, fills, n, o_n):
            def up(m):
                A_free(pe, fills, n + m)
                for kt in range(KT):
                    last = products(pe, Ab[(n + m) % 2][:, :], pair(fcw, kt, slice(m * P, (m + 1) * P)), pair(aT, kt),
                                    kt == 0, kt == KT - 1)
                last.then_inc(S["A_full"], 1)
                return last

            def down(m):
                pe.wait_ge(S["g_high"], m + 1)
                pe.wait_ge(S["g_low"], m + 1)
                if m == 0 and o_n:
                    pe.wait_ge(S["O_read"], o_n)
                for b in range(NB):
                    bank = Ob[(o_n + b // 2) % 2][:, (b % 2) * D:(b % 2 + 1) * D]
                    left = pair(gT[:, m % 2], slice(b * P, (b + 1) * P))
                    right = pair(pjw, m)
                    pe.matmul(bank, left[0], right[0], start=(m == 0 and b % 2 == 0), stop=False, skip_group_check=True)
                    pe.matmul(bank, left[1], right[0], start=False, stop=False, skip_group_check=True)
                    last = pe.matmul(bank, left[0], right[1], start=False, stop=(m == MT - 1), skip_group_check=True)
                last.then_inc(S["g_used"], 1)

            for m in range(MT + 2):
                if m < MT:
                    up(m)
                if m >= 2:
                    down(m - 2)

        def mlp_act(act, fills, n, func, bias):
            for m in range(MT):
                act.wait_ge(S["A_full"], n + m + 1)
                if m >= 2:
                    act.wait_ge(S["g_low"], m - 1)
                    act.wait_ge(S["g_used"], m - 1)
                nc.scalar.activation(g[:, m % 2], Ab[(n + m) % 2][:, :], func, bias=col(bias, m)).then_inc(S["A_act"], 1)
                act.wait_ge(S["A_act"], read_by(fills, n + m + 1, "A"))
                nc.scalar.activation(gT[:, m % 2, 0], g[:, m % 2], ACT.Copy).then_inc(S["g_high"], 1)

        def mlp_dve(dve):
            for m in range(MT):
                dve.wait_ge(S["g_high"], m + 1)
                nc.vector.tensor_tensor(gT[:, m % 2, 1], g[:, m % 2], gT[:, m % 2, 0].bitcast(F32), ALU.subtract).then_inc(S["g_low"], 1)

        def mlp_add(dve, o_n):
            dve.wait_ge(S["g_used"], MT)
            for f in range(2):
                nc.vector.tensor_tensor(xh[:, 2 * f:2 * f + 2], Ob[(o_n + f) % 2][:, :].rearrange("p (b d) -> p b d", b=2),
                                        xh[:, 2 * f:2 * f + 2], ALU.add).then_inc(S["O_read"], 1)

        fT = {n: first(T_FILLS, n) for n in ("c", "x", "p0", "z1", "ctx1", "z2", "x2", "ctx2")}
        fA = {n: first(A_FILLS, n) for n in ("q0", "v0", "k1", "v1", "q1", "o1", "k2", "v2", "fc", "q2", "o2")}

        nc.sync.sem_clear(inputs_loaded)
        nc.all_engine_barrier()
        with nc.Fori(0, HALVES) as half:
            with nc.Block() as block:
                @block.sync
                def _(sp):
                    other = bass.ds(NB - half * NB, NB)
                    sp.wait_ge(S["T_full"], fT["z2"] + KT)
                    load_ctx(sp, other)
                    sp.wait_ge(S["S_read"], len(S_FILLS))
                    load_masks(sp, other)
                    sp.wait_ge(S["x_out"], 1)
                    load_x(sp, other)
                    sp.wait_ge(inputs_loaded, 4 * 16)

                @block.tensor
                def _(pe):
                    turn(pe, z, T_FILLS, fT["c"])
                    turn(pe, xh, T_FILLS, fT["x"])
                    pe.wait_ge(S["T_act"], 4)
                    pe.wait_ge(S["T_dve"], 4)
                    project_T(pe, m0w, aT, A_FILLS, fA["q0"])
                    project(pe, v0w, D, cT, A_FILLS, fA["v0"])
                    pe.wait_ge(S["A_act"], 2)
                    pe.wait_ge(S["A_dve"], 2)
                    for b in range(NB):
                        for kt in range(KT):
                            last = products(pe, Sb[0][:, b * P:(b + 1) * P], pair(qT, kt, slice(b * P, (b + 1) * P)),
                                            pair(cT, kt, slice(b * P, (b + 1) * P)), kt == 0, kt == KT - 1)
                    last.then_inc(S["S_full"], 1)
                    project_T(pe, w1[1], cT, A_FILLS, fA["k1"])
                    project(pe, w1[2], D, cT, A_FILLS, fA["v1"])
                    T_free(pe, T_FILLS, fT["p0"])
                    pe.wait_ge(S["P_ready"], 1)
                    for b in range(NB):
                        last = nc.tensor.transpose(Tb[fT["p0"] % 2][:, b * P:(b + 1) * P], E[:, 0, b, :], ident[:, :])
                    last.then_inc(S["T_full"], 1)
                    pe.wait_ge(S["T_act"], fT["p0"] + 1)
                    pe.wait_ge(S["A_dve"], read_by(A_FILLS, fA["v0"] + 2, "V"))
                    for b in range(NB):
                        if b >= 2:
                            pe.wait_ge(S["O_read"], b - 1)
                        last = pe.matmul(Ob[b % 2][:, 0:D + 1], PT[:, 0, b, :], v0[:, b, :], start=True, stop=True)
                        last.then_inc(S["O_full" if b < NB - 1 else "pv_done"], 1)
                    turn(pe, z, T_FILLS, fT["z1"], 0)
                    project_T(pe, w1[0], aT, A_FILLS, fA["q1"], fT["z1"])
                    attend_pe(pe, LAYERS[1])
                    pe.wait_ge(S["A_dve"], read_by(A_FILLS, LAYERS[1]["ctx"] + 4, "V"))
                    turn(pe, o, T_FILLS, fT["ctx1"])
                    pe.wait_ge(S["T_act"], fT["ctx1"] + KT)
                    pe.wait_ge(S["T_dve"], splits_in(T_FILLS, fT["ctx1"] + KT))
                    project(pe, w1[3], D, aT, A_FILLS, fA["o1"])
                    project_T(pe, w2[1], cT, A_FILLS, fA["k2"])
                    project(pe, w2v, 64, cT, A_FILLS, fA["v2"])
                    turn(pe, z, T_FILLS, fT["z2"], 1)
                    pe.wait_ge(S["T_act"], fT["z2"] + KT)
                    pe.wait_ge(S["T_dve"], splits_in(T_FILLS, fT["z2"] + KT))
                    mlp_pe(pe, A_FILLS, fA["fc"], first(O_FILLS, "mlp"))
                    pe.wait_ge(S["O_read"], LAYERS[2]["O"])
                    turn(pe, xh, T_FILLS, fT["x2"])
                    project_T(pe, w2[0], aT, A_FILLS, fA["q2"], fT["x2"])
                    attend_pe(pe, LAYERS[2])
                    pe.wait_ge(S["A_dve"], read_by(A_FILLS, LAYERS[2]["ctx"] + 8, "V"))
                    turn(pe, o, T_FILLS, fT["ctx2"])
                    pe.wait_ge(S["T_act"], fT["ctx2"] + KT)
                    pe.wait_ge(S["T_dve"], splits_in(T_FILLS, fT["ctx2"] + KT))
                    project(pe, w2[2], D, aT, A_FILLS, fA["o2"])

                @block.scalar
                def _(act):
                    split_high(act, cT, fT["c"])
                    split_high(act, aT, fT["x"])
                    A_high(act, qT, fA["q0"])
                    act.wait_ge(S["S_read"], 1)
                    nc.scalar.activation(E[:, 0], E[:, 0], ACT.Exp, scale=D ** -0.5).then_inc(S["P_ready"], 1)
                    A_high(act, kT, fA["k1"], "L1_xattn_k_b")
                    evict_probs(act, 0, fT["p0"])
                    a_free(act, "q0", 2)
                    split_high(act, aT, fT["z1"])
                    act.wait_ge(S["S_full"], 1)
                    A_high(act, qT, fA["q1"], "L1_xattn_q_b")
                    attend_act(act, LAYERS[1])
                    a_free(act, "q1", 2)
                    split_high(act, aT, fT["ctx1"])
                    act.wait_ge(S["km_high"], 16)
                    act.wait_ge(S["km_low"], 4)
                    A_high(act, kT, fA["k2"], "L2_xattn_bk")
                    a_free(act, "o1", 2)
                    split_high(act, aT, fT["z2"])
                    mlp_act(act, A_FILLS, fA["fc"], ACT.Gelu_apprx_tanh, "L1_xattn_fc_b")
                    a_free(act, "fc", MT)
                    split_high(act, aT, fT["x2"])
                    act.wait_ge(S["S_full"], LAYERS[2]["S"])
                    A_high(act, qT, fA["q2"], "L2_xattn_bq")
                    attend_act(act, LAYERS[2])
                    a_free(act, "q2", 2)
                    split_high(act, aT, fT["ctx2"])

                @block.gpsimd
                def _(pool):
                    psteps[0] = 0
                    power(pool, 1, NB, LN_EPS)
                    pool.wait_ge(S["norm_ready"], NB)
                    nc.gpsimd.tensor_tensor(xh[:, :, :], xh[:, :, :], row("L1_xattn_cproj_b")[:, None, :].broadcast_to([P, NB, D]),
                                            ALU.add).then_inc(S["x_biased"], 1)
                    pool.wait_ge(S["A_act"], read_by(A_FILLS, fA["k1"] + KT, "A"))
                    pool.wait_ge(S["A_dve"], read_by(A_FILLS, fA["k1"] + KT, "V"))
                    for hg in range(4):
                        mask_high(pool, LAYERS[1], hg)
                    power(pool, 2, NB, LN_EPS)
                    pool.wait_ge(S["norm_ready"], 2 * NB)
                    nc.gpsimd.tensor_tensor(xh[:, :, :], xh[:, :, :], row("L1_xattn_proj_b")[:, None, :].broadcast_to([P, NB, D]),
                                            ALU.add).then_inc(S["x_biased"], 1)
                    pool.wait_ge(S["A_act"], read_by(A_FILLS, fA["k2"] + KT, "A"))
                    pool.wait_ge(S["A_dve"], read_by(A_FILLS, fA["k2"] + KT, "V"))
                    for hg in range(2):
                        mask_high(pool, LAYERS[2], hg)
                    pool.wait_ge(S["T_full"], fT["x2"] + KT)
                    pool.wait_ge(S["O_read"], LAYERS[2]["O"])
                    nc.gpsimd.tensor_tensor(xh[:, :, :], xh[:, :, :], row("L2_xattn_bo")[:, None, :].broadcast_to([P, NB, D]),
                                            ALU.add).then_inc(S["x_biased"], 1)
                    for hg in range(2, 8):
                        mask_high(pool, LAYERS[2], hg)
                    power(pool, 3, NB, LN2_EPS)

                @block.vector
                def _(dve):
                    steps[0] = norms[0] = 0
                    nc.vector.tensor_scalar(masks[1][:, :, :], mask1b[:, :, :], 1.0, BIG, ALU.subtract, ALU.mult).then_inc(S["mask1_ready"], 1)
                    split_low(dve, cT, fT["c"])
                    split_low(dve, aT, fT["x"])
                    A_low(dve, qT, fA["q0"])
                    for f in range(2):
                        n = fA["v0"] + f
                        dve.wait_ge(S["A_full"], n + 1)
                        nc.vector.tensor_copy(v0[:, 2 * f:2 * f + 2, 0:D], Ab[n % 2][:, :].rearrange("p (b d) -> p b d", b=2)).then_inc(S["A_dve"], 1)
                    bank = Sb[0][:, :].rearrange("p (b t) -> p b t", b=NB)
                    dve.wait_ge(S["S_full"], 1)
                    nc.vector.tensor_reduce(mx[:, 0], bank, AX_X, ALU.max).then_inc(S["vstep"], 1)
                    steps[0] += 1
                    dve.wait_ge(S["vstep"], steps[0])
                    nc.vector.tensor_tensor(E[:, 0], bank, mx[:, 0, :, None].broadcast_to([P, NB, P]), ALU.subtract).then_inc(S["S_read"], 1)
                    A_low(dve, kT, fA["k1"], "L1_xattn_k_b")
                    for f in range(2):
                        n = fA["v1"] + f
                        dve.wait_ge(S["A_full"], n + 1)
                        nc.vector.tensor_tensor(v1[:, 2 * f:2 * f + 2, :, 0:16], Ab[n % 2][:, :].rearrange("p (b h d) -> p b h d", b=2, d=16),
                                                row("L1_xattn_v_b").rearrange("p (h d) -> p h d", d=16)[:, None].broadcast_to([P, 2, 16, 16]),
                                                ALU.add).then_inc(S["A_dve"], 1)
                    for b in range(NB):
                        if b < NB - 1:
                            dve.wait_ge(S["O_full"], b + 1)
                        else:
                            dve.wait_ge(S["pv_done"], 1)
                        nc.vector.reciprocal(r0[:, b:b + 1], Ob[b % 2][:, D:D + 1]).then_inc(S["vstep"], 1)
                        steps[0] += 1
                        dve.wait_ge(S["vstep"], steps[0])
                        nc.vector.tensor_scalar(r0[:, b:b + 1], r0[:, b:b + 1], alpha[:, 0:1], None, ALU.mult).then_inc(S["vstep"], 1)
                        steps[0] += 1
                        dve.wait_ge(S["vstep"], steps[0])
                        dve.wait_ge(S["T_full"], fT["x"] + KT)
                        nc.vector.scalar_tensor_tensor(out=xh[:, b], in0=Ob[b % 2][:, 0:D], scalar=r0[:, b:b + 1], in1=xh[:, b],
                                                       op0=ALU.mult, op1=ALU.add).then_inc(S["O_read"], 1)
                    dve.wait_ge(S["O_read"], NB)
                    norm(dve, lambda b: xh[:, b], z, NB, row("L1_xattn_ln1_w"))
                    for b in range(NB):
                        nc.vector.scalar_tensor_tensor(out=z[:, b], in0=z[:, b], scalar=rstd[:, b:b + 1], in1=row("L1_xattn_ln1_b"),
                                                       op0=ALU.mult, op1=ALU.add).then_inc(S["norm_ready"], 1)
                    split_low(dve, aT, fT["z1"])
                    A_low(dve, qT, fA["q1"], "L1_xattn_q_b")
                    attend_dve(dve, LAYERS[1])
                    split_low(dve, aT, fT["ctx1"])
                    dve.wait_ge(S["x_biased"], 1)
                    for f in range(2):
                        n = fA["o1"] + f
                        dve.wait_ge(S["A_full"], n + 1)
                        nc.vector.tensor_tensor(xh[:, 2 * f:2 * f + 2], Ab[n % 2][:, :].rearrange("p (b d) -> p b d", b=2),
                                                xh[:, 2 * f:2 * f + 2], ALU.add).then_inc(S["A_dve"], 1)
                    dve.wait_ge(S["A_dve"], read_by(A_FILLS, fA["o1"] + 2, "V"))
                    dve.wait_ge(S["T_full"], fT["z1"] + KT)
                    norm(dve, lambda b: xh[:, b], z, NB, row("L1_xattn_ln2_w"))
                    for b in range(NB):
                        nc.vector.scalar_tensor_tensor(out=z[:, b], in0=z[:, b], scalar=rstd[:, b:b + 1], in1=row("L1_xattn_ln2_b"),
                                                       op0=ALU.mult, op1=ALU.add).then_inc(S["norm_ready"], 1)
                    dve.wait_ge(S["km_high"], 16)
                    A_low(dve, kT, fA["k2"], "L2_xattn_bk")
                    n = fA["v2"]
                    dve.wait_ge(S["A_full"], n + 1)
                    nc.vector.tensor_tensor(v2[:, :, :, 0:8], Ab[n % 2][:, 0:NB * 64].rearrange("p (b h d) -> p b h d", b=NB, d=8),
                                            bv2[:, :].rearrange("p (h d) -> p h d", d=8)[:, None].broadcast_to([P, NB, 8, 8]),
                                            ALU.add).then_inc(S["A_dve"], 1)
                    split_low(dve, aT, fT["z2"])
                    mlp_dve(dve)
                    dve.wait_ge(S["x_biased"], 2)
                    mlp_add(dve, first(O_FILLS, "mlp"))
                    split_low(dve, aT, fT["x2"])
                    A_low(dve, qT, fA["q2"], "L2_xattn_bq")
                    attend_dve(dve, LAYERS[2])
                    split_low(dve, aT, fT["ctx2"])
                    dve.wait_ge(S["x_biased"], 3)
                    for f in range(2):
                        n = fA["o2"] + f
                        dve.wait_ge(S["A_full"], n + 1)
                        nc.vector.tensor_tensor(xh[:, 2 * f:2 * f + 2], Ab[n % 2][:, :].rearrange("p (b d) -> p b d", b=2),
                                                xh[:, 2 * f:2 * f + 2], ALU.add).then_inc(S["A_dve"], 1)
                    dve.wait_ge(S["A_dve"], read_by(A_FILLS, fA["o2"] + 2, "V"))
                    dve.wait_ge(S["T_full"], fT["ctx2"] + KT)
                    norm(dve, lambda b: xh[:, b], o, NB, row("L2_xattn_gamma"))
                    for b in range(NB):
                        nc.vector.scalar_tensor_tensor(out=x_all[:, bass.ds(half * NB + b, 1), :], in0=o[:, b:b + 1], scalar=rstd[:, b:b + 1],
                                                       in1=row("L2_xattn_beta")[:, None, :], op0=ALU.mult, op1=ALU.add).then_inc(S["x_out"], 1)
            for each in [*S.values(), inputs_loaded]:
                nc.sync.sem_clear(each)
            nc.all_engine_barrier()

        s3 = ExitStack()
        cT3 = sb("cT3", [P, 2, KT, B * P], R32, s3)
        hT3 = sb("hT3", [P, 2, KT, B * P], R32, s3)
        t3 = ExitStack()
        c3 = sb("c3", [P, B, D], F32, t3)
        z3 = sb("z3", [P, B, D], F32, t3)
        t3.close()
        ctxT3 = sb("ctxT3", [P, 2, HG3, B * P], R32, s3)
        qT3 = sb("qT3", [P, 2, 2, B * P], R32, s3)
        fc_st = sb("fc_st", [P, KT, INNER], F32, s3)
        pj_st = sb("pj_st", [P, MT, D], F32, s3)
        wst = [sb(f"wst_{n}", [P, KT, HG3 * P], F32, s3) for n in "qkv"]
        wo_st = sb("wo_st", [P, HG3, D], F32, s3)
        w3 = [sb(f"w3_{n}", [P, 2, KT, HG3 * P], R32, s3) for n in "qkv"]
        wo3 = sb("wo3", [P, 2, HG3, D], R32, s3)
        v_row = sb("v_row", [P, HG3 * P], F32, s3)
        bias_v_row = sb("bias_v_row", [P, HG3 * P], F32, s3)
        kT3 = sb("kT3", [P, 2, 2, B, T3], R32, s3)
        vf = sb("vf", [P, 2, 2, HG3 * P], F32, s3)
        v3 = sb("v3", [P, 2, B, HG3 * P], R32, s3)
        E3 = sb("E3", [P, EXPS, 3, T3], F32, s3)
        PT3 = sb("PT3", [P, 2, 2, 3 * P], R32, s3)
        mx3 = sb("mx3", [P, EXPS, 3], F32, s3)
        nm3 = sb("nm3", [P, EXPS, 3], F32, s3)
        sum3 = sb("sum3", [P, EXPS, 3], F32, s3)
        rs3 = sb("rs3", [P, EXPS, 3], F32, s3)
        s3.close()
        SCALE3 = float(P) ** -0.5

        PASS = [("S", 0, 0, 0), ("q", 0, 1, 0), ("P", 0, 0, 0), ("T", -1, 1, 2), ("q", 0, 1, 1), ("PV", -1, 1, 1), ("W", 1, 0, 0), ("v", 0, 0, 1),
                ("S", 0, 0, 1), ("v", 0, 0, 2), ("P", 0, 0, 1), ("T", 0, 0, 0), ("k", 0, 1, 0), ("PV", -1, 1, 2), ("v", 0, 0, 3),
                ("S", 0, 0, 2), ("k", 0, 1, 1), ("P", 0, 0, 2), ("T", 0, 0, 1), ("W", 1, 1, 0), ("out", -1, 0, 0), ("PV", 0, 0, 0), ("W", 1, 2, 0),
                ("out", -1, 0, 1),
                ("S", 0, 1, 0), ("out", -1, 0, 2), ("P", 0, 1, 0), ("T", 0, 0, 2), ("out", -1, 0, 3), ("row", 1, 0, 0), ("PV", 0, 0, 1), ("WO", 0, 0, 0),
                ("S", 0, 1, 1), ("k", 1, 0, 0), ("P", 0, 1, 1), ("T", 0, 1, 0), ("k", 1, 0, 1), ("PV", 0, 0, 2), ("q", 1, 0, 0),
                ("S", 0, 1, 2), ("q", 1, 0, 1), ("P", 0, 1, 2), ("T", 0, 1, 1), ("PV", 0, 1, 0), ("v", 1, 0, 0)]
        AHEAD_W = [("W", 1, n, 0) for n in range(3)] + [("row", 1, 0, 0)]
        AHEAD_K = [w for w in PASS if w[1] == 1 and w[0] == "k"]
        AHEAD_QV = [w for w in PASS if w[1] == 1 and w[0] in "qv"]
        HEAD_START = AHEAD_K + AHEAD_QV
        FINISH = [w for w in PASS if w[1] == -1]
        PAIRS = H3 // HG3
        FILLS = [w for w in PASS if w[0] in ("q", "k", "v", "out")]
        A_READS = [w for w in FILLS if w[0] in ("q", "k")]
        NF, NG, NC, NV = len(FILLS), 3 * HG3, 2 * HG3, B // 2
        AHEAD = sum(w[1] == 1 for w in FILLS)
        OUTS = NF - sum(w[0] != "out" for w in FILLS)

        def steps_of(p):
            if isinstance(p, int) and p == PAIRS:
                return FINISH
            if isinstance(p, int) and p == 0:
                return [w for w in PASS if w[1] != -1]
            if isinstance(p, int) and p == PAIRS - 1:
                return [w for w in PASS if w[1] != 1]
            return PASS

        def fill3(p, step):
            if isinstance(p, int) and p == -1:
                return FILLS.index(step) % 2, HEAD_START.index(step)
            at = FILLS.index(step)
            if isinstance(p, int) and p == 0:
                outs = sum(w[0] == "out" for w in FILLS[:at])
                return at % 2, AHEAD + at - outs
            if isinstance(p, int) and p == PAIRS:
                return at % 2, NF * PAIRS - OUTS + [w for w in FINISH if w[0] == "out"].index(step)
            return at % 2, p * NF + (AHEAD - OUTS + at)

        def high3(p, step):
            if isinstance(p, int) and p == -1:
                return [w for w in HEAD_START if w[0] in "qk"].index(step) + 1
            return p * len(A_READS) + (sum(w[1] == 1 for w in A_READS) + A_READS.index(step) + 1)

        def passes(eng, do):
            do(0)
            with eng.Fori(1, PAIRS - 1) as p:
                do(p)
            do(PAIRS - 1)
            do(PAIRS)

        def reached(eng, sem, value):
            if not isinstance(value, int) or value > 0:
                eng.wait_ge(sem, value)

        sem = lambda n: ctx.enter_context(nc.semaphore(f"{n}3"))
        N = {n: sem(n) for n in (
            "wq_loaded", "wk_loaded", "wv_loaded", "wo_loaded", "rows_loaded", "rowb_loaded", "w_high", "w_low", "wo_high", "wo_low",
            "v_row_ready", "A_full", "A_act", "A_dve", "bias_high", "bias_low", "v_high", "v_low",
            "S_full", "max_ready", "nm_ready", "exp_done", "r_ready", "P_ready", "T_full", "T_act", "T_dve", "pv_done",
            "ctx_high", "ctx_low", "act_apart", "pool_apart")}

        def attention3(att):
            names = {n: f"L3_xattn_{n}{att + 1}" for n in ("wq", "wk", "wv", "wo", "bv", "bias_v")}
            ln_w, ln_b, bo = f"L3_xattn_ln{att + 1}_scale", f"L3_xattn_ln{att + 1}_offset", f"L3_xattn_bo{att + 1}"
            cols = colsA[:, atA["L3_xattn_bq1"]:atA["L3_xattn_bq1"] + 4 * H3] if att == 0 else colsB[:, 0:4 * H3]
            cols = cols.rearrange("p (k h) -> p k h", k=4)

            turns = ([("c", f) for f in range(4)] if att == 0 else []) + [("h", f) for f in range(4)]

            def turn3(pe, what):
                for n, (which, f) in enumerate(turns):
                    if which != what:
                        continue
                    if n >= 2:
                        pe.wait_ge(S["T_act"], n - 1)
                        pe.wait_ge(S["T_dve"], n - 1)
                    kt, half = divmod(f, 2)
                    src = c3 if what == "c" else z3
                    for b in range(NB):
                        if what == "h" and kt == 0:
                            pe.wait_ge(S["norm_ready"], half * NB + b + 1)
                        last = nc.tensor.transpose(Tb[n % 2][:, b * P:(b + 1) * P],
                                                   src[:, half * NB + b, kt * P:(kt + 1) * P], ident[:, :])
                    last.then_inc(S["T_full"], 1)

            def split3_high(act, what):
                for n, (which, f) in enumerate(turns):
                    if which == what:
                        kt, half = divmod(f, 2)
                        dst = cT3 if what == "c" else hT3
                        act.wait_ge(S["T_full"], n + 1)
                        nc.scalar.activation(dst[:, 0, kt, half * TOK:(half + 1) * TOK], Tb[n % 2][:, :], ACT.Copy).then_inc(S["T_act"], 1)

            def split3_low(dve, what):
                for n, (which, f) in enumerate(turns):
                    if which == what:
                        kt, half = divmod(f, 2)
                        dst = cT3 if what == "c" else hT3
                        part = slice(half * TOK, (half + 1) * TOK)
                        dve.wait_ge(S["T_act"], n + 1)
                        nc.vector.tensor_tensor(dst[:, 1, kt, part], Tb[n % 2][:, :], dst[:, 0, kt, part].bitcast(F32),
                                                ALU.subtract).then_inc(S["T_dve"], 1)

            def const(kind, p, h):
                return cols[:, kind, bass.ds(p * HG3 + h, 1)]

            with nc.Block() as block:
                @block.sync
                def _(sp):
                    def load_pair(p):
                        at = bass.ds(p * HG3 * P, HG3 * P)
                        for n, (w, t) in enumerate((("wq", wst[0]), ("wk", wst[1]), ("wv", wst[2]))):
                            reached(sp, N["w_low"], p * 3 + (n - 2))
                            sp.dma_start(t[:, :, :], a[names[w]][:, at].rearrange("(k p) n -> p k n", p=P)).then_inc(N[w + "_loaded"], 16)
                        reached(sp, N["v_low"], p * NV)
                        sp.dma_start(v_row[:, :], a[names["bv"]][at][None, :].broadcast_to([P, HG3 * P])).then_inc(N["rows_loaded"], 16)
                        sp.dma_start(bias_v_row[:, :], a[names["bias_v"]].rearrange("a b h k -> (a b h k)")[at][None, :]
                                     .broadcast_to([P, HG3 * P])).then_inc(N["rowb_loaded"], 16)

                    def load_out(p):
                        reached(sp, N["wo_low"], p * 1)
                        sp.dma_start(wo_st[:, :, :], a[names["wo"]][bass.ds(p * HG3 * P, HG3 * P), :].rearrange("(h p) n -> p h n", p=P)
                                     ).then_inc(N["wo_loaded"], 16)

                    if att == 0:
                        sp.dma_start(c3[:, :, :], a["ctx_2048"].rearrange("b t d -> t b d")).then_inc(S["c_loaded"], 16)
                    load_pair(0)
                    load_out(0)
                    if att == 1:
                        sp.dma_start(fc_st[:, :, :], a["L3_xattn_w_fc1"].rearrange("(k p) n -> p k n", p=P)).then_inc(fc_in, 16)
                        sp.dma_start(pj_st[:, :, :], a["L3_xattn_w_fc2"].rearrange("(m p) n -> p m n", p=P)).then_inc(pj_in, 16)
                    load_pair(1)
                    with sp.Fori(1, PAIRS - 1) as p:
                        load_out(p)
                        load_pair(p + 1)
                    load_out(PAIRS - 1)

                @block.gpsimd
                def _(pool):
                    def do(p, steps=None):
                        for step in steps or steps_of(p):
                            what, dp, h, j = step
                            if what == "row":
                                pool.wait_ge(N["rows_loaded"], (p + 2) * 16)
                                pool.wait_ge(N["rowb_loaded"], (p + 2) * 16)
                                nc.gpsimd.tensor_tensor(v_row[:, :], v_row[:, :], bias_v_row[:, :], ALU.subtract).then_inc(N["v_row_ready"], 1)
                            elif what == "WO":
                                pool.wait_ge(N["wo_loaded"], (p + 1) * 16)
                                if not (isinstance(p, int) and p == 0):
                                    pool.wait_ge(N["A_full"], fill3(p, ("out", -1, 0, NB - 1))[1] + 1)
                                pool.sem_inc(N["pool_apart"], 1)
                                nc.gpsimd.tensor_scalar(wo3[:, 0], wo_st[:, :, :], 1.0, 1.0, ALU.mult, ALU.mult).then_inc(N["wo_high"], 1)
                                pool.wait_ge(N["wo_high"], p + 1)
                                nc.gpsimd.tensor_tensor(wo3[:, 1], wo_st[:, :, :], wo3[:, 0].bitcast(F32), ALU.subtract).then_inc(N["wo_low"], 1)
                            elif what == "v":
                                pool.wait_ge(N["v_high"], (p + dp) * NV + (j + 1))
                                nc.gpsimd.tensor_tensor(v3[:, 1, 2 * j:2 * j + 2], vf[:, j % 2], v3[:, 0, 2 * j:2 * j + 2].bitcast(F32),
                                                        ALU.subtract).then_inc(N["v_low"], 1)
                            elif what == "P":
                                g_ = 3 * h + j
                                nb = GROUPS3[j][1] - GROUPS3[j][0]
                                pool.wait_ge(N["r_ready"], p * NG + (g_ + 1))
                                e = E3[:, g_ % EXPS, 0:nb, 0:P]
                                nc.gpsimd.tensor_tensor(e, e, rs3[:, g_ % EXPS, 0:nb, None].broadcast_to([P, nb, P]),
                                                        ALU.mult).then_inc(N["P_ready"], 1)
                    psteps[0] = 0
                    if att == 0:
                        nc.gpsimd.memset(kT3[:, :, :, :, P + 1:T3].bitcast(F32), 0.0).then_inc(pad_cleared, 1)
                    power(pool, 1, B, LN_EPS)
                    for n in range(3):
                        pool.wait_ge(N["w_high"], n + 1)
                        nc.gpsimd.tensor_tensor(w3[n][:, 1], wst[n][:, :, :], w3[n][:, 0].bitcast(F32), ALU.subtract).then_inc(N["w_low"], 1)
                    do(-1, AHEAD_W)
                    if att == 1:
                        pool.wait_ge(split3, 1)
                        nc.gpsimd.tensor_tensor(fcw[:, 1], fc_st[:, :, :], fcw[:, 0].bitcast(F32), ALU.subtract)
                    do(-1, HEAD_START)
                    do(0)
                    pool.wait_ge(S["norm_ready"], B)
                    if att == 0:
                        pool.wait_ge(rows_in, 16 * len(ROWS3))
                    nc.gpsimd.tensor_tensor(x_all[:, :, :], x_all[:, :, :], row(bo)[:, None, :].broadcast_to([P, B, D]),
                                            ALU.add).then_inc(S["x_biased"], 1)
                    if att == 1:
                        pool.wait_ge(split3, 2)
                        nc.gpsimd.tensor_tensor(pjw[:, 1], pj_st[:, :, :], pjw[:, 0].bitcast(F32), ALU.subtract)
                    with pool.Fori(1, PAIRS - 1) as p:
                        do(p)
                    do(PAIRS - 1)
                    do(PAIRS)

                @block.scalar
                def _(act):
                    if att == 0:
                        for i, name in enumerate(ROWS3):
                            act.dma_start(rows[:, i, :], a[name][None, :].broadcast_to([P, D])).then_inc(rows_in, 16)

                    def do(p, steps=None):
                        for step in steps or steps_of(p):
                            what, dp, h, j = step
                            if what == "W":
                                act.wait_ge(N[("wq", "wk", "wv")[h] + "_loaded"], (p + 2) * 16)
                                if not (isinstance(p, int) and p == -1):
                                    last = (("q", 0, 1, 1), ("k", 0, 1, 1), ("v", 0, 0, 3))[h]
                                    act.wait_ge(N["A_full"], fill3(p, last)[1] + 1)
                                nc.scalar.activation(w3[h][:, 0], wst[h][:, :, :], ACT.Copy).then_inc(N["w_high"], 1)
                            elif what in ("q", "k"):
                                bank, n = fill3(p, step)
                                act.wait_ge(N["A_full"], n + 1)
                                reached(act, N["S_full"], (p + dp) * NG + (3 * h - 3))
                                act.sem_inc(N["act_apart"], 1)
                                c = const(0 if what == "q" else 1, p + dp, h)
                                if what == "q":
                                    nc.scalar.activation(qT3[:, h, 0, j * TOK:(j + 1) * TOK], Ab[bank][:, :], ACT.Identity,
                                                         bias=c).then_inc(N["A_act"], 1)
                                else:
                                    nc.scalar.activation(kT3[:, h, 0, j * NB:(j + 1) * NB, 0:P],
                                                         Ab[bank][:, :].rearrange("p (b t) -> p b t", b=NB), ACT.Identity,
                                                         bias=c).then_inc(N["A_act"], 1)
                            elif what == "v":
                                act.wait_ge(N["A_dve"], fill3(p, step)[1] + 1)
                                group = [2 * j + 1 in range(*g_) for g_ in GROUPS3].index(True)
                                reached(act, N["pv_done"], (p + dp) * NG + (3 + group + 1 - NG))
                                nc.scalar.activation(v3[:, 0, 2 * j:2 * j + 2], vf[:, j % 2], ACT.Copy).then_inc(N["v_high"], 1)
                            elif what == "S":
                                g_ = 3 * h + j
                                act.wait_ge(N["nm_ready"], p * NG + (g_ + 1))
                                reached(act, N["T_full"], p * NG + (g_ - EXPS + 1))
                                reached(act, N["r_ready"], p * NG + (g_ - EXPS + 1))
                                for b in range(GROUPS3[j][1] - GROUPS3[j][0]):
                                    last = nc.scalar.activation(E3[:, g_ % EXPS, b, 0:P + 1], Sb[g_ % 2][:, b * T3:b * T3 + P + 1], ACT.Exp,
                                                                scale=SCALE3, bias=nm3[:, g_ % EXPS, b:b + 1],
                                                                accum_out=sum3[:, g_ % EXPS, b:b + 1])
                                last.then_inc(N["exp_done"], 1)
                            elif what == "T":
                                g_ = 3 * h + j
                                w = (GROUPS3[j][1] - GROUPS3[j][0]) * P
                                act.wait_ge(N["T_full"], (p + dp) * NG + (g_ + 1))
                                reached(act, N["pv_done"], (p + dp) * NG + (g_ - 1))
                                nc.scalar.activation(PT3[:, g_ % 2, 0, 0:w], Tb[g_ % 2][:, 0:w], ACT.Copy).then_inc(N["T_act"], 1)
                            elif what == "PV" and j >= 1:
                                act.wait_ge(N["pv_done"], (p + dp) * NG + (3 * h + j + 1))
                                if (h, j) == (0, 1) and not (isinstance(p, int) and p == 0):
                                    act.wait_ge(N["A_full"], fill3(p, ("out", -1, 0, NB - 1))[1] + 1)
                                act.sem_inc(N["act_apart"], 1)
                                nc.scalar.activation(ctxT3[:, 0, h, (j - 1) * TOK:j * TOK], Ob[j - 1][:, :], ACT.Identity,
                                                     bias=const(3, p + dp, h)).then_inc(N["ctx_high"], 1)
                    do(-1, AHEAD_W)
                    if att == 1:
                        act.wait_ge(fc_in, 16)
                        nc.scalar.activation(fcw[:, 0], fc_st[:, :, :], ACT.Copy).then_inc(split3, 1)
                        act.wait_ge(pj_in, 16)
                        nc.scalar.activation(pjw[:, 0], pj_st[:, :, :], ACT.Copy).then_inc(split3, 1)
                    split3_high(act, "c")
                    do(-1, AHEAD_K)
                    split3_high(act, "h")
                    do(-1, AHEAD_QV)
                    passes(act, do)

                @block.vector
                def _(dve):
                    def do(p, steps=None):
                        pending = []

                        def settle(keep=0):
                            while len(pending) > keep:
                                g_, nb = pending.pop(0)
                                dve.wait_ge(N["exp_done"], p * NG + (g_ + 1))
                                reached(dve, N["P_ready"], p * NG + (g_ - EXPS + 1))
                                nc.vector.reciprocal(rs3[:, g_ % EXPS, 0:nb], sum3[:, g_ % EXPS, 0:nb]).then_inc(N["r_ready"], 1)

                        for step in steps or steps_of(p):
                            what, dp, h, j = step
                            if what == "P":
                                settle()
                            elif what == "W":
                                dve.wait_ge(N["w_high"], p * 3 + (3 + h + 1))
                                nc.vector.tensor_tensor(w3[h][:, 1], wst[h][:, :, :], w3[h][:, 0].bitcast(F32), ALU.subtract).then_inc(N["w_low"], 1)
                            elif what in ("q", "k"):
                                bank, n = fill3(p, step)
                                dve.wait_ge(N["A_act"], high3(p, step))
                                c = const(0 if what == "q" else 1, p + dp, h)
                                if what == "q":
                                    high, low, full = (qT3[:, h, 0, j * TOK:(j + 1) * TOK], qT3[:, h, 1, j * TOK:(j + 1) * TOK], Ab[bank][:, :])
                                else:
                                    high, low = kT3[:, h, 0, j * NB:(j + 1) * NB, 0:P], kT3[:, h, 1, j * NB:(j + 1) * NB, 0:P]
                                    full = Ab[bank][:, :].rearrange("p (b t) -> p b t", b=NB)
                                nc.vector.scalar_tensor_tensor(out=low, in0=full, scalar=c, in1=high.bitcast(F32), op0=ALU.add,
                                                               op1=ALU.subtract).then_inc(N["A_dve"], 1)
                                if what == "k" and j == 1:
                                    key = const(2, p + dp, h).broadcast_to([P, B])
                                    nc.vector.tensor_copy(kT3[:, h, 0, :, P], key).then_inc(N["bias_high"], 1)
                                    dve.wait_ge(N["bias_high"], (p + dp) * HG3 + (h + 1))
                                    nc.vector.tensor_tensor(kT3[:, h, 1, :, P], key, kT3[:, h, 0, :, P].bitcast(F32),
                                                            ALU.subtract).then_inc(N["bias_low"], 1)
                            elif what == "v":
                                bank, n = fill3(p, step)
                                dve.wait_ge(N["A_full"], n + 1)
                                if j == 0:
                                    dve.wait_ge(N["v_row_ready"], p + (dp + 1))
                                reached(dve, N["v_low"], (p + dp) * NV + (j - 1))
                                nc.vector.tensor_tensor(vf[:, j % 2], Ab[bank][:, :].rearrange("p (b n) -> p b n", b=2),
                                                        v_row[:, None, :].broadcast_to([P, 2, HG3 * P]), ALU.add).then_inc(N["A_dve"], 1)
                            elif what == "S":
                                g_ = 3 * h + j
                                nb = GROUPS3[j][1] - GROUPS3[j][0]
                                dve.wait_ge(N["S_full"], p * NG + (g_ + 1))
                                bank = Sb[g_ % 2][:, 0:nb * T3].rearrange("p (b t) -> p b t", b=nb)[:, :, 0:P + 1]
                                nc.vector.tensor_reduce(mx3[:, g_ % EXPS, 0:nb], bank, AX_X, ALU.max).then_inc(N["max_ready"], 1)
                                dve.wait_ge(N["max_ready"], p * NG + (g_ + 1))
                                nc.vector.tensor_scalar(nm3[:, g_ % EXPS, 0:nb], mx3[:, g_ % EXPS, 0:nb], -SCALE3, None,
                                                        ALU.mult).then_inc(N["nm_ready"], 1)
                                pending.append((g_, nb))
                            elif what == "T":
                                g_ = 3 * h + j
                                w = (GROUPS3[j][1] - GROUPS3[j][0]) * P
                                dve.wait_ge(N["T_act"], (p + dp) * NG + (g_ + 1))
                                nc.vector.tensor_tensor(PT3[:, g_ % 2, 1, 0:w], Tb[g_ % 2][:, 0:w], PT3[:, g_ % 2, 0, 0:w].bitcast(F32),
                                                        ALU.subtract).then_inc(N["T_dve"], 1)
                            elif what == "PV" and j >= 1:
                                dve.wait_ge(N["ctx_high"], (p + dp) * NC + (2 * h + j))
                                nc.vector.scalar_tensor_tensor(
                                    out=ctxT3[:, 1, h, (j - 1) * TOK:j * TOK], in0=Ob[j - 1][:, :], scalar=const(3, p + dp, h),
                                    in1=ctxT3[:, 0, h, (j - 1) * TOK:j * TOK].bitcast(F32), op0=ALU.add,
                                    op1=ALU.subtract).then_inc(N["ctx_low"], 1)
                            elif what == "out":
                                bank, n = fill3(p, step)
                                if j == 0:
                                    dve.wait_ge(S["x_biased"], 1)
                                dve.wait_ge(N["A_full"], n + 1)
                                nc.vector.tensor_tensor(x_all[:, 2 * j:2 * j + 2], Ab[bank][:, :].rearrange("p (b d) -> p b d", b=2),
                                                        x_all[:, 2 * j:2 * j + 2], ALU.add).then_inc(N["A_dve"], 1)
                        settle()
                    steps[0] = norms[0] = 0
                    norm(dve, lambda b: x_all[:, b], z3, B, row(ln_w), (rows_in, 16 * len(ROWS3)) if att == 0 else None,
                         lambda: split3_low(dve, "c"))
                    for b in range(B):
                        nc.vector.scalar_tensor_tensor(out=z3[:, b], in0=z3[:, b], scalar=rstd[:, b:b + 1], in1=row(ln_b),
                                                       op0=ALU.mult, op1=ALU.add).then_inc(S["norm_ready"], 1)
                    do(-1, AHEAD_K)
                    split3_low(dve, "h")
                    do(-1, AHEAD_QV)
                    passes(dve, do)

                @block.tensor
                def _(pe):
                    def do(p, steps=None):
                        for step in steps or steps_of(p):
                            what, dp, h, j = step
                            if what in ("q", "k", "v", "out"):
                                bank, n = fill3(p, step)
                                reached(pe, N["A_dve"], n - 1)
                            if what in ("q", "k"):
                                w = 0 if what == "q" else 1
                                if dp == 1 and j == 0:
                                    pe.wait_ge(N["w_low"], p * 3 + (3 + w + 1))
                                src = hT3 if what == "q" else cT3
                                for kt in range(KT):
                                    last = products(pe, Ab[bank][:, :], pair(w3[w], kt, slice(h * P, (h + 1) * P)),
                                                    pair(src, kt, slice(j * TOK, (j + 1) * TOK)), kt == 0, kt == KT - 1)
                                last.then_inc(N["A_full"], 1)
                            elif what == "v":
                                if dp == 1 and j == 0:
                                    pe.wait_ge(N["w_low"], p * 3 + (3 + 3))
                                for e in range(2):
                                    b = 2 * j + e
                                    for kt in range(KT):
                                        last = products(pe, Ab[bank][:, e * HG3 * P:(e + 1) * HG3 * P],
                                                        pair(cT3, kt, slice(b * P, (b + 1) * P)), pair(w3[2], kt), kt == 0, kt == KT - 1)
                                last.then_inc(N["A_full"], 1)
                            elif what == "S":
                                g_ = 3 * h + j
                                reached(pe, N["exp_done"], p * NG + (g_ - 1))
                                if j == 0:
                                    if h == 1:
                                        pe.wait_ge(N["A_dve"], fill3(p, ("k", 0, 1, 1))[1] + 1)
                                    else:
                                        after_q = len(HEAD_START) - HEAD_START.index(("q", 1, 0, 1)) - 1
                                        pe.wait_ge(N["A_dve"], (AHEAD if isinstance(p, int) and p == 0 else p * NF + (AHEAD - OUTS)) - after_q)
                                    pe.wait_ge(N["bias_low"], p * HG3 + (h + 1))
                                for b in range(*GROUPS3[j]):
                                    e = b - GROUPS3[j][0]
                                    last = products(pe, Sb[g_ % 2][:, e * T3:(e + 1) * T3],
                                                    (qT3[:, h, 0, b * P:(b + 1) * P], qT3[:, h, 1, b * P:(b + 1) * P]),
                                                    (kT3[:, h, 0, b], kT3[:, h, 1, b]), True, True)
                                last.then_inc(N["S_full"], 1)
                            elif what == "T":
                                g_ = 3 * h + j
                                reached(pe, N["T_dve"], (p + dp) * NG + (g_ - 1))
                                pe.wait_ge(N["P_ready"], (p + dp) * NG + (g_ + 1))
                                for e in range(GROUPS3[j][1] - GROUPS3[j][0]):
                                    last = nc.tensor.transpose(Tb[g_ % 2][:, e * P:(e + 1) * P], E3[:, g_ % EXPS, e, 0:P], ident[:, :])
                                last.then_inc(N["T_full"], 1)
                            elif what == "PV":
                                g_ = 3 * h + j
                                pe.wait_ge(N["T_dve"], (p + dp) * NG + (g_ + 1))
                                if h == 0:
                                    pe.wait_ge(N["v_low"], (p + dp) * NV + (j + 2))
                                if j < 2:
                                    reached(pe, N["ctx_low"], (p + dp) * NC + (2 * h + j - 1))
                                for b in range(*GROUPS3[j]):
                                    e = b - GROUPS3[j][0]
                                    last = products(pe, Ob[b // NB][:, (b % NB) * P:(b % NB + 1) * P],
                                                    (v3[:, 0, b, h * P:(h + 1) * P], v3[:, 1, b, h * P:(h + 1) * P]),
                                                    (PT3[:, g_ % 2, 0, e * P:(e + 1) * P], PT3[:, g_ % 2, 1, e * P:(e + 1) * P]), True, True)
                                last.then_inc(N["pv_done"], 1)
                            elif what == "out":
                                if j == 0:
                                    pe.wait_ge(N["wo_low"], p * 1)
                                pe.wait_ge(N["ctx_low"], p * NC + (j // 2 - 1))
                                for e in range(2):
                                    b = 2 * j + e
                                    for hh in range(HG3):
                                        last = products(pe, Ab[bank][:, e * D:(e + 1) * D], pair(ctxT3, hh, slice(b * P, (b + 1) * P)),
                                                        pair(wo3, hh), hh == 0, hh == HG3 - 1)
                                last.then_inc(N["A_full"], 1)
                    if att == 0:
                        pe.wait_ge(S["c_loaded"], 16)
                        turn3(pe, "c")
                        pe.wait_ge(S["T_act"], 4)
                        pe.wait_ge(S["T_dve"], 4)
                        pe.wait_ge(pad_cleared, 1)
                    do(-1, AHEAD_K)
                    turn3(pe, "h")
                    pe.wait_ge(S["T_act"], len(turns))
                    pe.wait_ge(S["T_dve"], len(turns))
                    do(-1, AHEAD_QV)
                    passes(pe, do)

            for each in N.values():
                nc.sync.sem_clear(each)
            for n in ("c_loaded", "T_full", "T_act", "T_dve", "vstep", "var_ready", "rstd_ready", "norm_ready", "pool_step", "x_biased"):
                nc.sync.sem_clear(S[n])
            nc.all_engine_barrier()

        rows_in = ctx.enter_context(nc.semaphore("rows_in"))
        fc_in, pj_in, split3 = (ctx.enter_context(nc.semaphore(n)) for n in ("fc_in", "pj_in", "split3"))
        pad_cleared = ctx.enter_context(nc.semaphore("pad_cleared"))
        attention3(0)
        attention3(1)

        s4 = ExitStack()
        z4 = sb("z4", [P, B, D], F32, s4)
        hT4 = sb("hT4", [P, HALVES, 2, KT, TOK], R32, s4)
        g4 = sb("g4", [P, 2, TOK], F32, s4)
        gT4 = sb("gT4", [P, 2, 2, TOK], R32, s4)
        s4.close()
        stored = ctx.enter_context(nc.semaphore("stored"))
        TILES = HALVES * MT
        sums4 = [Ob, Sb]
        TURN2 = 3
        with nc.Block() as block:
            @block.vector
            def _(dve):
                steps[0] = norms[0] = 0

                def norm_half(half):
                    at = half * NB
                    norm(dve, lambda b: x_all[:, at + b], z4[:, at:at + NB], NB, row("L3_xattn_ln_mlp_scale"))
                    for b in range(NB):
                        nc.vector.scalar_tensor_tensor(out=z4[:, at + b], in0=z4[:, at + b], scalar=rstd[:, b:b + 1],
                                                       in1=row("L3_xattn_ln_mlp_offset"), op0=ALU.mult, op1=ALU.add).then_inc(S["norm_ready"], 1)

                norm_half(0)
                split_low(dve, hT4[:, 0], 0)
                norm_half(1)
                split_low(dve, hT4[:, 1], KT)
                for half in range(HALVES):
                    dve.wait_ge(S["x_biased"], half + 1)
                    dve.wait_ge(S["g_used"], MT * (half + 1))
                    for f in range(2):
                        at = half * NB + 2 * f
                        nc.vector.tensor_tensor(x_all[:, at:at + 2], sums4[half][f][:, :].rearrange("p (b d) -> p b d", b=2),
                                                x_all[:, at:at + 2], ALU.add).then_inc(S["O_read"], 1)

            @block.gpsimd
            def _(pool):
                psteps[0] = 0
                power(pool, 1, NB, LN_EPS)
                pool.wait_ge(S["norm_ready"], NB)
                power(pool, 2, NB, LN_EPS)
                for t in range(TILES):
                    pool.wait_ge(S["g_high"], t + 1)
                    nc.gpsimd.tensor_tensor(gT4[:, t % 2, 1], g4[:, t % 2], gT4[:, t % 2, 0].bitcast(F32), ALU.subtract).then_inc(S["g_low"], 1)
                    if t % MT in (1, 2):
                        at = t // MT * NB + 2 * (t % MT - 1)
                        pool.wait_ge(S["norm_ready"], (t // MT + 1) * NB)
                        i = nc.gpsimd.tensor_tensor(x_all[:, at:at + 2], x_all[:, at:at + 2],
                                                    row("L3_xattn_b_fc2")[:, None, :].broadcast_to([P, 2, D]), ALU.add)
                        if t % MT == 2:
                            i.then_inc(S["x_biased"], 1)

            @block.scalar
            def _(act):
                split_high(act, hT4[:, 0], 0)
                for t in range(TILES):
                    act.wait_ge(S["A_full"], t + 1)
                    if t >= 2:
                        act.wait_ge(S["g_low"], t - 1)
                        act.wait_ge(S["g_used"], t - 1)
                    nc.scalar.activation(g4[:, t % 2], Ab[t % 2][:, :], ACT.Gelu, bias=col("L3_xattn_b_fc1", t % MT)).then_inc(S["A_act"], 1)
                    act.wait_ge(S["A_act"], t + 1)
                    nc.scalar.activation(gT4[:, t % 2, 0], g4[:, t % 2], ACT.Copy).then_inc(S["g_high"], 1)
                    if t == TURN2:
                        split_high(act, hT4[:, 1], KT)

            @block.tensor
            def _(pe):
                def down(t):
                    half, m = divmod(t, MT)
                    pe.wait_ge(S["g_high"], t + 1)
                    pe.wait_ge(S["g_low"], t + 1)
                    for b in range(NB):
                        bank = sums4[half][b // 2][:, (b % 2) * D:(b % 2 + 1) * D]
                        left, right = pair(gT4[:, t % 2], slice(b * P, (b + 1) * P)), pair(pjw, m)
                        pe.matmul(bank, left[0], right[0], start=(m == 0 and b % 2 == 0), stop=False, skip_group_check=True)
                        pe.matmul(bank, left[1], right[0], start=False, stop=False, skip_group_check=True)
                        last = pe.matmul(bank, left[0], right[1], start=False, stop=(m == MT - 1), skip_group_check=True)
                    last.then_inc(S["g_used"], 1)

                turn(pe, z4, MLP_T, 0, 0)
                for t in range(TILES + 2):
                    if t < TILES:
                        half, m = divmod(t, MT)
                        if t >= 2:
                            pe.wait_ge(S["A_act"], t - 1)
                        for kt in range(KT):
                            if m == 0:
                                pe.wait_ge(S["T_act"], half * KT + kt + 1)
                                pe.wait_ge(S["T_dve"], half * KT + kt + 1)
                            last = products(pe, Ab[t % 2][:, :], pair(fcw, kt, slice(m * P, (m + 1) * P)), pair(hT4[:, half], kt),
                                            kt == 0, kt == KT - 1)
                        last.then_inc(S["A_full"], 1)
                    if t >= 2:
                        down(t - 2)
                    if t == TURN2:
                        turn(pe, z4[:, NB:B], MLP_T, KT, 1)

            @block.sync
            def _(sp):
                for half in range(HALVES):
                    sp.wait_ge(S["O_read"], 2 * (half + 1))
                    sp.dma_start(out[half * NB:(half + 1) * NB].rearrange("b t d -> t b d"), x_all[:, half * NB:(half + 1) * NB, :]
                                 ).then_inc(stored, 16)
                sp.wait_ge(stored, 16 * HALVES)


_OUTS = [((B, P, D), "float32")]


def kernel(**inputs):
    import numpy as _np
    import concourse.bacc as _bacc
    from concourse import mybir as _mybir
    from concourse.bass_utils import run_bass_kernel_spmd as _run

    nc = _bacc.Bacc("TRN2", target_bir_lowering=False, num_devices=1)
    arrays, args = {}, {}
    for name, value in inputs.items():
        v = _np.ascontiguousarray(value).reshape(_np.shape(value) or (1,))
        arrays[f"in_{name}_dram"] = v
        args[name] = nc.dram_tensor(f"in_{name}_dram", v.shape, _mybir.dt.from_np(v.dtype), kind="ExternalInput").ap()
    out = nc.dram_tensor("out_0_dram", _OUTS[0][0], F32, kind="ExternalOutput").ap()
    network(nc, args, out)
    r = _run(nc, [arrays], core_ids=[0])
    return r.results[0]["out_0_dram"]
```
